# Optimizing a Trainium2 kernel written in Bass

```python
import numpy as np
import jax
import jax.numpy as jnp

def _softmax(x, axis=-1):
    return jax.nn.softmax(x, axis=axis)

def _gelu(x):
    return jax.nn.gelu(x, approximate=True)

def _silu(x):
    return jax.nn.silu(x)

def _sigmoid(x):
    return jax.nn.sigmoid(x)

def _layernorm(x, axis=-1, eps=1e-05):
    m = jnp.mean(x, axis=axis, keepdims=True)
    v = jnp.var(x, axis=axis, keepdims=True)
    return (x - m) / jnp.sqrt(v + eps)

def _scatter_add(tgt, idx, src, axis=0):
    return tgt.at[idx].add(src)

def _segment_sum(src, seg, n):
    return jax.ops.segment_sum(src, seg, n)
kernel_name = 'mk_metaformer_d4_conv_nchw384_r4_38385e'

def setup_inputs(seed: int=0):
    np.random.seed(seed)
    _w = jnp.asarray

    def _rec_inputs():
        import jax
        import jax.numpy as jnp
        _gk = jax.random.key(seed)
        x = -0.0002221 + 1 * jax.random.normal(jax.random.fold_in(_gk, 1), (16, 96, 16, 16), jnp.float32)
        return x
    x = _rec_inputs()

    def _L0_conv_setup():
        import jax, jax.numpy as jnp
        import numpy as np
        EPS = 1e-05

        def _dwconv(x, w, pad):
            return jax.lax.conv_general_dilated(x, w, window_strides=(1, 1), padding=[(pad, pad), (pad, pad)], feature_group_count=w.shape[0], dimension_numbers=('NCHW', 'OIHW', 'NCHW'))

        def _bn(y, g, b, m, v):
            scale = (g / jnp.sqrt(v + EPS))[None, :, None, None]
            shift = (b - m * g / jnp.sqrt(v + EPS))[None, :, None, None]
            return y * scale + shift
        key = jax.random.key(seed)
        ks = jax.random.split(key, 16)
        C, KL, KS = (96, 13, 3)
        N, H, W = (16, 16, 16)
        inp = {'x': jax.random.normal(ks[0], (N, C, H, W), jnp.float32), 'w_large': jax.random.normal(ks[1], (C, 1, KL, KL), jnp.float32) * 0.05, 'w_small': jax.random.normal(ks[2], (C, 1, KS, KS), jnp.float32) * 0.2, 'g_l': jax.random.normal(ks[3], (C,), jnp.float32), 'b_l': jax.random.normal(ks[4], (C,), jnp.float32), 'm_l': jax.random.normal(ks[5], (C,), jnp.float32), 'v_l': jax.random.uniform(ks[6], (C,), jnp.float32, 0.5, 1.5), 'g_s': jax.random.normal(ks[7], (C,), jnp.float32), 'b_s': jax.random.normal(ks[8], (C,), jnp.float32), 'm_s': jax.random.normal(ks[9], (C,), jnp.float32), 'v_s': jax.random.uniform(ks[10], (C,), jnp.float32, 0.5, 1.5), 'g_i': jax.random.normal(ks[11], (C,), jnp.float32), 'b_i': jax.random.normal(ks[12], (C,), jnp.float32), 'm_i': jax.random.normal(ks[13], (C,), jnp.float32), 'v_i': jax.random.uniform(ks[14], (C,), jnp.float32, 0.5, 1.5)}
        return inp
    _L0_conv_all = _L0_conv_setup()
    _L0_conv_in = {k: v for k, v in _L0_conv_all.items() if k in ('w_large', 'w_small', 'g_l', 'b_l', 'm_l', 'v_l', 'g_s', 'b_s', 'm_s', 'v_s', 'g_i', 'b_i', 'm_i', 'v_i')}
    del _L0_conv_all

    def _L0_ffn_setup():
        import jax, jax.numpy as jnp
        import numpy as np
        NUM_EXPERTS = 4
        TOP_K = 2
        DIM = 96
        HID = 4 * DIM
        key = jax.random.key(seed)
        ks = jax.random.split(key, 5)
        B, S = (16, 512)
        scale_in = 1.0 / np.sqrt(DIM)
        scale_hid = 1.0 / np.sqrt(HID)
        return {'x': jax.random.normal(ks[0], (B, S, DIM), dtype=jnp.float32), 'gate_w': jax.random.normal(ks[1], (DIM, NUM_EXPERTS), dtype=jnp.float32) * scale_in, 'gate_b': jnp.zeros((NUM_EXPERTS,), dtype=jnp.float32), 'w1': jax.random.normal(ks[2], (NUM_EXPERTS, DIM, HID), dtype=jnp.float32) * scale_in, 'b1': jnp.zeros((NUM_EXPERTS, HID), dtype=jnp.float32), 'w2': jax.random.normal(ks[3], (NUM_EXPERTS, HID, DIM), dtype=jnp.float32) * scale_hid, 'b2': jnp.zeros((NUM_EXPERTS, DIM), dtype=jnp.float32)}
    _L0_ffn_all = _L0_ffn_setup()
    _L0_ffn_in = {k: v for k, v in _L0_ffn_all.items() if k in ('gate_w', 'gate_b', 'w1', 'b1', 'w2', 'b2')}
    del _L0_ffn_all

    def _L1_conv_setup():
        import jax, jax.numpy as jnp
        import numpy as np
        NUM_HEADS = 6
        KEY_DIM = 16
        D_HEAD = 32

        def conv1x1_bn(x, W, scale, bias):
            y = jnp.einsum('oi,bihw->bohw', W, x)
            return y * scale[None, :, None, None] + bias[None, :, None, None]
        key = jax.random.key(seed)
        ks = jax.random.split(key, 16)
        B, C, H, W = (4, 96, 48, 48)
        dim_s = C // 4
        nh_kd = NUM_HEADS * KEY_DIM
        dh = NUM_HEADS * D_HEAD

        def w(k, o, i):
            return jax.random.normal(k, (o, i), dtype=jnp.float32) / np.sqrt(i)
        return {'xx': jax.random.normal(ks[0], (B, C, H, W), dtype=jnp.float32), 'Wq': w(ks[1], nh_kd, dim_s), 'q_scale': jax.random.uniform(ks[2], (nh_kd,), dtype=jnp.float32, minval=0.5, maxval=1.5), 'q_bias': 0.1 * jax.random.normal(ks[3], (nh_kd,), dtype=jnp.float32), 'Wk': w(ks[4], nh_kd, C), 'k_scale': jax.random.uniform(ks[5], (nh_kd,), dtype=jnp.float32, minval=0.5, maxval=1.5), 'k_bias': 0.1 * jax.random.normal(ks[6], (nh_kd,), dtype=jnp.float32), 'Wv': w(ks[7], dh, C), 'v_scale': jax.random.uniform(ks[8], (dh,), dtype=jnp.float32, minval=0.5, maxval=1.5), 'v_bias': 0.1 * jax.random.normal(ks[9], (dh,), dtype=jnp.float32), 'Wp': w(ks[10], dim_s, dh), 'p_scale': jax.random.uniform(ks[11], (dim_s,), dtype=jnp.float32, minval=0.5, maxval=1.5), 'p_bias': 0.1 * jax.random.normal(ks[12], (dim_s,), dtype=jnp.float32), 'Wo': w(ks[13], C, dim_s), 'o_scale': jax.random.uniform(ks[14], (C,), dtype=jnp.float32, minval=0.5, maxval=1.5), 'o_bias': 0.1 * jax.random.normal(ks[15], (C,), dtype=jnp.float32)}
    _L1_conv_all = _L1_conv_setup()
    _L1_conv_in = {k: v for k, v in _L1_conv_all.items() if k in ('Wq', 'q_scale', 'q_bias', 'Wk', 'k_scale', 'k_bias', 'Wv', 'v_scale', 'v_bias', 'Wp', 'p_scale', 'p_bias', 'Wo', 'o_scale', 'o_bias')}
    del _L1_conv_all

    def _L1_ffn_setup():
        import jax, jax.numpy as jnp
        import numpy as np
        NUM_EXPERTS = 4
        TOP_K = 2
        DIM = 96
        HID = 4 * DIM
        key = jax.random.key(seed)
        ks = jax.random.split(key, 5)
        B, S = (16, 512)
        scale_in = 1.0 / np.sqrt(DIM)
        scale_hid = 1.0 / np.sqrt(HID)
        return {'x': jax.random.normal(ks[0], (B, S, DIM), dtype=jnp.float32), 'gate_w': jax.random.normal(ks[1], (DIM, NUM_EXPERTS), dtype=jnp.float32) * scale_in, 'gate_b': jnp.zeros((NUM_EXPERTS,), dtype=jnp.float32), 'w1': jax.random.normal(ks[2], (NUM_EXPERTS, DIM, HID), dtype=jnp.float32) * scale_in, 'b1': jnp.zeros((NUM_EXPERTS, HID), dtype=jnp.float32), 'w2': jax.random.normal(ks[3], (NUM_EXPERTS, HID, DIM), dtype=jnp.float32) * scale_hid, 'b2': jnp.zeros((NUM_EXPERTS, DIM), dtype=jnp.float32)}
    _L1_ffn_all = _L1_ffn_setup()
    _L1_ffn_in = {k: v for k, v in _L1_ffn_all.items() if k in ('gate_w', 'gate_b', 'w1', 'b1', 'w2', 'b2')}
    del _L1_ffn_all

    def _L2_conv_setup():
        import jax, jax.numpy as jnp
        import numpy as np
        from jax import lax
        B, C, H, W = (4, 96, 56, 56)
        NH, HC, STRIDE = (12, 32, 2)
        SCALE = HC ** (-0.5)

        def _dwconv(x, w, b, stride):
            y = lax.conv_general_dilated(x, w, (stride, stride), [(1, 1), (1, 1)], dimension_numbers=('NCHW', 'OIHW', 'NCHW'), feature_group_count=x.shape[1])
            return y + b[None, :, None, None]

        def _grid_sample_bilinear(value, grid):
            Hh, Ww = (value.shape[2], value.shape[3])
            ix = (grid[..., 0] + 1.0) * 0.5 * (Ww - 1)
            iy = (grid[..., 1] + 1.0) * 0.5 * (Hh - 1)
            x0 = jnp.floor(ix)
            y0 = jnp.floor(iy)
            wx = ix - x0
            wy = iy - y0
            x0i = jnp.clip(x0, 0, Ww - 1).astype(jnp.int32)
            x1i = jnp.clip(x0 + 1, 0, Ww - 1).astype(jnp.int32)
            y0i = jnp.clip(y0, 0, Hh - 1).astype(jnp.int32)
            y1i = jnp.clip(y0 + 1, 0, Hh - 1).astype(jnp.int32)

            def per_b(img, y0i, y1i, x0i, x1i, wx, wy):
                v00 = img[:, y0i, x0i]
                v01 = img[:, y0i, x1i]
                v10 = img[:, y1i, x0i]
                v11 = img[:, y1i, x1i]
                return v00 * (1 - wx) * (1 - wy) + v01 * wx * (1 - wy) + v10 * (1 - wx) * wy + v11 * wx * wy
            return jax.vmap(per_b)(value, y0i, y1i, x0i, x1i, wx, wy)

        def _ref_points(Hk, Wk):
            ref_y = jnp.linspace(0.5, Hk - 0.5, Hk)
            ref_x = jnp.linspace(0.5, Wk - 0.5, Wk)
            ry, rx = jnp.meshgrid(ref_y, ref_x, indexing='ij')
            return jnp.stack([ry / Hk * 2 - 1, rx / Wk * 2 - 1], axis=-1)
        key = jax.random.key(seed)
        ks = jax.random.split(key, 10)
        s = 0.05
        return {'x': jax.random.normal(ks[0], (B, C, H, W), jnp.float32), 'w_v': jax.random.normal(ks[1], (C, 1, 3, 3), jnp.float32) * s, 'b_v': jnp.zeros((C,), jnp.float32), 'w_q': jax.random.normal(ks[2], (C, 1, 3, 3), jnp.float32) * s, 'b_q': jnp.zeros((C,), jnp.float32), 'w_k': jax.random.normal(ks[3], (C, 1, 3, 3), jnp.float32) * s, 'b_k': jnp.zeros((C,), jnp.float32), 'w_off1': jax.random.normal(ks[4], (C, 1, 3, 3), jnp.float32) * s, 'b_off1': jnp.zeros((C,), jnp.float32), 'ln_g': jnp.ones((C,), jnp.float32), 'ln_b': jnp.zeros((C,), jnp.float32), 'w_off2': jax.random.normal(ks[5], (2, C), jnp.float32) * s, 'w_out': jax.random.normal(ks[6], (C, C), jnp.float32) * s}
    _L2_conv_all = _L2_conv_setup()
    _L2_conv_in = {k: v for k, v in _L2_conv_all.items() if k in ('w_v', 'b_v', 'w_q', 'b_q', 'w_k', 'b_k', 'w_off1', 'b_off1', 'ln_g', 'ln_b', 'w_off2', 'w_out')}
    del _L2_conv_all

    def _L2_ffn_setup():
        import jax, jax.numpy as jnp
        import numpy as np
        NUM_EXPERTS = 4
        TOP_K = 2
        DIM = 96
        HID = 4 * DIM
        key = jax.random.key(seed)
        ks = jax.random.split(key, 5)
        B, S = (16, 512)
        scale_in = 1.0 / np.sqrt(DIM)
        scale_hid = 1.0 / np.sqrt(HID)
        return {'x': jax.random.normal(ks[0], (B, S, DIM), dtype=jnp.float32), 'gate_w': jax.random.normal(ks[1], (DIM, NUM_EXPERTS), dtype=jnp.float32) * scale_in, 'gate_b': jnp.zeros((NUM_EXPERTS,), dtype=jnp.float32), 'w1': jax.random.normal(ks[2], (NUM_EXPERTS, DIM, HID), dtype=jnp.float32) * scale_in, 'b1': jnp.zeros((NUM_EXPERTS, HID), dtype=jnp.float32), 'w2': jax.random.normal(ks[3], (NUM_EXPERTS, HID, DIM), dtype=jnp.float32) * scale_hid, 'b2': jnp.zeros((NUM_EXPERTS, DIM), dtype=jnp.float32)}
    _L2_ffn_all = _L2_ffn_setup()
    _L2_ffn_in = {k: v for k, v in _L2_ffn_all.items() if k in ('gate_w', 'gate_b', 'w1', 'b1', 'w2', 'b2')}
    del _L2_ffn_all

    def _L3_conv_setup():
        import jax, jax.numpy as jnp
        import numpy as np
        from jax import lax
        DIM = 96
        HEADS = 8
        DIM_HEAD = 16
        INNER = HEADS * DIM_HEAD
        K = 3
        B, H, W = (8, 56, 56)
        EPS = 1e-05
        SCALE = DIM_HEAD ** (-0.5)

        def _dw_proj(x, w_dw, bn_g, bn_b, bn_m, bn_v, w_pw):
            c_in = x.shape[1]
            y = lax.conv_general_dilated(x, w_dw, window_strides=(1, 1), padding='SAME', feature_group_count=c_in, dimension_numbers=('NCHW', 'OIHW', 'NCHW'))
            inv = bn_g / jnp.sqrt(bn_v + EPS)
            y = y * inv[None, :, None, None] + (bn_b - bn_m * inv)[None, :, None, None]
            return jnp.einsum('bchw,oc->bohw', y, w_pw)

        def _split_heads(t):
            b, _, hh, ww = t.shape
            t = t.reshape(b, HEADS, DIM_HEAD, hh * ww)
            return t.transpose(0, 1, 3, 2).reshape(b * HEADS, hh * ww, DIM_HEAD)
        key = jax.random.key(seed)
        ks = jax.random.split(key, 12)
        inp = {'x': jax.random.normal(ks[0], (B, DIM, H, W), jnp.float32), 'wq_dw': jax.random.normal(ks[1], (DIM, 1, K, K), jnp.float32) * 0.1, 'wq_bn_g': jax.random.normal(ks[2], (DIM,), jnp.float32) * 0.1 + 1.0, 'wq_bn_b': jax.random.normal(ks[3], (DIM,), jnp.float32) * 0.1, 'wq_bn_m': jax.random.normal(ks[4], (DIM,), jnp.float32) * 0.1, 'wq_bn_v': jax.random.uniform(ks[5], (DIM,), jnp.float32, 0.5, 1.5), 'wq_pw': jax.random.normal(ks[6], (INNER, DIM), jnp.float32) * DIM ** (-0.5), 'wkv_dw': jax.random.normal(ks[7], (DIM, 1, K, K), jnp.float32) * 0.1, 'wkv_bn_g': jax.random.normal(ks[8], (DIM,), jnp.float32) * 0.1 + 1.0, 'wkv_bn_b': jax.random.normal(ks[9], (DIM,), jnp.float32) * 0.1, 'wkv_bn_m': jax.random.normal(ks[10], (DIM,), jnp.float32) * 0.1, 'wkv_bn_v': jax.random.uniform(ks[11], (DIM,), jnp.float32, 0.5, 1.5)}
        k2 = jax.random.split(jax.random.fold_in(key, 1), 3)
        inp['wkv_pw'] = jax.random.normal(k2[0], (2 * INNER, DIM), jnp.float32) * DIM ** (-0.5)
        inp['wo'] = jax.random.normal(k2[1], (DIM, INNER), jnp.float32) * INNER ** (-0.5)
        inp['bo'] = jax.random.normal(k2[2], (DIM,), jnp.float32) * 0.01
        return inp
    _L3_conv_all = _L3_conv_setup()
    _L3_conv_in = {k: v for k, v in _L3_conv_all.items() if k in ('wq_dw', 'wq_bn_g', 'wq_bn_b', 'wq_bn_m', 'wq_bn_v', 'wq_pw', 'wkv_dw', 'wkv_bn_g', 'wkv_bn_b', 'wkv_bn_m', 'wkv_bn_v', 'wkv_pw', 'wo', 'bo')}
    del _L3_conv_all

    def _L3_ffn_setup():
        import jax, jax.numpy as jnp
        import numpy as np
        NUM_GROUPS = 5
        EPS = 1e-05
        QB = 128.0

        def _binarize_weights_groupwise(W):
            n_out = W.shape[0]
            gs = n_out // NUM_GROUPS
            Wb = jnp.zeros_like(W)
            for g in range(NUM_GROUPS):
                wg = W[g * gs:(g + 1) * gs]
                z = wg - wg.mean()
                ste = z + jax.lax.stop_gradient(jnp.sign(z) - z)
                Wb = Wb.at[g * gs:(g + 1) * gs].set(ste)
            return Wb

        def _quantize_activations_groupwise(x):
            n = x.shape[0]
            gs = n // NUM_GROUPS
            xq = jnp.zeros_like(x)
            for g in range(NUM_GROUPS):
                ag = x[g * gs:(g + 1) * gs]
                gamma = jnp.max(jnp.abs(ag))
                xq = xq.at[g * gs:(g + 1) * gs].set(jnp.clip(ag * QB / (gamma + EPS), -QB + EPS, QB - EPS))
            return xq

        def _bitlinear(x, W, b):
            Wb = _binarize_weights_groupwise(W)
            y = jnp.einsum('btc,oc->bto', x, Wb) + b
            return _quantize_activations_groupwise(y)
        key = jax.random.key(seed)
        k1, k2, k3, k4, k5 = jax.random.split(key, 5)
        B, T, C = (10, 512, 96)
        H = 4 * C
        lim1 = 1.0 / np.sqrt(C)
        lim2 = 1.0 / np.sqrt(H)
        x = jax.random.normal(k1, (B, T, C), dtype=jnp.float32)
        W1 = jax.random.uniform(k2, (H, C), minval=-lim1, maxval=lim1, dtype=jnp.float32)
        b1 = jax.random.uniform(k3, (H,), minval=-lim1, maxval=lim1, dtype=jnp.float32)
        W2 = jax.random.uniform(k4, (C, H), minval=-lim2, maxval=lim2, dtype=jnp.float32)
        b2 = jax.random.uniform(k5, (C,), minval=-lim2, maxval=lim2, dtype=jnp.float32)
        return {'x': x, 'W1': W1, 'b1': b1, 'W2': W2, 'b2': b2}
    _L3_ffn_all = _L3_ffn_setup()
    _L3_ffn_in = {k: v for k, v in _L3_ffn_all.items() if k in ('W1', 'b1', 'W2', 'b2')}
    del _L3_ffn_all
    return {'x': x, 'L0_conv_w_large': _L0_conv_in['w_large'], 'L0_conv_w_small': _L0_conv_in['w_small'], 'L0_conv_g_l': _L0_conv_in['g_l'], 'L0_conv_b_l': _L0_conv_in['b_l'], 'L0_conv_m_l': _L0_conv_in['m_l'], 'L0_conv_v_l': _L0_conv_in['v_l'], 'L0_conv_g_s': _L0_conv_in['g_s'], 'L0_conv_b_s': _L0_conv_in['b_s'], 'L0_conv_m_s': _L0_conv_in['m_s'], 'L0_conv_v_s': _L0_conv_in['v_s'], 'L0_conv_g_i': _L0_conv_in['g_i'], 'L0_conv_b_i': _L0_conv_in['b_i'], 'L0_conv_m_i': _L0_conv_in['m_i'], 'L0_conv_v_i': _L0_conv_in['v_i'], 'L0_ffn_gate_w': _L0_ffn_in['gate_w'], 'L0_ffn_gate_b': _L0_ffn_in['gate_b'], 'L0_ffn_w1': _L0_ffn_in['w1'], 'L0_ffn_b1': _L0_ffn_in['b1'], 'L0_ffn_w2': _L0_ffn_in['w2'], 'L0_ffn_b2': _L0_ffn_in['b2'], 'L1_conv_Wq': _L1_conv_in['Wq'], 'L1_conv_q_scale': _L1_conv_in['q_scale'], 'L1_conv_q_bias': _L1_conv_in['q_bias'], 'L1_conv_Wk': _L1_conv_in['Wk'], 'L1_conv_k_scale': _L1_conv_in['k_scale'], 'L1_conv_k_bias': _L1_conv_in['k_bias'], 'L1_conv_Wv': _L1_conv_in['Wv'], 'L1_conv_v_scale': _L1_conv_in['v_scale'], 'L1_conv_v_bias': _L1_conv_in['v_bias'], 'L1_conv_Wp': _L1_conv_in['Wp'], 'L1_conv_p_scale': _L1_conv_in['p_scale'], 'L1_conv_p_bias': _L1_conv_in['p_bias'], 'L1_conv_Wo': _L1_conv_in['Wo'], 'L1_conv_o_scale': _L1_conv_in['o_scale'], 'L1_conv_o_bias': _L1_conv_in['o_bias'], 'L1_ffn_gate_w': _L1_ffn_in['gate_w'], 'L1_ffn_gate_b': _L1_ffn_in['gate_b'], 'L1_ffn_w1': _L1_ffn_in['w1'], 'L1_ffn_b1': _L1_ffn_in['b1'], 'L1_ffn_w2': _L1_ffn_in['w2'], 'L1_ffn_b2': _L1_ffn_in['b2'], 'L2_conv_w_v': _L2_conv_in['w_v'], 'L2_conv_b_v': _L2_conv_in['b_v'], 'L2_conv_w_q': _L2_conv_in['w_q'], 'L2_conv_b_q': _L2_conv_in['b_q'], 'L2_conv_w_k': _L2_conv_in['w_k'], 'L2_conv_b_k': _L2_conv_in['b_k'], 'L2_conv_w_off1': _L2_conv_in['w_off1'], 'L2_conv_b_off1': _L2_conv_in['b_off1'], 'L2_conv_ln_g': _L2_conv_in['ln_g'], 'L2_conv_ln_b': _L2_conv_in['ln_b'], 'L2_conv_w_off2': _L2_conv_in['w_off2'], 'L2_conv_w_out': _L2_conv_in['w_out'], 'L2_ffn_gate_w': _L2_ffn_in['gate_w'], 'L2_ffn_gate_b': _L2_ffn_in['gate_b'], 'L2_ffn_w1': _L2_ffn_in['w1'], 'L2_ffn_b1': _L2_ffn_in['b1'], 'L2_ffn_w2': _L2_ffn_in['w2'], 'L2_ffn_b2': _L2_ffn_in['b2'], 'L3_conv_wq_dw': _L3_conv_in['wq_dw'], 'L3_conv_wq_bn_g': _L3_conv_in['wq_bn_g'], 'L3_conv_wq_bn_b': _L3_conv_in['wq_bn_b'], 'L3_conv_wq_bn_m': _L3_conv_in['wq_bn_m'], 'L3_conv_wq_bn_v': _L3_conv_in['wq_bn_v'], 'L3_conv_wq_pw': _L3_conv_in['wq_pw'], 'L3_conv_wkv_dw': _L3_conv_in['wkv_dw'], 'L3_conv_wkv_bn_g': _L3_conv_in['wkv_bn_g'], 'L3_conv_wkv_bn_b': _L3_conv_in['wkv_bn_b'], 'L3_conv_wkv_bn_m': _L3_conv_in['wkv_bn_m'], 'L3_conv_wkv_bn_v': _L3_conv_in['wkv_bn_v'], 'L3_conv_wkv_pw': _L3_conv_in['wkv_pw'], 'L3_conv_wo': _L3_conv_in['wo'], 'L3_conv_bo': _L3_conv_in['bo'], 'L3_ffn_W1': _L3_ffn_in['W1'], 'L3_ffn_b1': _L3_ffn_in['b1'], 'L3_ffn_W2': _L3_ffn_in['W2'], 'L3_ffn_b2': _L3_ffn_in['b2']}

def reference(x, L0_conv_w_large, L0_conv_w_small, L0_conv_g_l, L0_conv_b_l, L0_conv_m_l, L0_conv_v_l, L0_conv_g_s, L0_conv_b_s, L0_conv_m_s, L0_conv_v_s, L0_conv_g_i, L0_conv_b_i, L0_conv_m_i, L0_conv_v_i, L0_ffn_gate_w, L0_ffn_gate_b, L0_ffn_w1, L0_ffn_b1, L0_ffn_w2, L0_ffn_b2, L1_conv_Wq, L1_conv_q_scale, L1_conv_q_bias, L1_conv_Wk, L1_conv_k_scale, L1_conv_k_bias, L1_conv_Wv, L1_conv_v_scale, L1_conv_v_bias, L1_conv_Wp, L1_conv_p_scale, L1_conv_p_bias, L1_conv_Wo, L1_conv_o_scale, L1_conv_o_bias, L1_ffn_gate_w, L1_ffn_gate_b, L1_ffn_w1, L1_ffn_b1, L1_ffn_w2, L1_ffn_b2, L2_conv_w_v, L2_conv_b_v, L2_conv_w_q, L2_conv_b_q, L2_conv_w_k, L2_conv_b_k, L2_conv_w_off1, L2_conv_b_off1, L2_conv_ln_g, L2_conv_ln_b, L2_conv_w_off2, L2_conv_w_out, L2_ffn_gate_w, L2_ffn_gate_b, L2_ffn_w1, L2_ffn_b1, L2_ffn_w2, L2_ffn_b2, L3_conv_wq_dw, L3_conv_wq_bn_g, L3_conv_wq_bn_b, L3_conv_wq_bn_m, L3_conv_wq_bn_v, L3_conv_wq_pw, L3_conv_wkv_dw, L3_conv_wkv_bn_g, L3_conv_wkv_bn_b, L3_conv_wkv_bn_m, L3_conv_wkv_bn_v, L3_conv_wkv_pw, L3_conv_wo, L3_conv_bo, L3_ffn_W1, L3_ffn_b1, L3_ffn_W2, L3_ffn_b2):
    import jax
    import jax.numpy as jnp

    def _L0_conv_ref(x, w_large, w_small, g_l, b_l, m_l, v_l, g_s, b_s, m_s, v_s, g_i, b_i, m_i, v_i):
        import jax, jax.numpy as jnp
        import numpy as np
        EPS = 1e-05

        def _dwconv(x, w, pad):
            return jax.lax.conv_general_dilated(x, w, window_strides=(1, 1), padding=[(pad, pad), (pad, pad)], feature_group_count=w.shape[0], dimension_numbers=('NCHW', 'OIHW', 'NCHW'))

        def _bn(y, g, b, m, v):
            scale = (g / jnp.sqrt(v + EPS))[None, :, None, None]
            shift = (b - m * g / jnp.sqrt(v + EPS))[None, :, None, None]
            return y * scale + shift
        kl = w_large.shape[-1]
        ks = w_small.shape[-1]
        out = _bn(_dwconv(x, w_large, kl // 2), g_l, b_l, m_l, v_l) + _bn(_dwconv(x, w_small, ks // 2), g_s, b_s, m_s, v_s) + _bn(x, g_i, b_i, m_i, v_i)
        return out

    def _L0_ffn_ref(x, gate_w, gate_b, w1, b1, w2, b2):
        import jax, jax.numpy as jnp
        import numpy as np
        NUM_EXPERTS = 4
        TOP_K = 2
        DIM = 96
        HID = 4 * DIM
        scores = jnp.einsum('bsd,de->bse', x, gate_w) + gate_b
        probs = jax.nn.softmax(scores, axis=-1)
        topk_vals, topk_idx = jax.lax.top_k(probs, TOP_K)
        mask = jnp.sum(jax.nn.one_hot(topk_idx, NUM_EXPERTS, dtype=probs.dtype), axis=-2)
        masked = probs * mask
        masked = masked / (jnp.sum(masked, axis=-1, keepdims=True) + 1e-09)
        h = jax.nn.gelu(jnp.einsum('bsd,edh->ebsh', x, w1) + b1[:, None, None, :], approximate=False)
        y = jnp.einsum('ebsh,ehd->ebsd', h, w2) + b2[:, None, None, :]
        out = jnp.einsum('bse,ebsd->bsd', masked, y)
        return out

    def _L1_conv_ref(xx, Wq, q_scale, q_bias, Wk, k_scale, k_bias, Wv, v_scale, v_bias, Wp, p_scale, p_bias, Wo, o_scale, o_bias):
        import jax, jax.numpy as jnp
        import numpy as np
        NUM_HEADS = 6
        KEY_DIM = 16
        D_HEAD = 32

        def conv1x1_bn(x, W, scale, bias):
            y = jnp.einsum('oi,bihw->bohw', W, x)
            return y * scale[None, :, None, None] + bias[None, :, None, None]
        B, C, H, W = xx.shape
        dim_s = C // 4
        N = H * W
        x = xx[:, 3 * dim_s:]
        q = conv1x1_bn(x, Wq, q_scale, q_bias)
        q = q.reshape(B, NUM_HEADS, KEY_DIM, N).transpose(0, 1, 3, 2)
        k = conv1x1_bn(xx, Wk, k_scale, k_bias).reshape(B, NUM_HEADS, KEY_DIM, N)
        v = conv1x1_bn(xx, Wv, v_scale, v_bias).reshape(B, NUM_HEADS, D_HEAD, N)
        attn = jax.nn.softmax(jnp.einsum('bhnk,bhkm->bhnm', q, k), axis=-1)
        out = jnp.einsum('bhnm,bhdm->bhdn', attn, v)
        out = out.reshape(B, NUM_HEADS * D_HEAD, H, W)
        out = conv1x1_bn(jax.nn.relu(out), Wp, p_scale, p_bias)
        xres = x + out
        y = jax.nn.relu(conv1x1_bn(xres, Wo, o_scale, o_bias))
        return y

    def _L1_ffn_ref(x, gate_w, gate_b, w1, b1, w2, b2):
        import jax, jax.numpy as jnp
        import numpy as np
        NUM_EXPERTS = 4
        TOP_K = 2
        DIM = 96
        HID = 4 * DIM
        scores = jnp.einsum('bsd,de->bse', x, gate_w) + gate_b
        probs = jax.nn.softmax(scores, axis=-1)
        topk_vals, topk_idx = jax.lax.top_k(probs, TOP_K)
        mask = jnp.sum(jax.nn.one_hot(topk_idx, NUM_EXPERTS, dtype=probs.dtype), axis=-2)
        masked = probs * mask
        masked = masked / (jnp.sum(masked, axis=-1, keepdims=True) + 1e-09)
        h = jax.nn.gelu(jnp.einsum('bsd,edh->ebsh', x, w1) + b1[:, None, None, :], approximate=False)
        y = jnp.einsum('ebsh,ehd->ebsd', h, w2) + b2[:, None, None, :]
        out = jnp.einsum('bse,ebsd->bsd', masked, y)
        return out

    def _L2_conv_ref(x, w_v, b_v, w_q, b_q, w_k, b_k, w_off1, b_off1, ln_g, ln_b, w_off2, w_out):
        import jax, jax.numpy as jnp
        import numpy as np
        from jax import lax
        B, C, H, W = (4, 96, 56, 56)
        NH, HC, STRIDE = (12, 32, 2)
        SCALE = HC ** (-0.5)

        def _dwconv(x, w, b, stride):
            y = lax.conv_general_dilated(x, w, (stride, stride), [(1, 1), (1, 1)], dimension_numbers=('NCHW', 'OIHW', 'NCHW'), feature_group_count=x.shape[1])
            return y + b[None, :, None, None]

        def _grid_sample_bilinear(value, grid):
            Hh, Ww = (value.shape[2], value.shape[3])
            ix = (grid[..., 0] + 1.0) * 0.5 * (Ww - 1)
            iy = (grid[..., 1] + 1.0) * 0.5 * (Hh - 1)
            x0 = jnp.floor(ix)
            y0 = jnp.floor(iy)
            wx = ix - x0
            wy = iy - y0
            x0i = jnp.clip(x0, 0, Ww - 1).astype(jnp.int32)
            x1i = jnp.clip(x0 + 1, 0, Ww - 1).astype(jnp.int32)
            y0i = jnp.clip(y0, 0, Hh - 1).astype(jnp.int32)
            y1i = jnp.clip(y0 + 1, 0, Hh - 1).astype(jnp.int32)

            def per_b(img, y0i, y1i, x0i, x1i, wx, wy):
                v00 = img[:, y0i, x0i]
                v01 = img[:, y0i, x1i]
                v10 = img[:, y1i, x0i]
                v11 = img[:, y1i, x1i]
                return v00 * (1 - wx) * (1 - wy) + v01 * wx * (1 - wy) + v10 * (1 - wx) * wy + v11 * wx * wy
            return jax.vmap(per_b)(value, y0i, y1i, x0i, x1i, wx, wy)

        def _ref_points(Hk, Wk):
            ref_y = jnp.linspace(0.5, Hk - 0.5, Hk)
            ref_x = jnp.linspace(0.5, Wk - 0.5, Wk)
            ry, rx = jnp.meshgrid(ref_y, ref_x, indexing='ij')
            return jnp.stack([ry / Hk * 2 - 1, rx / Wk * 2 - 1], axis=-1)
        Bx, Cx, Hx, Wx = x.shape
        value = _dwconv(x, w_v, b_v, 1)
        query = _dwconv(x, w_q, b_q, 1).reshape(Bx * NH, HC, -1)
        key = _dwconv(x, w_k, b_k, STRIDE).reshape(Bx * NH, HC, -1)
        off = _dwconv(x, w_off1, b_off1, STRIDE)
        o = jnp.transpose(off, (0, 2, 3, 1))
        mu = o.mean(-1, keepdims=True)
        var = o.var(-1, keepdims=True)
        o = (o - mu) / jnp.sqrt(var + 1e-05) * ln_g + ln_b
        o = jax.nn.gelu(o, approximate=False)
        offset = jnp.einsum('bhwc,pc->bhwp', o, w_off2)
        Hk, Wk = (offset.shape[1], offset.shape[2])
        ref = _ref_points(Hk, Wk)[None]
        pos = jnp.tanh(offset + ref)
        grid = pos[..., ::-1]
        v_sampled = _grid_sample_bilinear(value, grid)
        v_sampled = v_sampled.reshape(Bx * NH, HC, -1)
        attn = jnp.einsum('bcm,bcn->bmn', query, key) * SCALE
        out = jnp.einsum('bmn,bcn->bcm', attn, v_sampled)
        out = out.reshape(Bx, Cx, Hx, Wx)
        y = jnp.einsum('bchw,oc->bohw', out, w_out)
        return y

    def _L2_ffn_ref(x, gate_w, gate_b, w1, b1, w2, b2):
        import jax, jax.numpy as jnp
        import numpy as np
        NUM_EXPERTS = 4
        TOP_K = 2
        DIM = 96
        HID = 4 * DIM
        scores = jnp.einsum('bsd,de->bse', x, gate_w) + gate_b
        probs = jax.nn.softmax(scores, axis=-1)
        topk_vals, topk_idx = jax.lax.top_k(probs, TOP_K)
        mask = jnp.sum(jax.nn.one_hot(topk_idx, NUM_EXPERTS, dtype=probs.dtype), axis=-2)
        masked = probs * mask
        masked = masked / (jnp.sum(masked, axis=-1, keepdims=True) + 1e-09)
        h = jax.nn.gelu(jnp.einsum('bsd,edh->ebsh', x, w1) + b1[:, None, None, :], approximate=False)
        y = jnp.einsum('ebsh,ehd->ebsd', h, w2) + b2[:, None, None, :]
        out = jnp.einsum('bse,ebsd->bsd', masked, y)
        return out

    def _L3_conv_ref(x, wq_dw, wq_bn_g, wq_bn_b, wq_bn_m, wq_bn_v, wq_pw, wkv_dw, wkv_bn_g, wkv_bn_b, wkv_bn_m, wkv_bn_v, wkv_pw, wo, bo):
        import jax, jax.numpy as jnp
        import numpy as np
        from jax import lax
        DIM = 96
        HEADS = 8
        DIM_HEAD = 16
        INNER = HEADS * DIM_HEAD
        K = 3
        B, H, W = (8, 56, 56)
        EPS = 1e-05
        SCALE = DIM_HEAD ** (-0.5)

        def _dw_proj(x, w_dw, bn_g, bn_b, bn_m, bn_v, w_pw):
            c_in = x.shape[1]
            y = lax.conv_general_dilated(x, w_dw, window_strides=(1, 1), padding='SAME', feature_group_count=c_in, dimension_numbers=('NCHW', 'OIHW', 'NCHW'))
            inv = bn_g / jnp.sqrt(bn_v + EPS)
            y = y * inv[None, :, None, None] + (bn_b - bn_m * inv)[None, :, None, None]
            return jnp.einsum('bchw,oc->bohw', y, w_pw)

        def _split_heads(t):
            b, _, hh, ww = t.shape
            t = t.reshape(b, HEADS, DIM_HEAD, hh * ww)
            return t.transpose(0, 1, 3, 2).reshape(b * HEADS, hh * ww, DIM_HEAD)
        b, _, hh, ww = x.shape
        q = _dw_proj(x, wq_dw, wq_bn_g, wq_bn_b, wq_bn_m, wq_bn_v, wq_pw)
        kv = _dw_proj(x, wkv_dw, wkv_bn_g, wkv_bn_b, wkv_bn_m, wkv_bn_v, wkv_pw)
        k, v = (kv[:, :INNER], kv[:, INNER:])
        q, k, v = (_split_heads(q), _split_heads(k), _split_heads(v))
        diag = (q * k).sum(-1) * SCALE
        m0_sum = diag.sum()
        ktv = jnp.einsum('bnd,bne->bde', k, v)
        out = m0_sum * v + SCALE * jnp.einsum('bnd,bde->bne', q, ktv) - diag[..., None] * v
        out = out.reshape(b, HEADS, hh * ww, DIM_HEAD).transpose(0, 1, 3, 2)
        out = out.reshape(b, INNER, hh, ww)
        return jnp.einsum('bchw,oc->bohw', out, wo) + bo[None, :, None, None]

    def _L3_ffn_ref(x, W1, b1, W2, b2):
        import jax, jax.numpy as jnp
        import numpy as np
        NUM_GROUPS = 5
        EPS = 1e-05
        QB = 128.0

        def _binarize_weights_groupwise(W):
            n_out = W.shape[0]
            gs = n_out // NUM_GROUPS
            Wb = jnp.zeros_like(W)
            for g in range(NUM_GROUPS):
                wg = W[g * gs:(g + 1) * gs]
                z = wg - wg.mean()
                ste = z + jax.lax.stop_gradient(jnp.sign(z) - z)
                Wb = Wb.at[g * gs:(g + 1) * gs].set(ste)
            return Wb

        def _quantize_activations_groupwise(x):
            n = x.shape[0]
            gs = n // NUM_GROUPS
            xq = jnp.zeros_like(x)
            for g in range(NUM_GROUPS):
                ag = x[g * gs:(g + 1) * gs]
                gamma = jnp.max(jnp.abs(ag))
                xq = xq.at[g * gs:(g + 1) * gs].set(jnp.clip(ag * QB / (gamma + EPS), -QB + EPS, QB - EPS))
            return xq

        def _bitlinear(x, W, b):
            Wb = _binarize_weights_groupwise(W)
            y = jnp.einsum('btc,oc->bto', x, Wb) + b
            return _quantize_activations_groupwise(y)
        h = _bitlinear(x, W1, b1)
        h = jax.nn.gelu(h, approximate=False)
        out = _bitlinear(h, W2, b2)
        return out

    def _gn(v, G=32, eps=1e-05):
        B_, C_, H_, W_ = v.shape
        g = v.reshape(B_, G, C_ // G, H_, W_)
        m = jnp.mean(g, axis=(2, 3, 4), keepdims=True)
        s = jnp.var(g, axis=(2, 3, 4), keepdims=True)
        return ((g - m) / jnp.sqrt(s + eps)).reshape(v.shape)

    def _ln_c(v, eps=1e-06):
        m = jnp.mean(v, axis=1, keepdims=True)
        s = jnp.var(v, axis=1, keepdims=True)
        return (v - m) / jnp.sqrt(s + eps)

    def _ln_t(v, eps=1e-05):
        m = jnp.mean(v, axis=-1, keepdims=True)
        s = jnp.var(v, axis=-1, keepdims=True)
        return (v - m) / jnp.sqrt(s + eps)

    def _to_tokens(v):
        B_, C_, H_, W_ = v.shape
        return v.reshape(B_, C_, H_ * W_).transpose(0, 2, 1)

    def _from_tokens(t, like):
        B_, C_, H_, W_ = like.shape
        return t.transpose(0, 2, 1).reshape(B_, C_, H_, W_)
    x = x + _L0_conv_ref(_ln_c(x), L0_conv_w_large, L0_conv_w_small, L0_conv_g_l, L0_conv_b_l, L0_conv_m_l, L0_conv_v_l, L0_conv_g_s, L0_conv_b_s, L0_conv_m_s, L0_conv_v_s, L0_conv_g_i, L0_conv_b_i, L0_conv_m_i, L0_conv_v_i)
    t = _to_tokens(x)
    t = t + _L0_ffn_ref(_ln_t(t), L0_ffn_gate_w, L0_ffn_gate_b, L0_ffn_w1, L0_ffn_b1, L0_ffn_w2, L0_ffn_b2)
    x = _from_tokens(t, x)
    x = x + _L1_conv_ref(_ln_c(x), L1_conv_Wq, L1_conv_q_scale, L1_conv_q_bias, L1_conv_Wk, L1_conv_k_scale, L1_conv_k_bias, L1_conv_Wv, L1_conv_v_scale, L1_conv_v_bias, L1_conv_Wp, L1_conv_p_scale, L1_conv_p_bias, L1_conv_Wo, L1_conv_o_scale, L1_conv_o_bias)
    t = _to_tokens(x)
    t = t + _L1_ffn_ref(_ln_t(t), L1_ffn_gate_w, L1_ffn_gate_b, L1_ffn_w1, L1_ffn_b1, L1_ffn_w2, L1_ffn_b2)
    x = _from_tokens(t, x)
    x = x + _L2_conv_ref(_ln_c(x), L2_conv_w_v, L2_conv_b_v, L2_conv_w_q, L2_conv_b_q, L2_conv_w_k, L2_conv_b_k, L2_conv_w_off1, L2_conv_b_off1, L2_conv_ln_g, L2_conv_ln_b, L2_conv_w_off2, L2_conv_w_out)
    t = _to_tokens(x)
    t = t + _L2_ffn_ref(_ln_t(t), L2_ffn_gate_w, L2_ffn_gate_b, L2_ffn_w1, L2_ffn_b1, L2_ffn_w2, L2_ffn_b2)
    x = _from_tokens(t, x)
    x = x + _L3_conv_ref(_ln_c(x), L3_conv_wq_dw, L3_conv_wq_bn_g, L3_conv_wq_bn_b, L3_conv_wq_bn_m, L3_conv_wq_bn_v, L3_conv_wq_pw, L3_conv_wkv_dw, L3_conv_wkv_bn_g, L3_conv_wkv_bn_b, L3_conv_wkv_bn_m, L3_conv_wkv_bn_v, L3_conv_wkv_pw, L3_conv_wo, L3_conv_bo)
    t = _to_tokens(x)
    t = t + _L3_ffn_ref(_ln_t(t), L3_ffn_W1, L3_ffn_b1, L3_ffn_W2, L3_ffn_b2)
    x = _from_tokens(t, x)
    return x

_drawn_inputs = setup_inputs


def setup_inputs(seed=0):
    import zlib

    import numpy as np

    out = dict(_drawn_inputs(seed))
    spreads = {'L0_ffn_gate_b': (0.0, 0.1),
     'L0_ffn_b1': (0.0, 0.1),
     'L0_ffn_b2': (0.0, 0.1),
     'L1_ffn_gate_b': (0.0, 0.1),
     'L1_ffn_b1': (0.0, 0.3),
     'L1_ffn_b2': (0.0, 0.1),
     'L2_conv_b_v': (0.0, 0.1),
     'L2_conv_b_q': (0.0, 0.556),
     'L2_conv_b_k': (0.0, 0.367),
     'L2_conv_b_off1': (0.0, 0.8),
     'L2_conv_ln_g': (1.0, 0.6),
     'L2_conv_ln_b': (0.0, 0.8),
     'L2_ffn_gate_b': (0.0, 0.1),
     'L2_ffn_b1': (0.0, 0.413),
     'L2_ffn_b2': (0.0, 0.335)}
    factors = {'L1_conv_q_bias': 3.946,
     'L1_conv_k_bias': 200.0,
     'L2_conv_w_off1': 8.0,
     'L2_conv_w_off2': 8.0,
     'L3_conv_bo': 200.0,
     'L3_ffn_b1': 200.0,
     'L3_ffn_b2': 200.0,
     'L3_conv_wq_bn_b': 8.0}
    for name, (base, spread) in spreads.items():
        noise = np.random.default_rng([zlib.crc32(name.encode()), seed]).standard_normal(out[name].shape)
        drawn = base * np.exp(spread * noise) if base else spread * noise
        out[name] = jnp.asarray(drawn.astype(out[name].dtype))
    for name, factor in factors.items():
        out[name] = (out[name] * factor).astype(out[name].dtype)
    return out
```

```python
from contextlib import ExitStack

import numpy as np

import concourse.bass as bass
from concourse import mybir

F32 = mybir.dt.float32
ALU = mybir.AluOpType
ACT = mybir.ActivationFunctionType
AX = mybir.AxisListType

P = 128
C = 96
CB = C + 1
NI = 16
SIDE = 16
PIX = SIDE * SIDE
NT = NI * PIX // P
HALF = C // 2
KL, KS = 13, 3
GC = P // SIDE
NG = C // GC
NE, HID = 4, 4 * C
KC = HID // P
GT = 4
GW = GT * P
HEADS, KD, DH = 6, 16, 32
DS = C // 4
BN_EPS = 1e-5


def wait(eng, sem, count):
    if isinstance(count, int) and count <= 0:
        return
    eng.wait_ge(sem, count)


class Chain:

    def __init__(self, eng, sem, start=0):
        self.eng, self.sem, self.start, self.n = eng, sem, start, 0

    def sync(self, ins):
        ins.then_inc(self.sem, 1)
        self.n += 1
        self.eng.wait_ge(self.sem, self.start + self.n)


def layernorm_stats(dve, chain, tiles, stats, mean, var, eps, rows=P):
    n = len(tiles)
    for j, tile in enumerate(tiles):
        last = dve.bn_stats(stats[0:rows, j, :], tile)
    chain.sync(last)
    s = stats[0:rows, 0:n, :]
    dve.tensor_tensor(mean[0:rows, 0:n], s[:, :, 1], s[:, :, 4], ALU.subtract)
    chain.sync(dve.tensor_tensor(var[0:rows, 0:n], s[:, :, 2], s[:, :, 5], ALU.add))
    dve.scalar_tensor_tensor(out=mean[0:rows, 0:n], in0=mean[0:rows, 0:n], scalar=0.25,
                             in1=mean[0:rows, 0:n], op0=ALU.mult, op1=ALU.mult)
    chain.sync(dve.tensor_scalar(var[0:rows, 0:n], var[0:rows, 0:n], 1.0 / C, eps, ALU.mult, ALU.add))
    chain.sync(dve.tensor_tensor(var[0:rows, 0:n], var[0:rows, 0:n], mean[0:rows, 0:n], ALU.add))


def layernorm_apply(dve, chain, tiles, outs, stats, mean, rstd, rows=P):
    n = len(tiles)
    s = stats[0:rows, 0:n, :]
    chain.sync(dve.tensor_tensor(mean[0:rows, 0:n], s[:, :, 1], s[:, :, 4], ALU.add))
    chain.sync(dve.tensor_scalar(mean[0:rows, 0:n], mean[0:rows, 0:n], 0.5, None, ALU.mult))
    for j, (tile, out) in enumerate(zip(tiles, outs)):
        last = dve.tensor_scalar(out, tile, mean[0:rows, j:j + 1], rstd[0:rows, j:j + 1],
                                 ALU.subtract, ALU.mult)
    return last


class Scope:

    def __init__(self, nc, ctx, tag):
        self.nc, self.ctx, self.tag = nc, ctx, tag

    def sb(self, name, shape):
        return self.ctx.enter_context(self.nc.sbuf_tensor(f"{self.tag}_{name}", shape, F32))

    def psum(self, name, shape):
        return self.ctx.enter_context(self.nc.psum_tensor(f"{self.tag}_{name}", shape, F32))

    def sem(self, name):
        return self.nc.alloc_semaphore(name=f"{self.tag}_{name}")


def l0_conv(nc, T, A):
    with ExitStack() as ctx:
        s = Scope(nc, ctx, "l0c")
        x0 = s.sb("x0", [P, NT, C])
        xn = s.sb("xn", [P, 2, C, SIDE])
        xt = s.sb("xt", [P, NG, NI, SIDE])
        band = s.sb("band", [P, NG, KL, SIDE])
        band_s = s.sb("band_s", [P, NG, KS, SIDE])
        full = s.sb("full", [P, NG * KL, GC, SIDE])
        bn = s.sb("bn", [P, 4, 3, NG])
        inv = s.sb("inv", [P, 3, NG])
        shift = s.sb("shift", [P, 3, NG])
        eye = s.sb("eye", [P, SIDE])
        eyes = s.sb("eyes", [P, NG, SIDE])
        own = s.sb("own", [P, GC])
        mhalf = s.sb("mhalf", [P, 3 * NG])
        stats = s.sb("stats", [P, NT, 6])
        mean = s.sb("mean", [P, NT])
        var = s.sb("var", [P, NT])
        rstd = s.sb("rstd", [P, NT])
        conv = s.sb("conv", [P, 2, PIX])
        back = s.sb("back", [P, 2, SIDE, C])
        backB = s.sb("backB", [P, NT, C])
        tp = [s.psum(f"tp{i}", [P, 512]) for i in range(2)]
        cp = [s.psum(f"cp{i}", [P, 512]) for i in range(2)]
        bp = [s.psum(f"bp{i}", [P, 512]) for i in range(2)]
        x0_in, w_in, res_in, ident_in = (s.sem(n) for n in ("x0_in", "w_in", "res_in", "ident_in"))
        mhalf_set, v_eps, bn_pow, ln_var, ln_rstd = (s.sem(n) for n in
            ("mhalf_set", "v_eps", "bn_pow", "ln_var", "ln_rstd"))
        dve_step, band_done, full_act, full_dve, xn_done = (s.sem(n) for n in
            ("dve_step", "band_done", "full_act", "full_dve", "xn_done"))
        turned, xt_done, conv_done, conv_out, back_done, back_out = (s.sem(n) for n in
            ("turned", "xt_done", "conv_done", "conv_out", "back_done", "back_out"))
        stored, reread = s.sem("stored"), s.sem("reread")
        block = ctx.enter_context(nc.Block())

        @block.sync
        def _(sp):
            sp.dma_start(x0[:, :, :], A["x_rows"]).then_inc(x0_in, 16)
            sp.dma_start(T["ident"][:, :], A["ident"]).then_inc(ident_in, 16)
            sp.dma_start(T["X"][:, :, :], A["x_tokens"]).then_inc(res_in, 16)
            for n, (w1, w2, gw, b2) in enumerate(T["moe"]):
                sp.dma_start(w1[:, :, :], A[f"w1_{n}"]).then_inc(T["moe_in"][n], 16)
                sp.dma_start(w2[:, :, :], A[f"w2_{n}"]).then_inc(T["moe_in"][n], 16)
                sp.dma_start(gw[:, :], A[f"gw_{n}"]).then_inc(T["moe_in"][n], 16)
                sp.dma_start(b2[:, :, :], A[f"b2_{n}"]).then_inc(T["moe_in"][n], 16)
            sp.wait_ge(back_out, NG)
            for h in range(2):
                sp.dma_start(T["scratch"][h * (NI // 2) * PIX:(h + 1) * (NI // 2) * PIX, :]
                             .rearrange("(p x) c -> p x c", x=SIDE), back[:, h, :, :]).then_inc(stored, 16)
            sp.wait_ge(stored, 32)
            sp.dma_start(backB[:, :, :], T["scratch"].rearrange("(t p) c -> p t c", p=P)).then_inc(reread, 16)

        @block.gpsimd
        def _(pool):
            pool.memset(mhalf[:, :], -0.5).then_inc(mhalf_set, 1)
            pool.wait_ge(mhalf_set, 1)
            pool.wait_ge(v_eps, 1)
            pool.tensor_tensor(inv[:, :, :], shift[:, :, :], mhalf[:, :].rearrange("p (k g) -> p k g", k=3),
                               ALU.pow).then_inc(bn_pow, 1)
            pool.wait_ge(ln_var, 1)
            pool.tensor_tensor(rstd[:, :], var[:, :], mhalf[:, 0:NT], ALU.pow).then_inc(ln_rstd, 1)

        @block.scalar
        def _(act):
            act.dma_start(bn[:, :, :, :], A["bn"]).then_inc(w_in, 16)
            act.dma_start(band[:, :, :, :], A["band"]).then_inc(w_in, 16)
            act.dma_start(band_s[:, :, :, :], A["band_s"]).then_inc(w_in, 16)
            act.dma_start(eye[:, :], A["eye"]).then_inc(w_in, 16)
            act.dma_start(own[:, :], A["own"]).then_inc(w_in, 16)
            act.wait_ge(band_done, 1)
            for k in range(0, GC, 2):
                act.activation(full[:, :, k, :], band[:, :, :, :].rearrange("p g r x -> p (g r) x"), ACT.Copy,
                               scale=own[:, k:k + 1]).then_inc(full_act, 1)
            for g2 in range(NG // 2):
                act.wait_ge(turned, g2 + 1)
                act.activation(xt[:, 2 * g2:2 * g2 + 2, :, :].rearrange("p g i r -> p (g i r)"), tp[g2 % 2][:, :],
                               ACT.Copy).then_inc(xt_done, 1)
            for g in range(NG):
                act.wait_ge(conv_done, g + 1)
                if g >= 2:
                    act.wait_ge(back_done, g - 1)
                act.activation(conv[:, g % 2, :], cp[g % 2][:, 0:PIX], ACT.Identity,
                               bias=shift[:, 0, g:g + 1]).then_inc(conv_out, 1)

        @block.vector
        def _(dve):
            chain = Chain(dve, dve_step)
            dve.wait_ge(w_in, 80)
            chain.sync(dve.tensor_scalar(shift[:, :, :], bn[:, 3, :, :], BN_EPS, None, ALU.add))
            dve.sem_inc(v_eps, 1)
            dve.wait_ge(x0_in, 16)
            tiles = [x0[:, t, :] for t in range(NT)]
            layernorm_stats(dve, chain, tiles, stats, mean, var, 1e-6)
            dve.sem_inc(ln_var, 1)
            dve.wait_ge(bn_pow, 1)
            chain.sync(dve.tensor_tensor(inv[:, :, :], inv[:, :, :], bn[:, 0, :, :], ALU.mult))
            chain.sync(dve.tensor_tensor(shift[:, :, :], bn[:, 2, :, :], inv[:, :, :], ALU.mult))
            chain.sync(dve.tensor_tensor(shift[:, :, :], bn[:, 1, :, :], shift[:, :, :], ALU.subtract))
            chain.sync(dve.tensor_tensor(shift[:, 0, :], shift[:, 0, :], shift[:, 1, :], ALU.add))
            chain.sync(dve.tensor_tensor(shift[:, 0, :], shift[:, 0, :], shift[:, 2, :], ALU.add))
            bv = band[:, :, :, :].rearrange("p g r x -> p g (r x)")
            sv = band_s[:, :, :, :].rearrange("p g r x -> p g (r x)")
            dve.tensor_tensor(bv, bv, inv[:, 0, :].unsqueeze(2).broadcast_to([P, NG, KL * SIDE]), ALU.mult)
            dve.tensor_tensor(sv, sv, inv[:, 1, :].unsqueeze(2).broadcast_to([P, NG, KS * SIDE]), ALU.mult)
            chain.sync(dve.tensor_tensor(eyes[:, :, :], eye[:, :].unsqueeze(1).broadcast_to([P, NG, SIDE]),
                                         inv[:, 2, :].unsqueeze(2).broadcast_to([P, NG, SIDE]), ALU.mult))
            mid = (KL - KS) // 2
            inner = band[:, :, mid:mid + KS, :].rearrange("p g r x -> p g (r x)")
            chain.sync(dve.tensor_tensor(inner, inner, sv, ALU.add))
            chain.sync(dve.tensor_tensor(band[:, :, KL // 2, :], band[:, :, KL // 2, :], eyes[:, :, :], ALU.add))
            dve.sem_inc(band_done, 1)
            dve.wait_ge(ln_rstd, 1)
            layernorm_apply(dve, chain, tiles, [xn[:, t // SIDE, :, t % SIDE] for t in range(NT)],
                            stats, mean, rstd).then_inc(xn_done, 1)
            for k in range(1, GC, 2):
                last = dve.tensor_scalar(full[:, :, k, :], band[:, :, :, :].rearrange("p g r x -> p (g r) x"),
                                         own[:, k:k + 1], None, ALU.mult)
            last.then_inc(full_dve, 1)
            for g in range(NG):
                dve.wait_ge(back_done, g + 1)
                dve.tensor_copy(back[:, :, :, GC * g:GC * (g + 1)],
                                bp[g % 2][:, 0:PIX].rearrange("p (h c x) -> p h x c", h=2, x=SIDE)
                                ).then_inc(back_out, 1)
            dve.wait_ge(res_in, 16)
            dve.wait_ge(reread, 16)
            dve.tensor_tensor(T["X"][:, :, :], T["X"][:, :, :], backB[:, :, :], ALU.add)

        @block.tensor
        def _(pe):
            ident = T["ident"]
            pe.wait_ge(ident_in, 16)
            pe.wait_ge(xn_done, 1)
            for g2 in range(NG // 2):
                if g2 >= 2:
                    pe.wait_ge(xt_done, g2 - 1)
                for k in range(4):
                    g, h = 2 * g2 + k // 2, k % 2
                    last = pe.transpose(tp[g2 % 2][:, k * P:(k + 1) * P], xn[:, h, GC * g:GC * (g + 1), :]
                                        .rearrange("p c x -> p (c x)"), ident[:, :])
                last.then_inc(turned, 1)
            pe.wait_ge(full_act, GC // 2)
            pe.wait_ge(full_dve, 1)

            def conv_group(g):
                pe.wait_ge(xt_done, g // 2 + 1)
                if g >= 2:
                    pe.wait_ge(conv_out, g - 1)
                out = cp[g % 2][:, 0:PIX].rearrange("p (i r) -> p i r", r=SIDE)
                order = [KL // 2] + [r for r in range(KL) if r != KL // 2]
                for n, r in enumerate(order):
                    d = r - KL // 2
                    lo, hi = max(0, -d), min(SIDE, SIDE - d)
                    last = pe.matmul(out[:, :, lo:hi], full[:, g * KL + r, :, :].rearrange("p c x -> p (c x)"),
                                     xt[:, g, :, lo + d:hi + d], start=(n == 0), stop=(n == KL - 1))
                last.then_inc(conv_done, 1)

            def turn_back(g):
                pe.wait_ge(conv_out, g + 1)
                if g >= 2:
                    pe.wait_ge(back_out, g - 1)
                for h in range(2):
                    last = pe.transpose(bp[g % 2][:, h * P:(h + 1) * P], conv[:, g % 2, h * P:(h + 1) * P],
                                        ident[:, :])
                last.then_inc(back_done, 1)

            conv_group(0)
            for g in range(NG):
                if g + 1 < NG:
                    conv_group(g + 1)
                turn_back(g)


def moe(nc, T, A, layer):
    w1, w2, gw, b2 = T["moe"][layer]
    X, ident = T["X"], T["ident"]
    STEPS = NT // GT
    UPS = 4
    with ExitStack() as ctx:
        s = Scope(nc, ctx, f"moe{layer}")
        xn = s.sb("xn", [P, GT, C])
        xt = s.sb("xt", [CB, GW])
        hid = s.sb("hid", [P, NE * KC, GW])
        stats = s.sb("stats", [P, GT, 6])
        mean = s.sb("mean", [P, GT])
        var = s.sb("var", [P, GT])
        rstd = s.sb("rstd", [P, GT])
        mhalf = s.sb("mhalf", [P, GT])
        euler = s.sb("euler", [P, GT * NE])
        smax = s.sb("smax", [P, GT])
        logit = s.sb("logit", [P, GT, NE])
        prob = s.sb("prob", [P, GT, NE])
        ge = s.sb("ge", [P, 3, GT, NE])
        rank = s.sb("rank", [P, GT, NE])
        gate = s.sb("gate", [P, GT, NE])
        up = [s.psum(f"up{i}", [P, 512]) for i in range(UPS)]
        tp = s.psum("tp", [P, 512])
        gp = s.psum("gp", [P, 512])
        dn = [s.psum(f"dn{i}", [P, 512]) for i in range(2)]
        names = ("consts", "var_done", "rstd_done", "logit_done", "exp_done", "dve_step", "xn_done", "turned",
                 "xt_done", "gates_in", "gates_read", "up_done", "hid_done", "down_done", "added")
        (consts, var_done, rstd_done, logit_done, exp_done, dve_step, xn_done, turned,
         xt_done, gates_in, gates_read, up_done, hid_done, down_done, added) = (s.sem(n) for n in names)
        block = ctx.enter_context(nc.Block())

        @block.gpsimd
        def _(pool):
            pool.memset(mhalf[:, :], -0.5)
            pool.memset(euler[:, :], float(np.e)).then_inc(consts, 1)
            pool.wait_ge(consts, 1)

            def rstd_of(g):
                pool.wait_ge(var_done, g + 1)
                pool.tensor_tensor(rstd[:, :], var[:, :], mhalf[:, :], ALU.pow).then_inc(rstd_done, 1)

            def exp_of(g):
                pool.wait_ge(logit_done, g + 1)
                pool.tensor_tensor(prob[:, :, :], euler[:, :].rearrange("p (t e) -> p t e", e=NE),
                                   logit[:, :, :], ALU.pow).then_inc(exp_done, 1)

            with pool.Fori(0, STEPS) as g:
                rstd_of(g)
                exp_of(g)

        @block.vector
        def _(dve):
            dve.memset(xt[C:CB, :], 1.0)
            STATS, APPLY, GATES, SUM = 4, 2, 15, 2 * NE - 1

            def before(g, part):
                prep = STATS + APPLY + GATES
                n = prep + g * (SUM + 1 + prep)
                at = {"sum": 0, "e0": NE, "stats": NE + 1, "e1": NE + 1 + STATS,
                      "apply": NE + 2 + STATS, "e2": NE + 2 + STATS + APPLY, "e3": NE + 3 + STATS + APPLY,
                      "gates": NE + 4 + STATS + APPLY}
                return n + at[part]

            def stats_of(g, start):
                chain = Chain(dve, dve_step, start)
                layernorm_stats(dve, chain, [X[:, GT * g + j, :] for j in range(GT)], stats, mean, var, 1e-5)
                dve.sem_inc(var_done, 1)
                assert chain.n == STATS, chain.n

            def apply_of(g, start):
                chain = Chain(dve, dve_step, start)
                wait(dve, rstd_done, g + 1)
                wait(dve, turned, g)
                layernorm_apply(dve, chain, [X[:, GT * g + j, :] for j in range(GT)],
                                [xn[:, j, :] for j in range(GT)], stats, mean, rstd).then_inc(xn_done, 1)
                assert chain.n == APPLY

            def gates_of(g, start):
                chain = Chain(dve, dve_step, start)
                wide = lambda a: a.unsqueeze(2).broadcast_to([P, GT, NE])
                scores = gp[:, 0:GT * NE].rearrange("p (t e) -> p t e", e=NE)
                dve.wait_ge(gates_in, g + 1)
                chain.sync(dve.tensor_reduce(smax[:, :], scores, AX.X, ALU.max))
                chain.sync(dve.tensor_tensor(logit[:, :, :], scores, wide(smax[:, :]), ALU.subtract))
                dve.sem_inc(logit_done, 1)
                dve.sem_inc(gates_read, 1)
                dve.wait_ge(exp_done, g + 1)
                chain.sync(dve.tensor_reduce(smax[:, :], prob[:, :, :], AX.X, ALU.add))
                chain.sync(dve.reciprocal(smax[:, :], smax[:, :]))
                chain.sync(dve.tensor_tensor(prob[:, :, :], prob[:, :, :], wide(smax[:, :]), ALU.mult))
                for d in range(1, NE):
                    dve.tensor_tensor(ge[:, d - 1, :, 0:NE - d], prob[:, :, 0:NE - d], prob[:, :, d:NE], ALU.is_ge)
                for e in range(NE):
                    last = dve.memset(rank[:, :, e], float(NE - 1 - e))
                chain.sync(last)
                for d in range(1, NE):
                    ahead = ge[:, d - 1, :, 0:NE - d]
                    last = dve.tensor_tensor(rank[:, :, d:NE], rank[:, :, d:NE], ahead, ALU.add)
                    if d < NE / 2:
                        chain.sync(last)
                    chain.sync(dve.tensor_tensor(rank[:, :, 0:NE - d], rank[:, :, 0:NE - d], ahead, ALU.subtract))
                chain.sync(dve.scalar_tensor_tensor(
                    out=gate[:, :, :].rearrange("p t e -> p (t e)"), in0=rank[:, :, :].rearrange("p t e -> p (t e)"),
                    scalar=2.0, in1=prob[:, :, :].rearrange("p t e -> p (t e)"), op0=ALU.is_lt, op1=ALU.mult))
                chain.sync(dve.tensor_reduce(smax[:, :], gate[:, :, :], AX.X, ALU.add))
                chain.sync(dve.tensor_scalar(smax[:, :], smax[:, :], 1e-9, None, ALU.add))
                chain.sync(dve.reciprocal(smax[:, :], smax[:, :]))
                chain.sync(dve.tensor_tensor(gate[:, :, :], gate[:, :, :], wide(smax[:, :]), ALU.mult))
                assert chain.n == GATES, chain.n

            def bias_sums(g, start):
                chain = Chain(dve, dve_step, start)
                for e in range(NE):
                    for j in range(GT):
                        x = X[:, GT * g + j, :]
                        last = dve.scalar_tensor_tensor(out=x, in0=b2[:, e, :], scalar=gate[:, j, e:e + 1], in1=x,
                                                        op0=ALU.mult, op1=ALU.add)
                    chain.sync(last)

            def expert_sum(g, e, start):
                chain = Chain(dve, dve_step, start)
                dve.wait_ge(down_done, NE * g + e + 1)
                for j in range(GT):
                    x = X[:, GT * g + j, :]
                    last = dve.scalar_tensor_tensor(out=x, in0=dn[e % 2][:, j * C:(j + 1) * C],
                                                    scalar=gate[:, j, e:e + 1], in1=x, op0=ALU.mult, op1=ALU.add)
                chain.sync(last)
                dve.sem_inc(added, 1)

            def step(g, last):
                bias_sums(g, before(g, "sum"))
                expert_sum(g, 0, before(g, "e0"))
                n = -STATS if last else 0
                m = -STATS - APPLY if last else 0
                if not last:
                    stats_of(g + 1, before(g, "stats"))
                expert_sum(g, 1, before(g, "e1") + n)
                if not last:
                    apply_of(g + 1, before(g, "apply"))
                expert_sum(g, 2, before(g, "e2") + m)
                expert_sum(g, 3, before(g, "e3") + m)
                if not last:
                    gates_of(g + 1, before(g, "gates"))

            dve.wait_ge(consts, 1)
            stats_of(0, 0)
            apply_of(0, STATS)
            dve.wait_ge(T["moe_in"][layer], 64)
            gates_of(0, STATS + APPLY)
            with dve.Fori(0, STEPS - 1) as g:
                step(g, False)
            step(STEPS - 1, True)

        @block.scalar
        def _(act):
            def gelus(g, e):
                for k in range(KC):
                    n = e * KC + k
                    if k == 0:
                        wait(act, down_done, NE * (g - 1) + e + 1)
                    wait(act, up_done, NE * KC * g + n + 1)
                    act.activation(hid[:, n, :], up[n % UPS][:, :], ACT.Gelu).then_inc(hid_done, 1)

            def turned_out(g):
                act.wait_ge(turned, g + 1)
                wait(act, up_done, NE * KC * g)
                act.activation(xt[0:C, :], tp[0:C, :], ACT.Copy).then_inc(xt_done, 1)

            turned_out(0)
            gelus(0, 0)

            def step(g, last, first=False):
                for e in range(1, NE):
                    gelus(g, e)
                if not last:
                    turned_out(g + 1)
                    gelus(g + 1, 0)

            step(0, False)
            with act.Fori(1, STEPS - 1) as g:
                step(g, False)
            step(STEPS - 1, True)

        @block.tensor
        def _(pe):
            def turn(g):
                pe.wait_ge(xn_done, g + 1)
                wait(pe, xt_done, g)
                for j in range(GT):
                    last = pe.transpose(tp[0:C, j * P:(j + 1) * P], xn[:, j, :], ident[:, :])
                last.then_inc(turned, 1)

            def gates(g):
                pe.wait_ge(xt_done, g + 1)
                wait(pe, gates_read, g)
                for j in range(GT):
                    last = pe.matmul(gp[:, j * NE:(j + 1) * NE], xt[:, j * P:(j + 1) * P], gw[:, :],
                                     start=True, stop=True)
                last.then_inc(gates_in, 1)

            def ups(g, e):
                for k in range(KC):
                    n = e * KC + k
                    wait(pe, hid_done, NE * KC * g + n - UPS + 1)
                    pe.matmul(up[n % UPS][:, :], w1[:, n, :], xt[:, :], start=True, stop=True).then_inc(up_done, 1)

            def downs(g, e):
                pe.wait_ge(hid_done, NE * KC * g + (e + 1) * KC)
                wait(pe, added, NE * g + e - 1)
                for j in range(GT):
                    for k in range(KC):
                        n = e * KC + k
                        last = pe.matmul(dn[e % 2][:, j * C:(j + 1) * C], hid[:, n, j * P:(j + 1) * P], w2[:, n, :],
                                         start=(k == 0), stop=(k == KC - 1))
                last.then_inc(down_done, 1)

            def step(g, last):
                for e in range(1, NE):
                    ups(g, e)
                    if e < NE - 1:
                        downs(g, e - 1)
                if not last:
                    turn(g + 1)
                downs(g, NE - 2)
                if not last:
                    gates(g + 1)
                    ups(g + 1, 0)
                downs(g, NE - 1)

            pe.wait_ge(T["moe_in"][layer], 64)
            turn(0)
            gates(0)
            ups(0, 0)
            step(0, False)
            with pe.Fori(1, STEPS - 1) as g:
                step(g, False)
            step(STEPS - 1, True)


def l1_attention(nc, T, A):
    X, ident = T["X"], T["ident"]
    H, NB = HEADS, NI
    with ExitStack() as ctx:
        s = Scope(nc, ctx, "l1c")
        wq = s.sb("wq", [CB, 2, P])
        wk = s.sb("wk", [CB, 2, P])
        qk_sb = s.sb("qk_sb", [P, 2, 2, 2])
        wv = s.sb("wv", [CB, H * DH])
        sv = s.sb("sv", [C, H * DH])
        wp = s.sb("wp", [C, 2, DS])
        sp_ = s.sb("sp", [DS, 2])
        wo = s.sb("wo", [DS, C])
        wx = s.sb("wx", [CB, C])
        so = s.sb("so", [C, C])
        xn = s.sb("xn", [P, 2, 2, C])
        xi = s.sb("xi", [CB, 2, PIX])
        qs = s.sb("qs", [P, 2, 2, PIX])
        ks = s.sb("ks", [P, 2, 2, PIX])
        vs = s.sb("vs", [P, 2, 2, H * DH])
        prob = s.sb("prob", [P, 2, 2, PIX])
        pt = s.sb("pt", [P, 2, 2, PIX])
        nmax = s.sb("nmax", [P, 2, 2])
        sums = s.sb("sums", [P, 2, H, 2])
        rinv = s.sb("rinv", [P, 2, H])
        ro = s.sb("ro", [P, 2, H * DH])
        rt = s.sb("rt", [C, 2, PIX])
        u = s.sb("u", [DS, PIX])
        stats = s.sb("stats", [P, 2, 6])
        mean = s.sb("mean", [P, 2])
        var = s.sb("var", [P, 2])
        rstd = s.sb("rstd", [P, 2])
        mhalf = s.sb("mhalf", [P, 2])
        sc_ps = [s.psum(f"sc{i}", [P, 512]) for i in range(2)]
        tr_ps = [s.psum(f"tr{i}", [P, 512]) for i in range(2)]
        o_ps = [s.psum(f"o{i}", [P, 512]) for i in range(2)]
        m1 = s.psum("m1", [P, 512])
        m2 = s.psum("m2", [P, 512])
        names = ("w_in", "consts", "w_ready", "var_done", "rstd_done", "dve_step", "xn_done", "scored", "maxed",
                 "exped", "turned", "pt_done", "valued", "ro_done", "m1_in", "m2_in", "m1_out", "m2_out")
        (w_in, consts, w_ready, var_done, rstd_done, dve_step, xn_done, scored, maxed,
         exped, turned, pt_done, valued, ro_done, m1_in, m2_in, m1_out, m2_out) = (s.sem(n) for n in names)
        block = ctx.enter_context(nc.Block())
        loads = [(wq, "l1_wq"), (wk, "l1_wk"), (qk_sb, "l1_qk"), (wv, "l1_wv"), (sv, "l1_sv"), (wp, "l1_wp"),
                 (sp_, "l1_sp"), (wo, "l1_wo"), (wx, "l1_wx"), (so, "l1_so")]
        ODD = 1

        def images(eng, body):
            body(0, 0, True, False)
            with eng.Fori(0, NB // 2 - 1) as i:
                body(2 * i + ODD, 1, False, False)
                body(2 * i + ODD + 1, 0, False, False)
            body(NB - 1, 1, False, True)

        def tokens_n(b):
            return 3 * b + 1 if isinstance(b, int) and b <= 1 else 4 * b

        def tail_n(b):
            return 4 * NB if isinstance(b, int) and b == NB - 1 else 4 * b + 7

        def keys_n(b):
            return b + 1 if isinstance(b, int) and b <= 1 else 3 * b - 1

        def wp_n(b):
            return 3 * NB - 1 if isinstance(b, int) and b == NB - 1 else 3 * b + 3

        @block.sync
        def _(sp):
            for t, name in loads:
                sp.dma_start(t[tuple(slice(None) for _ in t.shape)], A[name]).then_inc(w_in, 16)

        @block.gpsimd
        def _(pool):
            pool.memset(mhalf[:, :], -0.5).then_inc(consts, 1)
            pool.wait_ge(consts, 1)
            with pool.Fori(0, NB) as b:
                pool.wait_ge(var_done, b + 1)
                pool.tensor_tensor(rstd[:, :], var[:, :], mhalf[:, :], ALU.pow).then_inc(rstd_done, 1)

        @block.vector
        def _(dve):
            PREP, TAIL = 6, 4

            def ln(b, p, start):
                chain = Chain(dve, dve_step, start)
                tiles = [X[:, 2 * b + t, :] for t in range(2)]
                layernorm_stats(dve, chain, tiles, stats, mean, var, 1e-6)
                dve.sem_inc(var_done, 1)
                wait(dve, rstd_done, b + 1)
                layernorm_apply(dve, chain, tiles, [xn[:, p, t, :] for t in range(2)], stats, mean, rstd
                                ).then_inc(xn_done, 1)
                assert chain.n == PREP

            def row_max(b, h):
                n = H * b + h
                dve.wait_ge(scored, n + 1)
                wait(dve, exped, 2 * (n - 1))
                dve.tensor_reduce(nmax[:, h % 2, :], sc_ps[h % 2][:, :].rearrange("p (t m) -> p t m", t=2),
                                  AX.X, ALU.max, negate=True).then_inc(maxed, 1)

            def turned_out(b, h):
                n = H * b + h
                wait(dve, turned, n + 1)
                wait(dve, valued, n - 1)
                dve.tensor_copy(pt[:, h % 2, :, :].rearrange("p m n -> p (m n)"), tr_ps[h % 2][:, :]
                                ).then_inc(pt_done, 1)

            def norm_heads(b, p, start):
                chain = Chain(dve, dve_step, start)
                wait(dve, exped, 2 * H * (b + 1))
                chain.sync(dve.reciprocal(rinv[:, :, :], sums[:, p, :, :].rearrange("p h t -> p t h")))
                wait(dve, valued, H * (b + 1))
                for t in range(2):
                    last = dve.scalar_tensor_tensor(
                        out=ro[:, t, :].rearrange("p (h d) -> p h d", h=H),
                        in0=o_ps[p][:, t * H * DH:(t + 1) * H * DH].rearrange("p (h d) -> p h d", h=H), scalar=0.0,
                        in1=rinv[:, t, :].unsqueeze(2).broadcast_to([P, H, DH]), op0=ALU.max, op1=ALU.mult)
                last.then_inc(ro_done, 1)

            def wp_out(b):
                wait(dve, m2_in, wp_n(b))
                dve.tensor_scalar(u[:, :], m2[0:DS, 0:PIX], sp_[:, 0:1], sp_[:, 1:2], ALU.mult, ALU.add
                                  ).then_inc(m2_out, 1)

            def wo_out(b):
                wait(dve, m2_in, wp_n(b) + 1)
                for t in range(2):
                    x = X[:, 2 * b + t, :]
                    last = dve.scalar_tensor_tensor(out=x, in0=m2[:, t * C:(t + 1) * C], scalar=0.0, in1=x,
                                                    op0=ALU.max, op1=ALU.add)
                last.then_inc(m2_out, 1)

            def tokens_out(b, p):
                wait(dve, m1_in, tokens_n(b))
                if not isinstance(b, int) or b >= 2:
                    wait(dve, m2_in, wp_n(b - 2) + 1)
                dve.tensor_scalar(xi[0:C, p, :], m1[0:C, 0:PIX], 1.0, None, ALU.mult).then_inc(m1_out, 1)

            def keys_out(b, p):
                wait(dve, m2_in, keys_n(b))
                wait(dve, scored, H * (b - 1))
                dve.tensor_scalar(ks[:, p, 0, :], m2[:, 0:PIX], qk_sb[:, 0, 1, 0:1], qk_sb[:, 1, 1, 0:1],
                                  ALU.mult, ALU.add)
                dve.tensor_scalar(ks[0:2 * DH, p, 1, :], m2[0:2 * DH, PIX:2 * PIX], qk_sb[0:2 * DH, 0, 1, 1:2],
                                  qk_sb[0:2 * DH, 1, 1, 1:2], ALU.mult, ALU.add).then_inc(m2_out, 1)

            def at(b, part):
                if part == "heads":
                    return PREP + PREP + (b - 1) * (PREP + 1)
                return PREP + b * (PREP + 1) if isinstance(b, int) and b == 0 else PREP + PREP + (b - 1) * (
                    PREP + 1) + 1

            def body(b, p, first, last):
                row_max(b, 1)
                turned_out(b, 0)
                if not first:
                    norm_heads(b - 1, 1 - p, at(b, "heads"))
                row_max(b, 2)
                if not last:
                    ln(b + 1, 1 - p, at(b, "ln"))
                turned_out(b, 1)
                row_max(b, 3)
                turned_out(b, 2)
                if not first:
                    wp_out(b - 1)
                row_max(b, 4)
                turned_out(b, 3)
                if not last:
                    tokens_out(b + 1, 1 - p)
                if not first:
                    wo_out(b - 1)
                row_max(b, 5)
                turned_out(b, 4)
                if not last:
                    keys_out(b + 1, 1 - p)
                    row_max(b + 1, 0)
                turned_out(b, 5)

            dve.memset(xi[C:CB, :, :], 1.0)
            dve.wait_ge(w_in, 16 * len(loads))
            dve.tensor_tensor(wv[0:C, :], wv[0:C, :], sv[:, :], ALU.mult)
            dve.tensor_tensor(wx[0:C, :], wx[0:C, :], so[:, :], ALU.mult)
            dve.tensor_tensor(wo[:, :], wo[:, :], so[0:DS, :], ALU.mult).then_inc(w_ready, 1)
            ln(0, 0, 0)
            tokens_out(0, 0)
            keys_out(0, 0)
            row_max(0, 0)
            images(dve, body)
            norm_heads(NB - 1, 1, PREP + PREP + (NB - 1) * (PREP + 1) - PREP)
            wp_out(NB - 1)
            wo_out(NB - 1)

        @block.scalar
        def _(act):
            def exps(b, p, h):
                n = H * b + h
                act.wait_ge(maxed, n + 1)
                wait(act, turned, n - 1)
                if h == 0:
                    wait(act, ro_done, b - 1)
                for t in range(2):
                    act.activation(prob[:, h % 2, t, :], sc_ps[h % 2][:, t * PIX:(t + 1) * PIX], ACT.Exp,
                                   bias=nmax[:, h % 2, t:t + 1], accum_out=sums[:, p, h, t:t + 1]).then_inc(exped, 1)

            def heads_out(b):
                wait(act, m1_in, tail_n(b))
                wait(act, m2_in, wp_n(b - 1))
                act.activation(rt[:, :, :].rearrange("p a n -> p (a n)"), m1[0:C, :], ACT.Copy).then_inc(m1_out, 1)

            def queries_out(b, p):
                wait(act, m1_in, tokens_n(b) + 1)
                wait(act, scored, H * (b - 1))
                act.activation(qs[:, p, 0, :], m1[:, 0:PIX], ACT.Identity, scale=qk_sb[:, 0, 0, 0:1],
                               bias=qk_sb[:, 1, 0, 0:1])
                act.activation(qs[0:2 * DH, p, 1, :], m1[0:2 * DH, PIX:2 * PIX], ACT.Identity,
                               scale=qk_sb[0:2 * DH, 0, 0, 1:2], bias=qk_sb[0:2 * DH, 1, 0, 1:2]).then_inc(m1_out, 1)

            def values_out(b, p):
                wait(act, m1_in, tokens_n(b) + 2)
                wait(act, valued, H * (b - 1))
                act.activation(vs[:, p, :, :].rearrange("p t c -> p (t c)"), m1[:, 0:2 * H * DH], ACT.Copy
                               ).then_inc(m1_out, 1)

            def body(b, p, first, last):
                exps(b, p, 1)
                if not first:
                    heads_out(b - 1)
                exps(b, p, 2)
                exps(b, p, 3)
                exps(b, p, 4)
                if not last:
                    queries_out(b + 1, 1 - p)
                exps(b, p, 5)
                if not last:
                    values_out(b + 1, 1 - p)
                    exps(b + 1, 1 - p, 0)

            act.wait_ge(w_in, 16 * len(loads))
            queries_out(0, 0)
            values_out(0, 0)
            exps(0, 0, 0)
            images(act, body)
            heads_out(NB - 1)

        @block.tensor
        def _(pe):
            def scores(b, p, h):
                n = H * b + h
                if h == 0:
                    wait(pe, m1_out, tokens_n(b) + 1)
                    wait(pe, m2_out, keys_n(b))
                wait(pe, exped, 2 * (n - 1))
                lo, g = DH * (h % 4), h // 4
                for t in range(2):
                    last = pe.matmul(sc_ps[h % 2][:, t * PIX:(t + 1) * PIX], qs[lo:lo + KD, p, g, t * P:(t + 1) * P],
                                     ks[lo:lo + KD, p, g, :], start=True, stop=True)
                last.then_inc(scored, 1)

            def turn(b, h):
                n = H * b + h
                pe.wait_ge(exped, 2 * (n + 1))
                wait(pe, pt_done, n - 1)
                for t in range(2):
                    for m in range(2):
                        last = pe.transpose(tr_ps[h % 2][:, m * PIX + t * P:m * PIX + (t + 1) * P],
                                            prob[:, h % 2, t, m * P:(m + 1) * P], ident[:, :])
                last.then_inc(turned, 1)

            def values(b, p, h):
                n = H * b + h
                wait(pe, pt_done, n + 1)
                if h == 0:
                    wait(pe, m1_out, tokens_n(b) + 2)
                    wait(pe, ro_done, b - 1)
                for t in range(2):
                    for m in range(2):
                        last = pe.matmul(o_ps[p][:, (t * H + h) * DH:(t * H + h + 1) * DH],
                                         pt[:, h % 2, m, t * P:(t + 1) * P], vs[:, p, m, h * DH:(h + 1) * DH],
                                         start=(m == 0), stop=(m == 1))
                last.then_inc(valued, 1)

            def turn_heads(b):
                wait(pe, ro_done, b + 1)
                wait(pe, m1_out, tail_n(b) - 1)
                for a in range(2):
                    for t in range(2):
                        last = pe.transpose(m1[0:C, a * PIX + t * P:a * PIX + (t + 1) * P],
                                            ro[:, t, a * C:(a + 1) * C], ident[:, :])
                last.then_inc(m1_in, 1)

            def mix_heads(b):
                wait(pe, m1_out, tail_n(b))
                wait(pe, m2_out, wp_n(b) - 1)
                for a in range(2):
                    last = pe.matmul(m2[0:DS, 0:PIX], wp[:, a, :], rt[:, a, :], start=(a == 0), stop=(a == 1))
                last.then_inc(m2_in, 1)

            def mix_out(b, p):
                wait(pe, m2_out, wp_n(b))
                for t in range(2):
                    pe.matmul(m2[:, t * C:(t + 1) * C], u[:, t * P:(t + 1) * P], wo[:, :], start=True, stop=False)
                    last = pe.matmul(m2[:, t * C:(t + 1) * C], xi[:, p, t * P:(t + 1) * P], wx[:, :],
                                     start=False, stop=True)
                last.then_inc(m2_in, 1)

            def turn_tokens(b, p):
                wait(pe, xn_done, b + 1)
                wait(pe, m1_out, tokens_n(b) - 1)
                for t in range(2):
                    last = pe.transpose(m1[0:C, t * P:(t + 1) * P], xn[:, p, t, :], ident[:, :])
                last.then_inc(m1_in, 1)

            def queries(b, p):
                wait(pe, m1_out, tokens_n(b))
                pe.matmul(m1[:, 0:PIX], wq[:, 0, :], xi[:, p, :], start=True, stop=True)
                pe.matmul(m1[0:2 * DH, PIX:2 * PIX], wq[:, 1, 0:2 * DH], xi[:, p, :], start=True, stop=True
                          ).then_inc(m1_in, 1)

            def keys(b, p):
                wait(pe, m2_out, keys_n(b) - 1)
                pe.matmul(m2[:, 0:PIX], wk[:, 0, :], xi[:, p, :], start=True, stop=True)
                pe.matmul(m2[0:2 * DH, PIX:2 * PIX], wk[:, 1, 0:2 * DH], xi[:, p, :], start=True, stop=True
                          ).then_inc(m2_in, 1)

            def value_tokens(b, p):
                wait(pe, m1_out, tokens_n(b) + 1)
                for t in range(2):
                    last = pe.matmul(m1[:, t * H * DH:(t + 1) * H * DH], xi[:, p, t * P:(t + 1) * P], wv[:, :],
                                     start=True, stop=True)
                last.then_inc(m1_in, 1)

            def body(b, p, first, last):
                scores(b, p, 1)
                turn(b, 0)
                if not first:
                    values(b - 1, 1 - p, H - 1)
                scores(b, p, 2)
                turn(b, 1)
                values(b, p, 0)
                if not first:
                    turn_heads(b - 1)
                scores(b, p, 3)
                turn(b, 2)
                values(b, p, 1)
                if not first:
                    mix_heads(b - 1)
                scores(b, p, 4)
                turn(b, 3)
                if not first:
                    mix_out(b - 1, 1 - p)
                if not last:
                    turn_tokens(b + 1, 1 - p)
                values(b, p, 2)
                scores(b, p, 5)
                turn(b, 4)
                if not last:
                    queries(b + 1, 1 - p)
                    keys(b + 1, 1 - p)
                values(b, p, 3)
                if not last:
                    value_tokens(b + 1, 1 - p)
                    scores(b + 1, 1 - p, 0)
                turn(b, 5)
                values(b, p, 4)

            pe.wait_ge(w_in, 16 * len(loads))
            pe.wait_ge(w_ready, 1)
            turn_tokens(0, 0)
            queries(0, 0)
            keys(0, 0)
            value_tokens(0, 0)
            scores(0, 0, 0)
            images(pe, body)
            values(NB - 1, 1, H - 1)
            turn_heads(NB - 1)
            mix_heads(NB - 1)
            mix_out(NB - 1, 1)


NH2, HC2 = 12, 32
KSIDE = SIDE // 2
KPIX = KSIDE * KSIDE
QP = PIX // 4
KP = KPIX // 4
HG = P // HC2
N3 = NH2 // HG
PAD = SIDE + 2
L2_LN_EPS = 1e-5
L2_SCALE = HC2 ** -0.5


def l2_sample(nc, T, A, R):
    X, ident = T["X"], T["ident"]
    Q, K, V = R["Q"], R["K"], R["V"]
    TAPS = KS * KS
    with ExitStack() as ctx:
        s = Scope(nc, ctx, "l2s")
        taps = s.sb("taps", [C, 4, TAPS])
        bias = s.sb("bias", [C, 4])
        diag = s.sb("diag", [C, 3, TAPS, C])
        lnp = s.sb("lnp", [C, 2])
        woff = s.sb("woff", [C, 2, P])
        ref = s.sb("ref", [P, 2, KPIX])
        coord = s.sb("coord", [P, 3])
        xn = s.sb("xn", [P, 2, C])
        xp = s.sb("xp", [C, 2, PAD, PAD])
        val = s.sb("val", [C, PIX])
        off = s.sb("off", [C, P])
        on = s.sb("on", [P, C])
        og = s.sb("og", [C, KPIX])
        pos = s.sb("pos", [P, 2, KPIX])
        th = s.sb("th", [P, 2, KPIX])
        dist = s.sb("dist", [P, 3, KPIX])
        hat = s.sb("hat", [P, 3, KPIX])
        bil = s.sb("bil", [P, 2, KPIX])
        vt = s.sb("vt", [P, 2, C])
        stats = s.sb("stats", [P, 2, 6])
        mean = s.sb("mean", [P, 2])
        var = s.sb("var", [P, 2])
        rstd = s.sb("rstd", [P, 2])
        ostats = s.sb("ostats", [P, 1, 6])
        omean = s.sb("omean", [P, 1])
        ovar = s.sb("ovar", [P, 1])
        orstd = s.sb("orstd", [P, 1])
        mhalf = s.sb("mhalf", [P, 2])
        tp, qp, kp, op, fp, gp, vp, sp_ = (s.psum(n, [P, 512]) for n in
                                           ("tp", "qp", "kp", "op", "fp", "gp", "vp", "sp"))
        names = ("w_in", "consts", "diag_done", "var_done", "rstd_done", "ovar_done", "orstd_done", "dve_step",
                 "xn_done", "turned", "xp_done", "q_in", "q_out", "k_in", "k_out", "off_in", "off_out",
                 "on_in", "on_done", "og_in", "og_out", "pos_in", "pos_out", "th_done", "dist_done", "hat_done",
                 "bil_done", "val_done", "vt_in", "vt_out", "smp_in", "smp_out")
        S = {n: s.sem(n) for n in names}
        block = ctx.enter_context(nc.Block())
        loads = [(taps, "l2_taps"), (bias, "l2_bias"), (lnp, "l2_lnp"), (woff, "l2_woff"), (ref, "l2_ref"),
                 (coord, "l2_coord")]

        @block.sync
        def _(sp):
            for t, name in loads:
                sp.dma_start(t[tuple(slice(None) for _ in t.shape)], A[name]).then_inc(S["w_in"], 16)

        @block.gpsimd
        def _(pool):
            pool.memset(xp[:, :, :, :], 0.0)
            pool.memset(off[:, :], 0.0)
            pool.memset(on[:, :], 0.0)
            pool.memset(mhalf[:, :], -0.5).then_inc(S["consts"], 1)
            pool.wait_ge(S["consts"], 1)

            def tokens_rstd(b):
                wait(pool, S["var_done"], b + 1)
                pool.tensor_tensor(rstd[:, :], var[:, :], mhalf[:, :], ALU.pow).then_inc(S["rstd_done"], 1)

            def offsets_rstd(b):
                wait(pool, S["ovar_done"], b + 1)
                pool.tensor_tensor(orstd[0:KPIX, :], ovar[0:KPIX, :], mhalf[0:KPIX, 0:1], ALU.pow
                                   ).then_inc(S["orstd_done"], 1)

            tokens_rstd(0)
            with pool.Fori(0, NI - 1) as b:
                offsets_rstd(b)
                tokens_rstd(b + 1)
            offsets_rstd(NI - 1)

        STATS, APPLY, TAPS_A, TAPS_B = 4, 2, 5, 3
        EACH = TAPS_A + STATS + TAPS_B + APPLY

        def images(eng, body):
            body(0, 0, False)
            with eng.Fori(0, NI // 2 - 1) as i:
                body(2 * i + 1, 1, False)
                body(2 * i + 2, 0, False)
            body(NI - 1, 1, True)

        @block.vector
        def _(dve):
            def ln_stats(b, chain):
                layernorm_stats(dve, chain, [X[:, 2 * b + t, :] for t in range(2)], stats, mean, var, 1e-6)
                dve.sem_inc(S["var_done"], 1)

            def ln_apply(b, chain):
                wait(dve, S["rstd_done"], b + 1)
                wait(dve, S["turned"], b)
                layernorm_apply(dve, chain, [X[:, 2 * b + t, :] for t in range(2)], [xn[:, t, :] for t in range(2)],
                                stats, mean, rstd).then_inc(S["xn_done"], 1)

            def bilinear(b):
                wait(dve, S["hat_done"], b + 1)
                wait(dve, S["smp_in"], b)
                dve.tensor_tensor(bil[:, :, :], hat[:, 1:3, :],
                                  hat[:, 0, :].unsqueeze(1).broadcast_to([P, 2, KPIX]), ALU.mult
                                  ).then_inc(S["bil_done"], 1)

            def body(b, p, last):
                chain = Chain(dve, S["dve_step"], STATS + APPLY + b * (STATS + APPLY + EACH))
                if not (isinstance(b, int) and b == 0):
                    bilinear(b - 1)
                wait(dve, S["xp_done"], b + 1)
                wait(dve, S["vt_in"], b)
                v3 = val[:, :].rearrange("c (y x) -> c y x", x=SIDE)
                for t in range(TAPS):
                    image = xp[:, p, t // KS:t // KS + SIDE, t % KS:t % KS + SIDE]
                    if t == 0:
                        ins = dve.tensor_scalar(v3, image, taps[:, 3, 0:1], bias[:, 3:4], ALU.mult, ALU.add)
                    else:
                        ins = dve.scalar_tensor_tensor(out=v3, in0=image, scalar=taps[:, 3, t:t + 1], in1=v3,
                                                       op0=ALU.mult, op1=ALU.add)
                    if t < TAPS - 1:
                        chain.sync(ins)
                    if t == TAPS_A - 1:
                        wait(dve, S["on_in"], b + 1)
                        layernorm_stats(dve, chain, [fp[0:KPIX, 0:C]], ostats, omean, ovar, L2_LN_EPS, KPIX)
                        dve.sem_inc(S["ovar_done"], 1)
                        if not last:
                            ln_stats(b + 1, chain)
                ins.then_inc(S["val_done"], 1)
                wait(dve, S["orstd_done"], b + 1)
                layernorm_apply(dve, chain, [fp[0:KPIX, 0:C]], [on[0:KPIX, :]], ostats, omean, orstd, KPIX
                                ).then_inc(S["on_done"], 1)
                if not last:
                    ln_apply(b + 1, chain)
                wait(dve, S["vt_in"], b + 1)
                wait(dve, S["smp_in"], b)
                dve.tensor_copy(vt[:, :, :].rearrange("p t c -> p (t c)"), vp[:, 0:2 * C]).then_inc(S["vt_out"], 1)
                wait(dve, S["pos_in"], b + 1)
                dve.tensor_tensor(pos[:, :, :], gp[:, 0:2 * KPIX].rearrange("p (a n) -> p a n", a=2), ref[:, :, :],
                                  ALU.add).then_inc(S["pos_out"], 1)
                assert chain.n == EACH + (0 if last else STATS + APPLY) - 0, chain.n

            dve.wait_ge(S["w_in"], 16 * len(loads))
            dve.wait_ge(S["consts"], 1)
            chain = Chain(dve, S["dve_step"])
            ln_stats(0, chain)
            ln_apply(0, chain)
            for w in range(3):
                for t in range(TAPS):
                    ins = dve.tensor_scalar(diag[:, w, t, :], ident[0:C, 0:C], taps[:, w, t:t + 1], None, ALU.mult)
            ins.then_inc(S["diag_done"], 1)
            images(dve, body)
            bilinear(NI - 1)

        @block.scalar
        def _(act):
            def tokens_out(b, p):
                wait(act, S["turned"], b + 1)
                wait(act, S["k_in"], b - 1)
                wait(act, S["val_done"], b - 1)
                act.activation(xp[:, p, 1:SIDE + 1, 1:SIDE + 1],
                               tp[0:C, 0:PIX].rearrange("c (y x) -> c y x", x=SIDE), ACT.Copy
                               ).then_inc(S["xp_done"], 1)

            def sampled_out(b):
                wait(act, S["smp_in"], b + 1)
                act.activation(V[:, b, :], sp_[0:C, 0:KPIX], ACT.Copy).then_inc(S["smp_out"], 1)

            def body(b, p, last):
                wait(act, S["off_in"], b + 1)
                act.activation(off[:, 0:KPIX], op[0:C, 0:KPIX], ACT.Identity, bias=bias[:, 2:3]
                               ).then_inc(S["off_out"], 1)
                wait(act, S["k_in"], b + 1)
                act.activation(K[:, b, :], kp[0:C, 0:KPIX], ACT.Identity, bias=bias[:, 1:2]
                               ).then_inc(S["k_out"], 1)
                wait(act, S["q_in"], b + 1)
                act.activation(Q[:, b, :], qp[0:C, 0:PIX], ACT.Identity, bias=bias[:, 0:1]
                               ).then_inc(S["q_out"], 1)
                if not (isinstance(b, int) and b == 0):
                    sampled_out(b - 1)
                if not last:
                    tokens_out(b + 1, 1 - p)
                wait(act, S["og_in"], b + 1)
                act.activation(og[:, :], fp[0:C, 0:KPIX], ACT.Gelu, scale=lnp[:, 0:1], bias=lnp[:, 1:2]
                               ).then_inc(S["og_out"], 1)
                wait(act, S["pos_out"], b + 1)
                act.activation(th[:, :, :], pos[:, :, :], ACT.Tanh).then_inc(S["th_done"], 1)
                wait(act, S["th_done"], b + 1)
                for k, comp in enumerate((0, 1, 1)):
                    ins = act.activation(dist[:, k, :], th[:, comp, :], ACT.Abs, scale=(SIDE - 1) / 2,
                                         bias=coord[:, k:k + 1])
                ins.then_inc(S["dist_done"], 1)
                wait(act, S["dist_done"], b + 1)
                wait(act, S["bil_done"], b)
                act.activation(hat[:, :, :], dist[:, :, :], ACT.Relu, scale=-1.0, bias=1.0
                               ).then_inc(S["hat_done"], 1)

            act.wait_ge(S["w_in"], 16 * len(loads))
            act.wait_ge(S["consts"], 1)
            tokens_out(0, 0)
            images(act, body)
            sampled_out(NI - 1)

        @block.tensor
        def _(pe):
            def turn(b):
                wait(pe, S["xn_done"], b + 1)
                wait(pe, S["xp_done"], b)
                for t in range(2):
                    ins = pe.transpose(tp[0:C, t * P:(t + 1) * P], xn[:, t, :], ident[:, :])
                ins.then_inc(S["turned"], 1)

            def conv(out, w, p, stride, done):
                side = SIDE // stride
                o = out[0:C, 0:side * side].rearrange("c (y x) -> c y x", x=side)
                for t in range(TAPS):
                    dy, dx = t // KS, t % KS
                    ins = pe.matmul(o, diag[:, w, t, :], xp[:, p, dy:dy + SIDE:stride, dx:dx + SIDE:stride],
                                    start=(t == 0), stop=(t == TAPS - 1))
                ins.then_inc(done, 1)

            def sample(b):
                wait(pe, S["vt_out"], b + 1)
                wait(pe, S["bil_done"], b + 1)
                wait(pe, S["smp_out"], b)
                for t in range(2):
                    ins = pe.matmul(sp_[0:C, 0:KPIX], vt[:, t, :], bil[:, t, :], start=(t == 0), stop=(t == 1))
                ins.then_inc(S["smp_in"], 1)

            def body(b, p, last):
                wait(pe, S["xp_done"], b + 1)
                wait(pe, S["off_out"], b)
                conv(op, 2, p, 2, S["off_in"])
                wait(pe, S["k_out"], b)
                conv(kp, 1, p, 2, S["k_in"])
                wait(pe, S["off_out"], b + 1)
                pe.transpose(fp[:, 0:C], off[:, :], ident[0:C, 0:C]).then_inc(S["on_in"], 1)
                wait(pe, S["q_out"], b)
                conv(qp, 0, p, 1, S["q_in"])
                if not (isinstance(b, int) and b == 0):
                    sample(b - 1)
                if not last:
                    turn(b + 1)
                wait(pe, S["on_done"], b + 1)
                pe.transpose(fp[0:C, 0:P], on[:, :], ident[:, :]).then_inc(S["og_in"], 1)
                wait(pe, S["val_done"], b + 1)
                wait(pe, S["vt_out"], b)
                for t in range(2):
                    ins = pe.transpose(vp[:, t * C:(t + 1) * C], val[:, t * P:(t + 1) * P], ident[0:C, 0:C])
                ins.then_inc(S["vt_in"], 1)
                wait(pe, S["og_out"], b + 1)
                wait(pe, S["pos_out"], b)
                for k in range(2):
                    ins = pe.matmul(gp[:, k * KPIX:(k + 1) * KPIX], woff[:, k, :], og[:, :], start=True, stop=True)
                ins.then_inc(S["pos_in"], 1)

            pe.wait_ge(S["w_in"], 16 * len(loads))
            turn(0)
            pe.wait_ge(S["diag_done"], 1)
            images(pe, body)
            sample(NI - 1)


def l2_mix(nc, T, A, R):
    X, ident = T["X"], T["ident"]
    Q, K, V = R["Q"], R["K"], R["V"]
    with ExitStack() as ctx:
        s = Scope(nc, ctx, "l2m")
        qr = s.sb("qr", [P, NI, N3, QP])
        kr = s.sb("kr", [P, NI, N3, KP])
        vr = s.sb("vr", [P, NI, N3, KP])
        orow = s.sb("orow", [P, NI, N3, QP])
        oc = s.sb("oc", [C, NI, PIX])
        mask = s.sb("mask", [P, HG])
        wout = s.sb("wout", [C, C])
        kb = s.sb("kb", [P, 2, N3, HG, KP])
        vb = s.sb("vb", [P, 2, N3, HG, KP])
        vbt = s.sb("vbt", [HG * KP, 2, N3 * P])
        at = s.sb("at", [HG * KP, 2, N3 * QP])
        vp = [s.psum(f"vp{i}", [P, 512]) for i in range(2)]
        ap_ = [s.psum(f"ap{i}", [P, 512]) for i in range(2)]
        op = [s.psum(f"op{i}", [P, 512]) for i in range(2)]
        yp = [s.psum(f"yp{i}", [P, 512]) for i in range(2)]
        names = ("w_in", "moved_dve", "moved_act", "moved_pool", "kb_done", "vb_done", "vbt_in", "vbt_out",
                 "at_in", "at_out", "o_in", "o_out", "back_dve", "back_act", "y_in", "y_out")
        S = {n: s.sem(n) for n in names}
        block = ctx.enter_context(nc.Block())
        PARTS = [(g, j) for g in range(N3) for j in range(4)]

        @block.sync
        def _(sp):
            sp.dma_start(mask[:, :], A["l2_mask"]).then_inc(S["w_in"], 16)
            sp.dma_start(wout[:, :], A["l2_wout"]).then_inc(S["w_in"], 16)

        def rows(t, g, j, n):
            return t[HC2 * j:HC2 * (j + 1), :, g, 0:n]

        def chans(t, g, j, n):
            return t[HC2 * g:HC2 * (g + 1), :, n * j:n * (j + 1)]

        @block.gpsimd
        def _(pool):
            for g, j in PARTS:
                ins = pool.tensor_copy(rows(vr, g, j, KP), chans(V, g, j, KP))
            ins.then_inc(S["moved_pool"], 1)

        @block.vector
        def _(dve):
            for g, j in PARTS:
                dve.tensor_copy(rows(kr, g, j, KP), chans(K, g, j, KP))
            for g, j in PARTS[0:6]:
                ins = dve.tensor_copy(rows(qr, g, j, QP), chans(Q, g, j, QP))
            ins.then_inc(S["moved_dve"], 1)
            dve.wait_ge(S["w_in"], 32)
            dve.wait_ge(S["moved_dve"], 1)
            dve.wait_ge(S["moved_pool"], 1)

            def block_diagonal(out, rows_, b, done):
                dve.tensor_tensor(out, rows_[:, b, :, :].unsqueeze(2).broadcast_to([P, N3, HG, KP]),
                                  mask[:, :].unsqueeze(1).unsqueeze(3).broadcast_to([P, N3, HG, KP]), ALU.mult
                                  ).then_inc(done, 1)

            def body(b, p):
                wait(dve, S["vbt_in"], b - 1)
                block_diagonal(vb[:, p, :, :, :], vr, b, S["vb_done"])
                wait(dve, S["at_in"], b - 1)
                block_diagonal(kb[:, p, :, :, :], kr, b, S["kb_done"])
                wait(dve, S["vbt_in"], b + 1)
                wait(dve, S["o_in"], b - 1)
                dve.tensor_scalar(vbt[:, p, :], vp[p][0:HG * KP, 0:N3 * P], L2_SCALE, None, ALU.mult
                                  ).then_inc(S["vbt_out"], 1)

            body(0, 0)
            body(1, 1)
            with dve.Fori(1, NI // 2) as i:
                body(2 * i, 0)
                body(2 * i + 1, 1)
            dve.wait_ge(S["o_out"], NI)
            for g, j in PARTS[0:7]:
                ins = dve.tensor_copy(chans(oc, g, j, QP), rows(orow, g, j, QP))
            ins.then_inc(S["back_dve"], 1)
            for n in range(NT // GT):
                dve.wait_ge(S["y_in"], n + 1)
                x = X[:, GT * n:GT * (n + 1), :].rearrange("p t c -> p (t c)")
                dve.tensor_tensor(x, yp[n % 2][:, 0:GT * C], x, ALU.add).then_inc(S["y_out"], 1)

        @block.scalar
        def _(act):
            for g, j in PARTS[6:]:
                ins = act.activation(rows(qr, g, j, QP), chans(Q, g, j, QP), ACT.Copy)
            ins.then_inc(S["moved_act"], 1)

            def body(b, p):
                wait(act, S["at_in"], b + 1)
                wait(act, S["o_in"], b - 1)
                act.activation(at[:, p, :], ap_[p][0:HG * KP, 0:N3 * QP], ACT.Copy).then_inc(S["at_out"], 1)
                wait(act, S["o_in"], b + 1)
                act.activation(orow[:, b, :, :], op[p][:, 0:N3 * QP].rearrange("p (g m) -> p g m", g=N3), ACT.Copy
                               ).then_inc(S["o_out"], 1)

            body(0, 0)
            body(1, 1)
            with act.Fori(1, NI // 2) as i:
                body(2 * i, 0)
                body(2 * i + 1, 1)
            act.wait_ge(S["o_out"], NI)
            for g, j in PARTS[7:]:
                ins = act.activation(chans(oc, g, j, QP), rows(orow, g, j, QP), ACT.Copy)
            ins.then_inc(S["back_act"], 1)

        @block.tensor
        def _(pe):
            pe.wait_ge(S["moved_act"], 1)
            pe.wait_ge(S["moved_dve"], 1)
            pe.wait_ge(S["w_in"], 32)

            def body(b, p):
                wait(pe, S["vb_done"], b + 1)
                wait(pe, S["vbt_out"], b - 1)
                wait(pe, S["kb_done"], b + 1)
                wait(pe, S["at_out"], b - 1)
                for g in range(N3):
                    ins = pe.matmul(ap_[p][0:HG * KP, g * QP:(g + 1) * QP],
                                    kb[:, p, g, :, :].rearrange("p h n -> p (h n)"), qr[:, b, g, :],
                                    start=True, stop=True)
                ins.then_inc(S["at_in"], 1)
                for g in range(N3):
                    ins = pe.transpose(vp[p][0:HG * KP, g * P:(g + 1) * P],
                                       vb[:, p, g, :, :].rearrange("p h n -> p (h n)"), ident[:, :])
                ins.then_inc(S["vbt_in"], 1)
                wait(pe, S["at_out"], b + 1)
                wait(pe, S["vbt_out"], b + 1)
                wait(pe, S["o_out"], b - 1)
                for g in range(N3):
                    ins = pe.matmul(op[p][:, g * QP:(g + 1) * QP], vbt[:, p, g * P:(g + 1) * P],
                                    at[:, p, g * QP:(g + 1) * QP], start=True, stop=True)
                ins.then_inc(S["o_in"], 1)

            body(0, 0)
            body(1, 1)
            with pe.Fori(1, NI // 2) as i:
                body(2 * i, 0)
                body(2 * i + 1, 1)
            pe.wait_ge(S["back_dve"], 1)
            pe.wait_ge(S["back_act"], 1)
            flat = oc[:, :, :].rearrange("c b n -> c (b n)")
            for n in range(NT // GT):
                wait(pe, S["y_out"], n - 1)
                for j in range(GT):
                    t = GT * n + j
                    ins = pe.matmul(yp[n % 2][:, j * C:(j + 1) * C], flat[:, t * P:(t + 1) * P], wout[:, :],
                                    start=True, stop=True)
                ins.then_inc(S["y_in"], 1)


def l2_conv(nc, T, A):
    with ExitStack() as ctx:
        s = Scope(nc, ctx, "l2")
        R = {"Q": s.sb("Q", [C, NI, PIX]), "K": s.sb("K", [C, NI, KPIX]), "V": s.sb("V", [C, NI, KPIX])}
        l2_sample(nc, T, A, R)
        l2_mix(nc, T, A, R)


L3H, L3D = 8, 16
INNER = L3H * L3D
L3_SCALE = L3D ** -0.5
QG = 5
GI = NI // QG
TG = GI * PIX // P
QB, Q_EPS = 128.0, 1e-5


def l3_conv(nc, T, A):
    X, ident = T["X"], T["ident"]
    TAPS = KS * KS
    VW = INNER + INNER + C
    with ExitStack() as ctx:
        s = Scope(nc, ctx, "l3c")
        taps = s.sb("taps", [C, 2, TAPS])
        bn = s.sb("bn", [C, 4, 2])
        inv = s.sb("inv", [C, 2])
        shift = s.sb("shift", [C, 2])
        diag = s.sb("diag", [C, TAPS, C])
        wq = s.sb("wq", [C, INNER])
        wkv = s.sb("wkv", [C, VW])
        wvt = s.sb("wvt", [INNER, C])
        wo = s.sb("wo", [INNER, C])
        bo = s.sb("bo", [P, C])
        mask = s.sb("mask", [INNER, L3H])
        ones = s.sb("ones", [P, P])
        xn = s.sb("xn", [P, 2, C])
        xp = s.sb("xp", [C, 2, PAD, PAD])
        yq = s.sb("yq", [C, PIX])
        ykv = s.sb("ykv", [C, PIX])
        q = s.sb("q", [INNER, PIX])
        kv = s.sb("kv", [P, 2, 2 * INNER])
        prod = s.sb("prod", [P, 2, INNER])
        dsum = s.sb("dsum", [P, NI, 2, L3H])
        dtot = s.sb("dtot", [P, 1])
        m0 = s.sb("m0", [P, 1])
        ktv = s.sb("ktv", [INNER, INNER])
        z = s.sb("z", [P, 2, INNER])
        zt = s.sb("zt", [INNER, 2, P])
        vw = s.sb("vw", [P, NT, C])
        stats = s.sb("stats", [P, 2, 6])
        mean = s.sb("mean", [P, 2])
        var = s.sb("var", [P, 2])
        rstd = s.sb("rstd", [P, 2])
        mhalf = s.sb("mhalf", [P, 2])
        tp, qp, cp, kv0, kv1, pp, zp, yp = (s.psum(n, [P, 512]) for n in
                                            ("tp", "qp", "cp", "kv0", "kv1", "pp", "zp", "yp"))
        names = ("w_in", "consts", "v_eps", "bn_pow", "vw_in", "vw_out", "diag_done", "var_done", "rstd_done",
                 "dve_step", "xn_done", "turned", "xp_done", "yq_in", "yq_out", "ykv_done", "q_in", "q_out",
                 "qt_in", "qt_out", "kv_in", "kv_out", "ktv_in", "ktv_out", "qkv_in", "z_out", "zt_in", "zt_out",
                 "y_in", "y_out", "tot_done", "m0_in")
        S = {n: s.sem(n) for n in names}
        block = ctx.enter_context(nc.Block())
        loads = [(taps, "l3_taps"), (bn, "l3_bn"), (wq, "l3_wq"), (wkv[:, 0:2 * INNER], "l3_wkv"), (wvt, "l3_wvt"),
                 (wo, "l3_wo"), (bo, "l3_bo"), (mask, "l3_mask")]

        def images(eng, body):
            body(0, 0, False)
            with eng.Fori(0, NI // 2 - 1) as i:
                body(2 * i + 1, 1, False)
                body(2 * i + 2, 0, False)
            body(NI - 1, 1, True)

        @block.sync
        def _(sp):
            for t, name in loads:
                sp.dma_start(t[tuple(slice(None) for _ in t.shape)], A[name]).then_inc(S["w_in"], 16)

        @block.gpsimd
        def _(pool):
            pool.memset(xp[:, :, :, :], 0.0)
            pool.memset(ones[:, :], 1.0)
            pool.memset(mhalf[:, :], -0.5).then_inc(S["consts"], 1)
            pool.wait_ge(S["consts"], 1)
            pool.wait_ge(S["v_eps"], 1)
            pool.tensor_tensor(inv[:, :], shift[:, :], mhalf[0:C, :], ALU.pow).then_inc(S["bn_pow"], 1)
            with pool.Fori(0, NI) as b:
                pool.wait_ge(S["var_done"], b + 1)
                pool.tensor_tensor(rstd[:, :], var[:, :], mhalf[:, :], ALU.pow).then_inc(S["rstd_done"], 1)

        STATS, APPLY = 4, 2
        EACH = TAPS + 2

        @block.vector
        def _(dve):
            def ln_stats(b, chain):
                layernorm_stats(dve, chain, [X[:, 2 * b + t, :] for t in range(2)], stats, mean, var, 1e-6)
                dve.sem_inc(S["var_done"], 1)

            def ln_apply(b, chain):
                wait(dve, S["rstd_done"], b + 1)
                wait(dve, S["turned"], b)
                layernorm_apply(dve, chain, [X[:, 2 * b + t, :] for t in range(2)], [xn[:, t, :] for t in range(2)],
                                stats, mean, rstd).then_inc(S["xn_done"], 1)

            def output(b):
                wait(dve, S["y_in"], b + 1)
                x = X[:, bass.ds(2 * b, 2), :].rearrange("p t c -> p (t c)")
                dve.tensor_tensor(x, yp[:, 0:2 * C], x, ALU.add).then_inc(S["y_out"], 1)

            def body(b, p, last):
                chain = Chain(dve, S["dve_step"], base + b * (STATS + APPLY + EACH))
                wait(dve, S["xp_done"], b + 1)
                wait(dve, S["kv_in"], b)
                y3 = ykv[:, :].rearrange("c (y x) -> c y x", x=SIDE)
                for t in range(TAPS):
                    image = xp[:, p, t // KS:t // KS + SIDE, t % KS:t % KS + SIDE]
                    if t == 0:
                        ins = dve.tensor_scalar(y3, image, taps[:, 1, 0:1], shift[:, 1:2], ALU.mult, ALU.add)
                    else:
                        ins = dve.scalar_tensor_tensor(out=y3, in0=image, scalar=taps[:, 1, t:t + 1], in1=y3,
                                                       op0=ALU.mult, op1=ALU.add)
                    if t < TAPS - 1:
                        chain.sync(ins)
                ins.then_inc(S["ykv_done"], 1)
                if not last:
                    ln_stats(b + 1, chain)
                if not (isinstance(b, int) and b == 0):
                    output(b - 1)
                if not last:
                    ln_apply(b + 1, chain)
                wait(dve, S["qt_in"], b + 1)
                wait(dve, S["kv_out"], b + 1)
                chain.sync(dve.tensor_tensor(prod[:, :, :], qp[:, 0:2 * INNER].rearrange("p (t c) -> p t c", t=2),
                                             kv[:, :, 0:INNER], ALU.mult))
                dve.sem_inc(S["qt_out"], 1)
                d = dsum[:, b, :, :].rearrange("p t h -> p (t h)")
                chain.sync(dve.tensor_reduce(d, prod[:, :, :].rearrange("p t (h d) -> p (t h) d", d=L3D), AX.X,
                                             ALU.add))
                wait(dve, S["ktv_in"], b + 1)
                dve.tensor_tensor(ktv[:, :].rearrange("p (h d) -> p h d", d=L3D),
                                  pp[:, 0:INNER].rearrange("p (h d) -> p h d", d=L3D),
                                  mask[:, :].unsqueeze(2).broadcast_to([INNER, L3H, L3D]), ALU.mult
                                  ).then_inc(S["ktv_out"], 1)
                chain.sync(dve.tensor_tensor(prod[:, :, :].rearrange("p t (h d) -> p (t h) d", d=L3D),
                                             kv[:, :, INNER:2 * INNER].rearrange("p t (h d) -> p t h d", d=L3D),
                                             d.unsqueeze(2).broadcast_to([P, 2 * L3H, L3D]), ALU.mult))
                wait(dve, S["qkv_in"], b + 1)
                wait(dve, S["zt_in"], b)
                dve.tensor_tensor(z[:, :, :].rearrange("p t c -> p (t c)"), pp[:, INNER:3 * INNER],
                                  prod[:, :, :].rearrange("p t c -> p (t c)"), ALU.subtract).then_inc(S["z_out"], 1)
                assert chain.n == EACH + (0 if last else STATS + APPLY)

            dve.wait_ge(S["w_in"], 16 * len(loads))
            chain = Chain(dve, S["dve_step"])
            chain.sync(dve.tensor_scalar(shift[:, :], bn[:, 3, :], BN_EPS, None, ALU.add))
            dve.sem_inc(S["v_eps"], 1)
            ln_stats(0, chain)
            dve.wait_ge(S["bn_pow"], 1)
            chain.sync(dve.tensor_tensor(inv[:, :], inv[:, :], bn[:, 0, :], ALU.mult))
            chain.sync(dve.tensor_tensor(shift[:, :], bn[:, 2, :], inv[:, :], ALU.mult))
            dve.tensor_tensor(shift[:, :], bn[:, 1, :], shift[:, :], ALU.subtract)
            chain.sync(dve.tensor_tensor(taps[:, :, :], taps[:, :, :], inv[:, :].unsqueeze(2)
                                         .broadcast_to([C, 2, TAPS]), ALU.mult))
            ln_apply(0, chain)
            for t in range(TAPS):
                ins = dve.tensor_scalar(diag[:, t, :], ident[0:C, 0:C], taps[:, 0, t:t + 1], None, ALU.mult)
            ins.then_inc(S["diag_done"], 1)
            dve.wait_ge(S["vw_in"], 1)
            dve.tensor_copy(wkv[:, 2 * INNER:VW], pp[0:C, 0:C]).then_inc(S["vw_out"], 1)
            base = chain.n
            images(dve, body)
            output(NI - 1)
            dve.tensor_reduce(dtot[:, :], dsum[:, :, :, :].rearrange("p b t h -> p (b t h)"), AX.X, ALU.add
                              ).then_inc(S["tot_done"], 1)
            dve.wait_ge(S["y_out"], NI)
            last = Chain(dve, S["dve_step"], base + NI * (STATS + APPLY + EACH) - (STATS + APPLY))
            last.sync(dve.tensor_tensor(X[:, :, :], X[:, :, :], bo[:, :].unsqueeze(1).broadcast_to([P, NT, C]),
                                        ALU.add))
            dve.wait_ge(S["m0_in"], 1)
            last.sync(dve.tensor_scalar(m0[:, :], pp[:, 0:1], L3_SCALE, None, ALU.mult))
            dve.scalar_tensor_tensor(out=X[:, :, :].rearrange("p t c -> p (t c)"),
                                     in0=vw[:, :, :].rearrange("p t c -> p (t c)"), scalar=m0[:, 0:1],
                                     in1=X[:, :, :].rearrange("p t c -> p (t c)"), op0=ALU.mult, op1=ALU.add)

        @block.scalar
        def _(act):
            def tokens_out(b, p):
                wait(act, S["turned"], b + 1)
                wait(act, S["yq_in"], b - 1)
                wait(act, S["ykv_done"], b - 1)
                act.activation(xp[:, p, 1:SIDE + 1, 1:SIDE + 1],
                               tp[0:C, 0:PIX].rearrange("c (y x) -> c y x", x=SIDE), ACT.Copy
                               ).then_inc(S["xp_done"], 1)

            def body(b, p, last):
                wait(act, S["yq_in"], b + 1)
                act.activation(yq[:, :], cp[0:C, 0:PIX], ACT.Identity, bias=shift[:, 0:1]).then_inc(S["yq_out"], 1)
                wait(act, S["q_in"], b + 1)
                act.activation(q[:, :], tp[:, 0:PIX], ACT.Copy).then_inc(S["q_out"], 1)
                if not last:
                    tokens_out(b + 1, 1 - p)
                wait(act, S["kv_in"], b + 1)
                wait(act, S["z_out"], b)
                for t, bank in enumerate((kv0, kv1)):
                    act.activation(kv[:, t, :], bank[:, 0:2 * INNER], ACT.Copy)
                for t, bank in enumerate((kv0, kv1)):
                    ins = act.activation(vw[:, 2 * b + t, :], bank[:, 2 * INNER:VW], ACT.Copy)
                ins.then_inc(S["kv_out"], 1)
                wait(act, S["zt_in"], b + 1)
                act.activation(zt[:, :, :].rearrange("p t n -> p (t n)"), zp[:, 0:2 * P], ACT.Copy, scale=L3_SCALE
                               ).then_inc(S["zt_out"], 1)

            act.wait_ge(S["vw_out"], 1)
            tokens_out(0, 0)
            images(act, body)

        @block.tensor
        def _(pe):
            def turn(b):
                wait(pe, S["xn_done"], b + 1)
                wait(pe, S["q_out"], b)
                for t in range(2):
                    ins = pe.transpose(tp[0:C, t * P:(t + 1) * P], xn[:, t, :], ident[:, :])
                ins.then_inc(S["turned"], 1)

            def body(b, p, last):
                wait(pe, S["xp_done"], b + 1)
                wait(pe, S["yq_out"], b)
                o = cp[0:C, 0:PIX].rearrange("c (y x) -> c y x", x=SIDE)
                for t in range(TAPS):
                    dy, dx = t // KS, t % KS
                    ins = pe.matmul(o, diag[:, t, :], xp[:, p, dy:dy + SIDE, dx:dx + SIDE],
                                    start=(t == 0), stop=(t == TAPS - 1))
                ins.then_inc(S["yq_in"], 1)
                if not (isinstance(b, int) and b == 0):
                    finish(b - 1)
                wait(pe, S["yq_out"], b + 1)
                pe.matmul(tp[:, 0:PIX], wq[:, :], yq[:, :], start=True, stop=True).then_inc(S["q_in"], 1)
                wait(pe, S["qt_out"], b)
                for t in range(2):
                    ins = pe.matmul(qp[:, t * INNER:(t + 1) * INNER], yq[:, t * P:(t + 1) * P], wq[:, :],
                                    start=True, stop=True)
                ins.then_inc(S["qt_in"], 1)
                if not last:
                    turn(b + 1)
                wait(pe, S["ykv_done"], b + 1)
                wait(pe, S["kv_out"], b)
                for t, bank in enumerate((kv0, kv1)):
                    ins = pe.matmul(bank[:, 0:VW], ykv[:, t * P:(t + 1) * P], wkv[:, :], start=True, stop=True)
                ins.then_inc(S["kv_in"], 1)
                wait(pe, S["kv_out"], b + 1)
                wait(pe, S["z_out"], b)
                for t in range(2):
                    ins = pe.matmul(pp[:, 0:INNER], kv[:, t, 0:INNER], kv[:, t, INNER:2 * INNER],
                                    start=(t == 0), stop=(t == 1))
                ins.then_inc(S["ktv_in"], 1)
                wait(pe, S["ktv_out"], b + 1)
                for t in range(2):
                    ins = pe.matmul(pp[:, (t + 1) * INNER:(t + 2) * INNER], q[:, t * P:(t + 1) * P], ktv[:, :],
                                    start=True, stop=True)
                ins.then_inc(S["qkv_in"], 1)

            def finish(b):
                wait(pe, S["z_out"], b + 1)
                wait(pe, S["zt_out"], b)
                for t in range(2):
                    ins = pe.transpose(zp[:, t * P:(t + 1) * P], z[:, t, :], ident[:, :])
                ins.then_inc(S["zt_in"], 1)
                wait(pe, S["zt_out"], b + 1)
                wait(pe, S["y_out"], b)
                for t in range(2):
                    ins = pe.matmul(yp[:, t * C:(t + 1) * C], zt[:, t, :], wo[:, :], start=True, stop=True)
                ins.then_inc(S["y_in"], 1)

            pe.wait_ge(S["w_in"], 16 * len(loads))
            pe.matmul(pp[0:C, 0:C], wvt[:, :], wo[:, :], start=True, stop=True).then_inc(S["vw_in"], 1)
            turn(0)
            pe.wait_ge(S["diag_done"], 1)
            pe.wait_ge(S["vw_out"], 1)
            images(pe, body)
            finish(NI - 1)
            pe.wait_ge(S["tot_done"], 1)
            pe.wait_ge(S["consts"], 1)
            pe.matmul(pp[:, 0:1], ones[:, :], dtot[:, :], start=True, stop=True).then_inc(S["m0_in"], 1)


def l3_ffn(nc, T, A, out):
    X, ident = T["X"], T["ident"]
    R1, R2 = HID // QG, C // QG
    TOKS = TG * P
    with ExitStack() as ctx:
        s = Scope(nc, ctx, "l3f")
        w1 = s.sb("w1", [CB, HID])
        w2 = s.sb("w2", [P, KC, C])
        b2 = s.sb("b2", [P, C])
        ones = s.sb("ones", [P, P])
        rs = s.sb("rs", [P, 2, QG])
        mu = s.sb("mu", [P, 2, QG])
        sg = s.sb("sg", [P, 2, HID])
        xn = s.sb("xn", [P, TG, C])
        xt = s.sb("xt", [CB, TOKS])
        hid = s.sb("hid", [P, KC, TOKS])
        y = s.sb("y", [P, TG, C])
        amax = s.sb("amax", [P, 2 * KC])
        bmax = s.sb("bmax", [P, 2])
        top = s.sb("top", [1, 2])
        gam = s.sb("gam", [P, 2])
        stats = s.sb("stats", [P, TG, 6])
        mean = s.sb("mean", [P, TG])
        var = s.sb("var", [P, TG])
        rstd = s.sb("rstd", [P, TG])
        mhalf = s.sb("mhalf", [P, TG])
        tp = [s.psum(f"tp{i}", [P, 512]) for i in range(2)]
        up = [s.psum(f"up{i}", [P, 512]) for i in range(4)]
        mp = s.psum("mp", [P, 512])
        gp = s.psum("gp", [P, 512])
        names = ("w_in", "consts", "rs_done", "mu_in", "centred", "signs", "w_done", "var_done", "rstd_done", "dve_step",
                 "xn_done", "turned", "xt_done", "up_in", "up_max", "up_out", "max_done", "max_in", "top_done",
                 "top_in", "clipped", "hid_done", "down_in", "y_done", "stored")
        S = {n: s.sem(n) for n in names}
        block = ctx.enter_context(nc.Block())
        loads = [(w1, "l3_w1"), (w2, "l3_w2"), (b2, "l3_b2")]
        LIM = float(np.float32(QB - Q_EPS))
        TB = TOKS - 512

        @block.sync
        def _(sp):
            for t, name in loads:
                sp.dma_start(t[tuple(slice(None) for _ in t.shape)], A[name]).then_inc(S["w_in"], 16)
            with sp.Fori(0, QG) as g:
                sp.wait_ge(S["y_done"], g + 1)
                sp.dma_start(out[:, bass.ds(TG * g, TG), :], y[:, :, :]).then_inc(S["stored"], 16)
            sp.dma_start(out[:, TG * QG:NT, :], X[:, TG * QG:NT, :]).then_inc(S["stored"], 16)
            sp.wait_ge(S["stored"], 16 * (QG + 1))

        @block.gpsimd
        def _(pool):
            pool.memset(ones[:, :], 1.0)
            pool.memset(mhalf[:, :], -0.5).then_inc(S["consts"], 1)
            pool.wait_ge(S["consts"], 1)
            with pool.Fori(0, QG) as g:
                pool.wait_ge(S["var_done"], g + 1)
                pool.tensor_tensor(rstd[:, :], var[:, :], mhalf[:, :], ALU.pow).then_inc(S["rstd_done"], 1)

        @block.vector
        def _(dve):
            LN, QUANT = 6, 14

            def ln(g, chain):
                tiles = [X[:, TG * g + j, :] for j in range(TG)]
                layernorm_stats(dve, chain, tiles, stats, mean, var, 1e-5)
                dve.sem_inc(S["var_done"], 1)
                wait(dve, S["rstd_done"], g + 1)
                wait(dve, S["turned"], g)
                layernorm_apply(dve, chain, tiles, [xn[:, j, :] for j in range(TG)], stats, mean, rstd
                                ).then_inc(S["xn_done"], 1)

            def factor(g, chain, k):
                dve.sem_inc(S["max_done"], 1)
                wait(dve, S["max_in"], 2 * g + k + 1)
                chain.sync(dve.tensor_reduce(top[:, k:k + 1], mp[0:1, 0:P], AX.X, ALU.max))
                dve.sem_inc(S["top_done"], 1)
                wait(dve, S["top_in"], 2 * g + k + 1)
                chain.sync(dve.tensor_scalar(gam[:, k:k + 1], gp[:, 0:1], Q_EPS, None, ALU.add))
                chain.sync(dve.reciprocal(gam[:, k:k + 1], gam[:, k:k + 1]))
                chain.sync(dve.tensor_scalar(gam[:, k:k + 1], gam[:, k:k + 1], QB, None, ALU.mult))

            def body(g, last):
                chain = Chain(dve, S["dve_step"], base + g * (LN + QUANT))
                for k in range(KC):
                    for h, n in ((0, 512), (1, TB)):
                        m = 2 * k + h
                        wait(dve, S["up_in"], 2 * KC * g + m + 1)
                        ins = dve.tensor_reduce(amax[:, m:m + 1], up[m % 4][:, 0:n], AX.X, ALU.max,
                                                apply_absolute_value=True)
                        if m < 2 * KC - 1:
                            ins.then_inc(S["up_max"], 1)
                chain.sync(ins)
                dve.sem_inc(S["up_max"], 1)
                chain.sync(dve.tensor_reduce(bmax[:, 0:1], amax[:, :], AX.X, ALU.max))
                factor(g, chain, 0)
                wait(dve, S["up_out"], 2 * KC * (g + 1))
                for k in range(KC):
                    ins = dve.tensor_scalar(hid[:, k, :], hid[:, k, :], gam[:, 0:1], LIM, ALU.mult, ALU.min)
                chain.sync(ins)
                if not last:
                    ln(g + 1, chain)
                for k in range(KC):
                    dve.tensor_scalar(hid[:, k, :], hid[:, k, :], -LIM, None, ALU.max).then_inc(S["clipped"], 1)
                wait(dve, S["down_in"], g + 1)
                if not (isinstance(g, int) and g == 0):
                    wait(dve, S["stored"], 16 * g)
                for h, (lo, n) in enumerate(((0, 4), (4, 2))):
                    ins = dve.tensor_tensor(y[:, lo:lo + n, :], tp[h][:, 0:n * C].rearrange("p (t c) -> p t c", c=C),
                                            b2[:, :].unsqueeze(1).broadcast_to([P, n, C]), ALU.add)
                chain.sync(ins)
                yf = y[:, :, :].rearrange("p t c -> p (t c)")
                chain.sync(dve.tensor_reduce(bmax[:, 1:2], yf, AX.X, ALU.max, apply_absolute_value=True))
                factor(g, chain, 1)
                chain.sync(dve.tensor_scalar(yf, yf, gam[:, 1:2], LIM, ALU.mult, ALU.min))
                x = X[:, bass.ds(TG * g, TG), :].rearrange("p t c -> p (t c)")
                dve.scalar_tensor_tensor(out=yf, in0=yf, scalar=-LIM, in1=x, op0=ALU.max, op1=ALU.add
                                         ).then_inc(S["y_done"], 1)
                assert chain.n == QUANT + (0 if last else LN)

            dve.wait_ge(S["w_in"], 16 * len(loads))
            dve.memset(xt[C:CB, :], 1.0)
            chain = Chain(dve, S["dve_step"])
            g1 = w1[0:C, 0:QG * R1].rearrange("c (g r) -> c g r", g=QG)
            dve.memset(rs[:, :, :], 0.0)
            chain.sync(dve.memset(sg[:, :, :], 0.0))
            dve.tensor_reduce(rs[0:C, 0, :], g1, AX.X, ALU.add)
            for k in range(KC):
                part = w2[:, k, 0:QG * R2].rearrange("p (g r) -> p g r", g=QG)
                chain.sync(dve.tensor_reduce(mu[:, 0, :], part, AX.X, ALU.add))
                chain.sync(dve.tensor_tensor(rs[:, 1, :], rs[:, 1, :], mu[:, 0, :], ALU.add))
            dve.sem_inc(S["rs_done"], 1)
            dve.wait_ge(S["mu_in"], 1)
            dve.tensor_scalar(mu[:, 0, :], gp[:, 0:QG], 1.0 / (R1 * C), None, ALU.mult)
            chain.sync(dve.tensor_scalar(mu[:, 1, :], gp[:, QG:2 * QG], 1.0 / (R2 * HID), None, ALU.mult))
            dve.tensor_tensor(g1, g1, mu[0:C, 0, :].unsqueeze(2).broadcast_to([C, QG, R1]), ALU.subtract)
            for k in range(KC):
                part = w2[:, k, 0:QG * R2].rearrange("p (g r) -> p g r", g=QG)
                ins = dve.tensor_tensor(part, part, mu[:, 1, :].unsqueeze(2).broadcast_to([P, QG, R2]), ALU.subtract)
            chain.sync(ins)
            dve.memset(w1[0:C, QG * R1:HID], 0.0)
            chain.sync(dve.memset(w2[:, :, QG * R2:C], 0.0))
            dve.sem_inc(S["centred"], 1)
            dve.wait_ge(S["signs"], 2)
            w2f = w2[:, :, :].rearrange("p k c -> p (k c)")
            dve.tensor_tensor(sg[0:C, 0, :], sg[0:C, 0, :], w1[0:C, :], ALU.subtract)
            chain.sync(dve.tensor_tensor(sg[:, 1, 0:KC * C], sg[:, 1, 0:KC * C], w2f, ALU.subtract))
            dve.tensor_tensor(w1[0:C, :], w1[0:C, :], sg[0:C, 0, :], ALU.add)
            chain.sync(dve.tensor_tensor(w2f, w2f, sg[:, 1, 0:KC * C], ALU.add))
            dve.sem_inc(S["w_done"], 1)
            ln(0, chain)
            base = chain.n
            body(0, False)
            with dve.Fori(1, QG - 1) as g:
                body(g, False)
            body(QG - 1, True)

        @block.scalar
        def _(act):
            act.wait_ge(S["centred"], 1)
            act.activation(sg[0:C, 0, :], w1[0:C, :], ACT.Sign).then_inc(S["signs"], 1)
            act.activation(sg[:, 1, 0:KC * C], w2[:, :, :].rearrange("p k c -> p (k c)"), ACT.Sign
                           ).then_inc(S["signs"], 1)

            def body(g, last):
                wait(act, S["turned"], g + 1)
                wait(act, S["up_in"], 2 * KC * g)
                act.activation(xt[0:C, 0:512], tp[0][0:C, :], ACT.Copy)
                act.activation(xt[0:C, 512:TOKS], tp[1][0:C, 0:TB], ACT.Copy).then_inc(S["xt_done"], 1)
                wait(act, S["down_in"], g)
                for m in range(2 * KC):
                    wait(act, S["up_max"], 2 * KC * g + m + 1)
                    k, lo, n = m // 2, 512 * (m % 2), (512, TB)[m % 2]
                    act.activation(hid[:, k, lo:lo + n], up[m % 4][:, 0:n], ACT.Copy).then_inc(S["up_out"], 1)
                for k in range(KC):
                    wait(act, S["clipped"], KC * g + k + 1)
                    act.activation(hid[:, k, :], hid[:, k, :], ACT.Gelu).then_inc(S["hid_done"], 1)

            body(0, False)
            with act.Fori(1, QG - 1) as g:
                body(g, False)
            body(QG - 1, True)

        @block.tensor
        def _(pe):
            def top_of(g, k):
                wait(pe, S["max_done"], 2 * g + k + 1)
                pe.matmul(mp[0:1, 0:P], bmax[:, k:k + 1], ident[:, :], start=True, stop=True).then_inc(S["max_in"], 1)
                wait(pe, S["top_done"], 2 * g + k + 1)
                pe.matmul(gp[:, 0:1], ones[0:1, :], top[:, k:k + 1], start=True, stop=True).then_inc(S["top_in"], 1)

            def body(g, last):
                wait(pe, S["xn_done"], g + 1)
                wait(pe, S["y_done"], g)
                for j in range(TG):
                    ins = pe.transpose(tp[j // 4][0:C, (j % 4) * P:(j % 4 + 1) * P], xn[:, j, :], ident[:, :])
                ins.then_inc(S["turned"], 1)
                wait(pe, S["xt_done"], g + 1)
                for m in range(2 * KC):
                    wait(pe, S["up_out"], 2 * KC * g + m - 3)
                    k, lo, n = m // 2, 512 * (m % 2), (512, TB)[m % 2]
                    pe.matmul(up[m % 4][:, 0:n], w1[:, k * P:(k + 1) * P], xt[:, lo:lo + n], start=True, stop=True
                              ).then_inc(S["up_in"], 1)
                top_of(g, 0)
                wait(pe, S["hid_done"], KC * (g + 1))
                for j in range(TG):
                    for k in range(KC):
                        ins = pe.matmul(tp[j // 4][:, (j % 4) * C:(j % 4 + 1) * C], hid[:, k, j * P:(j + 1) * P],
                                        w2[:, k, :], start=(k == 0), stop=(k == KC - 1))
                ins.then_inc(S["down_in"], 1)
                top_of(g, 1)

            pe.wait_ge(S["rs_done"], 1)
            pe.wait_ge(S["consts"], 1)
            pe.matmul(gp[:, 0:2 * QG], ones[:, :], rs[:, :, :].rearrange("p a g -> p (a g)"), start=True, stop=True
                      ).then_inc(S["mu_in"], 1)
            pe.wait_ge(S["w_done"], 1)
            body(0, False)
            with pe.Fori(1, QG - 1) as g:
                body(g, False)
            body(QG - 1, True)


PHASES = ("l0c", "m0", "l1c", "m1", "l2c", "m2", "l3c", "l3f")


def build(nc, A, out, phases=PHASES, load_x=False):
    with ExitStack() as ctx:
        s = Scope(nc, ctx, "all")
        T = {"X": s.sb("X", [P, NT, C]), "ident": s.sb("ident", [P, P])}
        T["scratch"] = nc.dram_tensor("conv_scratch", [NT * P, C], F32).ap()
        T["moe"] = [(s.sb(f"w1_{n}", [CB, NE * KC, P]), s.sb(f"w2_{n}", [P, NE * KC, C]),
                     s.sb(f"gw_{n}", [CB, NE]), s.sb(f"b2_{n}", [P, NE, C])) for n in range(3)]
        T["moe_in"] = [s.sem(f"moe_in{n}") for n in range(3)]
        if load_x:
            ld = s.sem("ld")
            with nc.Block() as block:
                @block.sync
                def _(sp):
                    sp.dma_start(T["ident"][:, :], A["ident"]).then_inc(ld, 16)
                    sp.dma_start(T["X"][:, :, :], A["x_tokens"]).then_inc(ld, 16)
                    for n, (w1, w2, gw, b2) in enumerate(T["moe"]):
                        sp.dma_start(w1[:, :, :], A[f"w1_{n}"]).then_inc(T["moe_in"][n], 16)
                        sp.dma_start(w2[:, :, :], A[f"w2_{n}"]).then_inc(T["moe_in"][n], 16)
                        sp.dma_start(gw[:, :], A[f"gw_{n}"]).then_inc(T["moe_in"][n], 16)
                        sp.dma_start(b2[:, :, :], A[f"b2_{n}"]).then_inc(T["moe_in"][n], 16)
                    sp.wait_ge(ld, 32)
                    for m in T["moe_in"]:
                        sp.wait_ge(m, 64)
        for ph in phases:
            before = nc.snapshot_sems()
            if ph == "l0c":
                l0_conv(nc, T, A)
            elif ph in ("m0", "m1", "m2"):
                moe(nc, T, A, int(ph[1]))
            elif ph == "l1c":
                l1_attention(nc, T, A)
            elif ph == "l2c":
                l2_conv(nc, T, A)
            elif ph == "l3c":
                l3_conv(nc, T, A)
            elif ph == "l3f":
                l3_ffn(nc, T, A, out)
            nc.clear_and_free_semaphores(nc.allocated_since(before))
            nc.all_engine_barrier()
        if "l3f" not in phases:
            st = s.sem("st")
            with nc.Block() as block:
                @block.sync
                def _(sp):
                    for m in T["moe_in"]:
                        sp.wait_ge(m, 64)
                    sp.dma_start(out, T["X"][:, :, :]).then_inc(st, 16)
                    sp.wait_ge(st, 16)


def tokens(x):
    return np.ascontiguousarray(np.transpose(x.reshape(NI, C, 2, P), (3, 0, 2, 1)).reshape(P, NT, C))


def layouts(v):
    f = np.float32
    v = {k: np.asarray(a) for k, a in v.items()}
    x = v["x"]
    A = {"x_tokens": tokens(x), "ident": np.eye(P, dtype=f)}
    A["x_rows"] = np.ascontiguousarray(
        np.transpose(x.reshape(2, 8, C, SIDE, SIDE), (1, 3, 0, 4, 2)).reshape(P, NT, C))

    def band(w):
        k = w.shape[-1]
        out = np.zeros((GC, SIDE, NG, k, SIDE), f)
        wg = w.reshape(NG, GC, k, k)
        for xi in range(SIDE):
            for xo in range(SIDE):
                d = xi - xo + k // 2
                if 0 <= d < k:
                    out[:, xi, :, :, xo] = np.transpose(wg[:, :, :, d], (1, 0, 2))
        return out.reshape(P, NG, k, SIDE)

    A["band"] = band(v["L0_conv_w_large"])
    A["band_s"] = band(v["L0_conv_w_small"])
    bn = np.stack([np.stack([v[f"L0_conv_{a}_{b}"] for b in "lsi"]) for a in "gbmv"])
    bn = np.transpose(bn.reshape(4, 3, NG, GC), (3, 0, 1, 2))
    A["bn"] = np.ascontiguousarray(np.repeat(bn, SIDE, axis=0))
    A["eye"] = np.tile(np.eye(SIDE, dtype=f), (GC, 1))
    A["own"] = np.repeat(np.eye(GC, dtype=f), SIDE, axis=0)
    for n in range(3):
        g = lambda name: v[f"L{n}_ffn_{name}"]
        w1 = np.concatenate([np.transpose(g("w1"), (1, 0, 2)).reshape(C, NE * HID), g("b1").reshape(1, -1)])
        A[f"w1_{n}"] = w1.reshape(CB, NE * KC, P)
        A[f"w2_{n}"] = np.ascontiguousarray(
            np.transpose(g("w2").reshape(NE * KC, P, C), (1, 0, 2)))
        A[f"gw_{n}"] = np.concatenate([g("gate_w"), g("gate_b").reshape(1, -1)])
        A[f"b2_{n}"] = np.ascontiguousarray(np.broadcast_to(g("b2")[None], (P, NE, C)))
    def spread(w):
        out = np.zeros(w.shape[:-1] + (2, 4, DH), f)
        w = w.reshape(w.shape[:-1] + (HEADS, KD))
        out[..., 0, :, 0:KD] = w[..., 0:4, :]
        out[..., 1, 0:2, 0:KD] = w[..., 4:6, :]
        return out.reshape(w.shape[:-2] + (2, P))

    c = {k[8:]: a for k, a in v.items() if k.startswith("L1_conv_")}
    wq = np.zeros((CB, HEADS * KD), f)
    wq[C - DS:C] = c["Wq"].T
    wk = np.zeros((CB, HEADS * KD), f)
    wk[0:C] = c["Wk"].T
    A["l1_wq"], A["l1_wk"] = spread(wq), spread(wk)
    qk = np.stack([np.stack([c["q_scale"], c["k_scale"]]), np.stack([c["q_bias"], c["k_bias"]])])
    A["l1_qk"] = np.transpose(spread(qk), (3, 0, 1, 2))
    A["l1_wv"] = np.concatenate([c["Wv"].T, c["v_bias"][None]])
    A["l1_sv"] = np.broadcast_to(c["v_scale"][None], (C, HEADS * DH))
    A["l1_wp"] = np.transpose(c["Wp"].T.reshape(2, C, DS), (1, 0, 2))
    A["l1_sp"] = np.stack([c["p_scale"], c["p_bias"]], axis=1)
    A["l1_wo"] = c["Wo"].T
    wx = np.zeros((CB, C), f)
    wx[C - DS:C] = c["Wo"].T
    wx[C] = c["o_bias"]
    A["l1_wx"] = wx
    A["l1_so"] = np.broadcast_to(c["o_scale"][None], (C, C))
    c = {k[8:]: a for k, a in v.items() if k.startswith("L2_conv_")}
    kinds = ("q", "k", "off1", "v")
    A["l2_taps"] = np.stack([c[f"w_{k}"].reshape(C, KS * KS) for k in kinds], axis=1)
    A["l2_bias"] = np.stack([c[f"b_{k}"] for k in kinds], axis=1)
    A["l2_lnp"] = np.stack([c["ln_g"], c["ln_b"]], axis=1)
    A["l2_woff"] = np.repeat(c["w_off2"][::-1].T[:, :, None], P, axis=2)
    line = (np.linspace(0.5, KSIDE - 0.5, KSIDE) / KSIDE * 2 - 1).astype(f)
    ref = np.stack([np.tile(line, KSIDE), np.repeat(line, KSIDE)])
    A["l2_ref"] = np.broadcast_to(ref[None], (P, 2, KPIX))
    px, py = np.arange(P) % SIDE, np.arange(P) // SIDE
    A["l2_coord"] = ((SIDE - 1) / 2 - np.stack([px, py, py + SIDE // 2], axis=1)).astype(f)
    A["l2_mask"] = (np.arange(P)[:, None] % HC2 // (HC2 // 4) == np.arange(HG)[None]).astype(f)
    A["l2_wout"] = c["w_out"].T
    c = {k[8:]: a for k, a in v.items() if k.startswith("L3_conv_")}
    A["l3_taps"] = np.stack([c["wq_dw"].reshape(C, KS * KS), c["wkv_dw"].reshape(C, KS * KS)], axis=1)
    A["l3_bn"] = np.transpose(np.stack([np.stack([c[f"{w}_bn_{a}"] for w in ("wq", "wkv")]) for a in "gbmv"]),
                              (2, 0, 1))
    A["l3_wq"], A["l3_wkv"], A["l3_wo"] = c["wq_pw"].T, c["wkv_pw"].T, c["wo"].T
    A["l3_wvt"] = c["wkv_pw"][INNER:]
    A["l3_bo"] = np.broadcast_to(c["bo"][None], (P, C))
    A["l3_mask"] = np.repeat(np.eye(L3H, dtype=f), L3D, axis=0)
    A["l3_w1"] = np.concatenate([v["L3_ffn_W1"].T, v["L3_ffn_b1"][None]])
    A["l3_w2"] = np.transpose(v["L3_ffn_W2"].T.reshape(KC, P, C), (1, 0, 2))
    A["l3_b2"] = np.broadcast_to(v["L3_ffn_b2"][None], (P, C))
    return {k: np.ascontiguousarray(a) for k, a in A.items()}


def kernel(**inputs):
    import concourse.bacc as bacc
    from concourse.bass_utils import run_bass_kernel_spmd

    arrays = layouts(inputs)
    nc = bacc.Bacc("TRN2", target_bir_lowering=False, num_devices=1)
    A = {name: nc.dram_tensor(name, a.shape, F32, kind="ExternalInput").ap() for name, a in arrays.items()}
    out = nc.dram_tensor("out_tokens", (P, NT, C), F32, kind="ExternalOutput").ap()
    build(nc, A, out, PHASES)
    y = run_bass_kernel_spmd(nc, [arrays], core_ids=[0]).results[0]["out_tokens"]
    return np.ascontiguousarray(y.reshape(P, NI, 2, C).transpose(1, 3, 2, 0).reshape(NI, C, SIDE, SIDE))
```

```python
from contextlib import ExitStack

import numpy as np

import concourse.bass as bass
from concourse import mybir

F32 = mybir.dt.float32
F32R = mybir.dt.float32r
ALU = mybir.AluOpType
ACT = mybir.ActivationFunctionType
AX = mybir.AxisListType

P = 128
C = 96
CB = C + 1
NI = 16
SIDE = 16
PIX = SIDE * SIDE
NT = NI * PIX // P
HALF = C // 2
KL, KS = 13, 3
GC = P // SIDE
NG = C // GC
NE, HID = 4, 4 * C
KC = HID // P
GT = 4
GW = GT * P
HEADS, KD, DH = 6, 16, 32
DS = C // 4
SG = HEADS // 2
KS3 = 4 * KD
BN_EPS = 1e-5


def wait(eng, sem, count):
    if isinstance(count, int) and count <= 0:
        return
    eng.wait_ge(sem, count)


class Chain:

    def __init__(self, eng, sem, start=0):
        self.eng, self.sem, self.start, self.n = eng, sem, start, 0

    def sync(self, ins):
        ins.then_inc(self.sem, 1)
        self.n += 1
        self.eng.wait_ge(self.sem, self.start + self.n)


def layernorm_stats(dve, chain, tiles, stats, mean, var, eps, rows=P):
    n = len(tiles)
    for j, tile in enumerate(tiles):
        last = dve.bn_stats(stats[0:rows, j, :], tile)
    chain.sync(last)
    s = stats[0:rows, 0:n, :]
    dve.tensor_tensor(mean[0:rows, 0:n], s[:, :, 1], s[:, :, 4], ALU.subtract)
    chain.sync(dve.tensor_tensor(var[0:rows, 0:n], s[:, :, 2], s[:, :, 5], ALU.add))
    dve.scalar_tensor_tensor(out=mean[0:rows, 0:n], in0=mean[0:rows, 0:n], scalar=0.25,
                             in1=mean[0:rows, 0:n], op0=ALU.mult, op1=ALU.mult)
    chain.sync(dve.tensor_scalar(var[0:rows, 0:n], var[0:rows, 0:n], 1.0 / C, eps, ALU.mult, ALU.add))
    chain.sync(dve.tensor_tensor(var[0:rows, 0:n], var[0:rows, 0:n], mean[0:rows, 0:n], ALU.add))


def layernorm_apply(dve, chain, tiles, outs, stats, mean, rstd, rows=P):
    n = len(tiles)
    s = stats[0:rows, 0:n, :]
    chain.sync(dve.tensor_tensor(mean[0:rows, 0:n], s[:, :, 1], s[:, :, 4], ALU.add))
    chain.sync(dve.tensor_scalar(mean[0:rows, 0:n], mean[0:rows, 0:n], 0.5, None, ALU.mult))
    for j, (tile, out) in enumerate(zip(tiles, outs)):
        last = dve.tensor_scalar(out, tile, mean[0:rows, j:j + 1], rstd[0:rows, j:j + 1],
                                 ALU.subtract, ALU.mult)
    return last


class Scope:

    def __init__(self, nc, ctx, tag):
        self.nc, self.ctx, self.tag = nc, ctx, tag

    def sb(self, name, shape, dtype=F32):
        return self.ctx.enter_context(self.nc.sbuf_tensor(f"{self.tag}_{name}", shape, dtype))

    def psum(self, name, shape):
        return self.ctx.enter_context(self.nc.psum_tensor(f"{self.tag}_{name}", shape, F32))

    def sem(self, name):
        return self.nc.alloc_semaphore(name=f"{self.tag}_{name}")


LATE = ("l3_w1", "l3_w2", "l3_b2", "l1_wqk", "l1_sqk", "l1_wv", "l1_sv", "l1_wp", "l1_sp", "l1_wo", "l1_wx", "l1_so",
        "l1_low", "l1_sel", "l2_taps", "l2_bias", "l2_lnp", "l2_woff", "l2_ref", "l2_coord", "l2_mask", "l2_wout",
        "l3_taps", "l3_bn", "l3_wq", "l3_wkv", "l3_wvt", "l3_wo", "l3_bo", "l3_mask")


def load_weights(sp, T, A):
    def moe_weights(n):
        for t, name in zip(T["moe"][n], ("w1", "w2", "gw", "b2")):
            sp.dma_start(t[tuple(slice(None) for _ in t.shape)], A[f"{name}_{n}"]).then_inc(T["moe_in"][n], 16)

    moe_weights(0)
    for name in LATE:
        t = T[name]
        if name == "l3_wkv":
            sp.dma_start(t[:, 0:2 * INNER], A[name]).then_inc(T["late_in"], 16)
        else:
            sp.dma_start(t[tuple(slice(None) for _ in t.shape)], A[name]).then_inc(T["late_in"], 16)
    moe_weights(1)
    moe_weights(2)


class WeightWork:

    def __init__(self, s, T, bank):
        self.T, self.bank = T, bank
        self.w1, self.w2 = T["l3_w1"], T["l3_w2"]
        self.w2f = self.w2[:, :, :].rearrange("p k c -> p (k c)")
        self.ones = s.sb("ones", [P, P])
        self.rs = s.sb("rs", [P, 2, QG])
        self.mu = s.sb("mu", [P, 2, QG])
        self.sg = s.sb("sg", [P, 2, HID])
        self.rs_done, self.mu_in, self.centred, self.signs = (
            s.sem(n) for n in ("rs_done", "mu_in", "centred", "signs"))

    def w2_groups(self, k):
        return self.w2[:, k, 0:QG * (C // QG)].rearrange("p (g r) -> p g r", g=QG)

    def dve_sums(self, dve, chain):
        T, rs, mu = self.T, self.rs, self.mu
        dve.memset(self.ones[:, :], 1.0)
        dve.memset(rs[:, :, :], 0.0)
        chain.sync(dve.memset(self.sg[:, :, :], 0.0))
        dve.wait_ge(T["late_in"], 16 * len(LATE))
        wqk, wv, wx, wo = T["l1_wqk"], T["l1_wv"], T["l1_wx"], T["l1_wo"]
        dve.tensor_tensor(wqk[0:C, :, :, :], wqk[0:C, :, :, :], T["l1_sqk"][:, :, :, :], ALU.mult)
        dve.tensor_tensor(wv[0:C, :], wv[0:C, :], T["l1_sv"][:, :], ALU.mult)
        dve.tensor_tensor(wx[0:C, :], wx[0:C, :], T["l1_so"][:, :], ALU.mult)
        dve.tensor_tensor(wo[:, :], wo[:, :], T["l1_so"][0:DS, :], ALU.mult)
        g1 = self.w1[0:C, 0:QG * (HID // QG)].rearrange("c (g r) -> c g r", g=QG)
        dve.tensor_reduce(rs[0:C, 0, :], g1, AX.X, ALU.add)
        for k in range(KC):
            chain.sync(dve.tensor_reduce(mu[:, 0, :], self.w2_groups(k), AX.X, ALU.add))
            chain.sync(dve.tensor_tensor(rs[:, 1, :], rs[:, 1, :], mu[:, 0, :], ALU.add))
        dve.sem_inc(self.rs_done, 1)

    def pe_means(self, pe):
        pe.wait_ge(self.rs_done, 1)
        pe.matmul(self.bank[:, 0:2 * QG], self.ones[:, :], self.rs[:, :, :].rearrange("p a g -> p (a g)"),
                  start=True, stop=True).then_inc(self.mu_in, 1)

    def dve_centre(self, dve, chain):
        w1, w2, mu = self.w1, self.w2, self.mu
        R1, R2 = HID // QG, C // QG
        dve.wait_ge(self.mu_in, 1)
        dve.tensor_scalar(mu[:, 0, :], self.bank[:, 0:QG], 1.0 / (R1 * C), None, ALU.mult)
        chain.sync(dve.tensor_scalar(mu[:, 1, :], self.bank[:, QG:2 * QG], 1.0 / (R2 * HID), None, ALU.mult))
        g1 = w1[0:C, 0:QG * R1].rearrange("c (g r) -> c g r", g=QG)
        dve.tensor_tensor(g1, g1, mu[0:C, 0, :].unsqueeze(2).broadcast_to([C, QG, R1]), ALU.subtract)
        for k in range(KC):
            part = self.w2_groups(k)
            dve.tensor_tensor(part, part, mu[:, 1, :].unsqueeze(2).broadcast_to([P, QG, R2]), ALU.subtract)
        dve.memset(w1[0:C, QG * R1:HID], 0.0)
        chain.sync(dve.memset(w2[:, :, QG * R2:C], 0.0))
        dve.sem_inc(self.centred, 1)

    def act_signs(self, act):
        act.wait_ge(self.centred, 1)
        act.activation(self.sg[0:C, 0, :], self.w1[0:C, :], ACT.Sign)
        act.activation(self.sg[:, 1, 0:KC * C], self.w2f, ACT.Sign).then_inc(self.signs, 1)

    def dve_binarise(self, dve, chain):
        w1, w2f, sg = self.w1, self.w2f, self.sg
        dve.wait_ge(self.signs, 1)
        dve.tensor_tensor(sg[0:C, 0, :], sg[0:C, 0, :], w1[0:C, :], ALU.subtract)
        chain.sync(dve.tensor_tensor(sg[:, 1, 0:KC * C], sg[:, 1, 0:KC * C], w2f, ALU.subtract))
        dve.tensor_tensor(w1[0:C, :], w1[0:C, :], sg[0:C, 0, :], ALU.add)
        dve.tensor_tensor(w2f, w2f, sg[:, 1, 0:KC * C], ALU.add)


def l0_conv(nc, T, A):
    with ExitStack() as ctx:
        s = Scope(nc, ctx, "l0c")
        x0 = s.sb("x0", [P, NT, C])
        xn = s.sb("xn", [P, 2, C, SIDE])
        xt = s.sb("xt", [P, NG, NI, SIDE])
        band = s.sb("band", [P, NG, KL, SIDE])
        band_s = s.sb("band_s", [P, NG, KS, SIDE])
        full = s.sb("full", [P, NG * KL, GC, SIDE])
        bn = s.sb("bn", [P, 4, 3, NG])
        inv = s.sb("inv", [P, 3, NG])
        shift = s.sb("shift", [P, 3, NG])
        eye = s.sb("eye", [P, SIDE])
        eyes = s.sb("eyes", [P, NG, SIDE])
        own = s.sb("own", [P, GC])
        mhalf = s.sb("mhalf", [P, 3 * NG])
        stats = s.sb("stats", [P, NT, 6])
        mean = s.sb("mean", [P, NT])
        var = s.sb("var", [P, NT])
        rstd = s.sb("rstd", [P, NT])
        conv = s.sb("conv", [P, 2, PIX])
        back = x0[:, :, :].rearrange("p (h x) c -> p h x c", h=2)
        backB = xn[:, :, :, :].rearrange("p h c x -> p (h c x)").rearrange("p (t c) -> p t c", c=C)
        tp = [s.psum(f"tp{i}", [P, 512]) for i in range(2)]
        cp = [s.psum(f"cp{i}", [P, 512]) for i in range(2)]
        bp = [s.psum(f"bp{i}", [P, 512]) for i in range(2)]
        x0_in = [s.sem(f"x0_in{h}") for h in range(2)]
        bn_in, w_in, res_in, ident_in = (s.sem(n) for n in ("bn_in", "w_in", "res_in", "ident_in"))
        mhalf_set, v_eps, bn_pow, ln_var, ln_rstd = (s.sem(n) for n in
            ("mhalf_set", "v_eps", "bn_pow", "ln_var", "ln_rstd"))
        dve_step, band_done, full_done, xn_done = (s.sem(n) for n in
            ("dve_step", "band_done", "full_done", "xn_done"))
        turned, xt_done, conv_done, conv_out, back_done, back_out = (s.sem(n) for n in
            ("turned", "xt_done", "conv_done", "conv_out", "back_done", "back_out"))
        stored = [s.sem(f"stored{k}") for k in range(2)]
        reread = [s.sem(f"reread{k}") for k in range(2)]
        FG = 3
        work = WeightWork(s, T, tp[0])
        block = ctx.enter_context(nc.Block())

        @block.sync
        def _(sp):
            for h in range(2):
                half = slice(h * SIDE, (h + 1) * SIDE)
                sp.dma_start(x0[:, half, :], A["x_rows"][:, half, :]).then_inc(x0_in[h], 16)
            sp.dma_start(T["ident"][:, :], A["ident"]).then_inc(ident_in, 16)
            sp.wait_ge(w_in, 64)
            sp.dma_start(T["X"][:, :, :], A["x_tokens"]).then_inc(res_in, 16)
            load_weights(sp, T, A)
            for k in range(2):
                chans = slice(k * HALF, (k + 1) * HALF)
                sp.wait_ge(back_out, (k + 1) * NG // 2)
                for h in range(2):
                    sp.dma_start(T["scratch"][h * (NI // 2) * PIX:(h + 1) * (NI // 2) * PIX, chans]
                                 .rearrange("(p x) c -> p x c", x=SIDE), back[:, h, :, chans]
                                 ).then_inc(stored[k], 16)
                sp.wait_ge(stored[k], 32)
                sp.dma_start(backB[:, :, chans], T["scratch"][:, chans].rearrange("(t p) c -> p t c", p=P)
                             ).then_inc(reread[k], 16)

        @block.gpsimd
        def _(pool):
            pool.memset(mhalf[:, :], -0.5).then_inc(mhalf_set, 1)
            pool.wait_ge(mhalf_set, 1)
            pool.wait_ge(v_eps, 1)
            pool.tensor_tensor(inv[:, :, :], shift[:, :, :], mhalf[:, :].rearrange("p (k g) -> p k g", k=3),
                               ALU.pow).then_inc(bn_pow, 1)
            for h in range(2):
                half = slice(h * SIDE, (h + 1) * SIDE)
                pool.wait_ge(ln_var, h + 1)
                pool.tensor_tensor(rstd[:, half], var[:, half], mhalf[:, 0:SIDE], ALU.pow).then_inc(ln_rstd, 1)

        @block.scalar
        def _(act):
            act.dma_start(bn[:, :, :, :], A["bn"]).then_inc(bn_in, 16)
            act.dma_start(band[:, :, :, :], A["band"]).then_inc(w_in, 16)
            act.dma_start(band_s[:, :, :, :], A["band_s"]).then_inc(w_in, 16)
            act.dma_start(eye[:, :], A["eye"]).then_inc(w_in, 16)
            act.dma_start(own[:, :], A["own"]).then_inc(w_in, 16)

            def fill(chunk):
                groups = slice(chunk * FG, (chunk + 1) * FG)
                rows = slice(chunk * FG * KL, (chunk + 1) * FG * KL)
                for k in range(GC):
                    last = act.activation(full[:, rows, k, :], band[:, groups, :, :].rearrange("p g r x -> p (g r) x"),
                                          ACT.Copy, scale=own[:, k:k + 1])
                last.then_inc(full_done, 1)

            act.wait_ge(band_done, 1)
            fill(0)
            fill(1)
            for g2 in range(NG // 2):
                act.wait_ge(turned, g2 + 1)
                act.activation(xt[:, 2 * g2:2 * g2 + 2, :, :].rearrange("p g i r -> p (g i r)"), tp[g2 % 2][:, :],
                               ACT.Copy).then_inc(xt_done, 1)
            for g in range(NG):
                act.wait_ge(conv_done, g + 1)
                if g >= 2:
                    act.wait_ge(back_done, g - 1)
                act.activation(conv[:, g % 2, :], cp[g % 2][:, 0:PIX], ACT.Identity,
                               bias=shift[:, 0, g:g + 1]).then_inc(conv_out, 1)
                if g in (0, 2):
                    fill(2 + g // 2)
            work.act_signs(act)

        @block.vector
        def _(dve):
            chain = Chain(dve, dve_step)
            dve.wait_ge(bn_in, 16)
            chain.sync(dve.tensor_scalar(shift[:, :, :], bn[:, 3, :, :], BN_EPS, None, ALU.add))
            dve.sem_inc(v_eps, 1)
            tiles = [x0[:, t, :] for t in range(NT)]
            halves = [slice(h * SIDE, (h + 1) * SIDE) for h in range(2)]
            for h, half in enumerate(halves):
                dve.wait_ge(x0_in[h], 16)
                layernorm_stats(dve, chain, tiles[half], stats[:, half, :], mean[:, half], var[:, half], 1e-6)
                dve.sem_inc(ln_var, 1)
            dve.wait_ge(bn_pow, 1)
            chain.sync(dve.tensor_tensor(inv[:, :, :], inv[:, :, :], bn[:, 0, :, :], ALU.mult))
            chain.sync(dve.tensor_tensor(shift[:, :, :], bn[:, 2, :, :], inv[:, :, :], ALU.mult))
            chain.sync(dve.tensor_tensor(shift[:, :, :], bn[:, 1, :, :], shift[:, :, :], ALU.subtract))
            chain.sync(dve.tensor_tensor(shift[:, 0, :], shift[:, 0, :], shift[:, 1, :], ALU.add))
            chain.sync(dve.tensor_tensor(shift[:, 0, :], shift[:, 0, :], shift[:, 2, :], ALU.add))
            dve.wait_ge(w_in, 64)
            bv = band[:, :, :, :].rearrange("p g r x -> p g (r x)")
            sv = band_s[:, :, :, :].rearrange("p g r x -> p g (r x)")
            dve.tensor_tensor(bv, bv, inv[:, 0, :].unsqueeze(2).broadcast_to([P, NG, KL * SIDE]), ALU.mult)
            dve.tensor_tensor(sv, sv, inv[:, 1, :].unsqueeze(2).broadcast_to([P, NG, KS * SIDE]), ALU.mult)
            chain.sync(dve.tensor_tensor(eyes[:, :, :], eye[:, :].unsqueeze(1).broadcast_to([P, NG, SIDE]),
                                         inv[:, 2, :].unsqueeze(2).broadcast_to([P, NG, SIDE]), ALU.mult))
            mid = (KL - KS) // 2
            inner = band[:, :, mid:mid + KS, :].rearrange("p g r x -> p g (r x)")
            chain.sync(dve.tensor_tensor(inner, inner, sv, ALU.add))
            chain.sync(dve.tensor_tensor(band[:, :, KL // 2, :], band[:, :, KL // 2, :], eyes[:, :, :], ALU.add))
            dve.sem_inc(band_done, 1)
            for h, half in enumerate(halves):
                dve.wait_ge(ln_rstd, h + 1)
                layernorm_apply(dve, chain, tiles[half], [xn[:, h, :, t] for t in range(SIDE)],
                                stats[:, half, :], mean[:, half], rstd[:, half]).then_inc(xn_done, 1)
            for g in range(NG):
                dve.wait_ge(back_done, g + 1)
                dve.tensor_copy(back[:, :, :, GC * g:GC * (g + 1)],
                                bp[g % 2][:, 0:PIX].rearrange("p (h c x) -> p h x c", h=2, x=SIDE)
                                ).then_inc(back_out, 1)
                if g == NG - 7:
                    work.dve_sums(dve, chain)
                if g == NG - 3:
                    work.dve_centre(dve, chain)
            work.dve_binarise(dve, chain)
            dve.wait_ge(res_in, 16)
            for k in range(2):
                chans = slice(k * HALF, (k + 1) * HALF)
                dve.wait_ge(reread[k], 16)
                dve.tensor_tensor(T["X"][:, :, chans], T["X"][:, :, chans], backB[:, :, chans], ALU.add)

        @block.tensor
        def _(pe):
            ident = T["ident"]
            pe.wait_ge(ident_in, 16)
            pe.wait_ge(xn_done, 2)
            for g2 in range(NG // 2):
                if g2 >= 2:
                    pe.wait_ge(xt_done, g2 - 1)
                for k in range(4):
                    g, h = 2 * g2 + k // 2, k % 2
                    last = pe.transpose(tp[g2 % 2][:, k * P:(k + 1) * P], xn[:, h, GC * g:GC * (g + 1), :]
                                        .rearrange("p c x -> p (c x)"), ident[:, :])
                last.then_inc(turned, 1)

            def conv_group(g):
                pe.wait_ge(xt_done, g // 2 + 1)
                pe.wait_ge(full_done, g // FG + 1)
                if g >= 2:
                    pe.wait_ge(conv_out, g - 1)
                out = cp[g % 2][:, 0:PIX].rearrange("p (i r) -> p i r", r=SIDE)
                order = [KL // 2] + [r for r in range(KL) if r != KL // 2]
                for n, r in enumerate(order):
                    d = r - KL // 2
                    lo, hi = max(0, -d), min(SIDE, SIDE - d)
                    last = pe.matmul(out[:, :, lo:hi], full[:, g * KL + r, :, :].rearrange("p c x -> p (c x)"),
                                     xt[:, g, :, lo + d:hi + d], start=(n == 0), stop=(n == KL - 1))
                last.then_inc(conv_done, 1)

            def turn_back(g):
                pe.wait_ge(conv_out, g + 1)
                if g >= 2:
                    pe.wait_ge(back_out, g - 1)
                for h in range(2):
                    last = pe.transpose(bp[g % 2][:, h * P:(h + 1) * P], conv[:, g % 2, h * P:(h + 1) * P],
                                        ident[:, :])
                last.then_inc(back_done, 1)

            conv_group(0)
            for g in range(NG):
                if g + 1 < NG:
                    conv_group(g + 1)
                turn_back(g)
                if g == NG - 4:
                    work.pe_means(pe)


def moe(nc, T, A, layer):
    w1, w2, gw, b2 = T["moe"][layer]
    X, ident = T["X"], T["ident"]
    STEPS = NT // GT
    UPS = 4
    with ExitStack() as ctx:
        s = Scope(nc, ctx, f"moe{layer}")
        w1h = s.sb("w1h", [CB, NE * KC, P], F32R)
        w1l = s.sb("w1l", [CB, NE * KC, P], F32R)
        xn = s.sb("xn", [P, GT, C])
        xt = s.sb("xt", [CB, 2, GW])
        xh = s.sb("xh", [CB, 2, GW], F32R)
        xl = s.sb("xl", [CB, 2, GW], F32R)
        hid = s.sb("hid", [P, NE * KC, GW])
        stats = s.sb("stats", [P, GT, 6])
        mean = s.sb("mean", [P, GT])
        var = s.sb("var", [P, GT])
        rstd = s.sb("rstd", [P, GT])
        mhalf = s.sb("mhalf", [P, GT])
        euler = s.sb("euler", [P, GT * NE])
        smax = s.sb("smax", [P, GT])
        logit = s.sb("logit", [P, GT, NE])
        prob = s.sb("prob", [P, GT, NE])
        ge = s.sb("ge", [P, 3, GT, NE])
        rank = s.sb("rank", [P, GT, NE])
        gate = s.sb("gate", [P, 2, GT, NE])
        up = [s.psum(f"up{i}", [P, 512]) for i in range(UPS)]
        tp = s.psum("tp", [P, 512])
        gp = s.psum("gp", [P, 512])
        dn = [s.psum(f"dn{i}", [P, 512]) for i in range(2)]
        names = ("consts", "var_done", "rstd_done", "logit_done", "exp_done", "dve_step", "xn_done", "turned",
                 "xt_done", "xl_done", "w_high", "w_low", "gates_in", "gates_read", "up_done", "hid_done",
                 "down_done", "added")
        (consts, var_done, rstd_done, logit_done, exp_done, dve_step, xn_done, turned, xt_done, xl_done, w_high,
         w_low, gates_in, gates_read, up_done, hid_done, down_done, added) = (s.sem(n) for n in names)
        block = ctx.enter_context(nc.Block())

        def steps(eng, step):
            step(0, 0, False)
            with eng.Fori(1, STEPS // 2) as i:
                step(2 * i - 1, 1, False)
                step(2 * i, 0, False)
            step(STEPS - 1, 1, True)

        def expert(t, e):
            return t[:, e * KC:(e + 1) * KC, :]

        @block.gpsimd
        def _(pool):
            pool.memset(mhalf[:, :], -0.5)
            pool.memset(euler[:, :], float(np.e)).then_inc(consts, 1)
            pool.wait_ge(consts, 1)

            def rstd_of(g):
                pool.wait_ge(var_done, g + 1)
                pool.tensor_tensor(rstd[:, :], var[:, :], mhalf[:, :], ALU.pow).then_inc(rstd_done, 1)

            def exp_of(g):
                pool.wait_ge(logit_done, g + 1)
                pool.tensor_tensor(prob[:, :, :], euler[:, :].rearrange("p (t e) -> p t e", e=NE),
                                   logit[:, :, :], ALU.pow).then_inc(exp_done, 1)

            with pool.Fori(0, STEPS) as g:
                rstd_of(g)
                exp_of(g)

        @block.vector
        def _(dve):
            STATS, APPLY, GATES = 4, 2, 15
            EACH = STATS + APPLY + GATES + 2 * NE

            def stats_of(g, chain):
                layernorm_stats(dve, chain, [X[:, GT * g + j, :] for j in range(GT)], stats, mean, var, 1e-5)
                dve.sem_inc(var_done, 1)

            def apply_of(g, chain):
                wait(dve, rstd_done, g + 1)
                wait(dve, turned, g)
                layernorm_apply(dve, chain, [X[:, GT * g + j, :] for j in range(GT)],
                                [xn[:, j, :] for j in range(GT)], stats, mean, rstd).then_inc(xn_done, 1)

            def low_of(g, p):
                wait(dve, xt_done, g + 1)
                dve.tensor_tensor(xl[0:C, p, :], xt[0:C, p, :], xh[0:C, p, :].bitcast(F32), ALU.subtract
                                  ).then_inc(xl_done, 1)

            def gates_of(g, p, chain):
                wide = lambda a: a.unsqueeze(2).broadcast_to([P, GT, NE])
                scores = gp[:, 0:GT * NE].rearrange("p (t e) -> p t e", e=NE)
                wait(dve, gates_in, g + 1)
                chain.sync(dve.tensor_reduce(smax[:, :], scores, AX.X, ALU.max))
                chain.sync(dve.tensor_tensor(logit[:, :, :], scores, wide(smax[:, :]), ALU.subtract))
                dve.sem_inc(logit_done, 1)
                dve.sem_inc(gates_read, 1)
                for e in range(NE):
                    dve.memset(rank[:, :, e], float(NE - 1 - e))
                wait(dve, exp_done, g + 1)
                chain.sync(dve.tensor_reduce(smax[:, :], prob[:, :, :], AX.X, ALU.add))
                chain.sync(dve.reciprocal(smax[:, :], smax[:, :]))
                chain.sync(dve.tensor_tensor(prob[:, :, :], prob[:, :, :], wide(smax[:, :]), ALU.mult))
                for d in range(1, NE):
                    last = dve.tensor_tensor(ge[:, d - 1, :, 0:NE - d], prob[:, :, 0:NE - d], prob[:, :, d:NE],
                                             ALU.is_ge)
                chain.sync(last)
                for d in range(1, NE):
                    ahead = ge[:, d - 1, :, 0:NE - d]
                    last = dve.tensor_tensor(rank[:, :, d:NE], rank[:, :, d:NE], ahead, ALU.add)
                    if d < NE / 2:
                        chain.sync(last)
                    chain.sync(dve.tensor_tensor(rank[:, :, 0:NE - d], rank[:, :, 0:NE - d], ahead, ALU.subtract))
                best = gate[:, p, :, :]
                chain.sync(dve.scalar_tensor_tensor(
                    out=best.rearrange("p t e -> p (t e)"), in0=rank[:, :, :].rearrange("p t e -> p (t e)"),
                    scalar=2.0, in1=prob[:, :, :].rearrange("p t e -> p (t e)"), op0=ALU.is_lt, op1=ALU.mult))
                chain.sync(dve.tensor_reduce(smax[:, :], best, AX.X, ALU.add))
                chain.sync(dve.tensor_scalar(smax[:, :], smax[:, :], 1e-9, None, ALU.add))
                chain.sync(dve.reciprocal(smax[:, :], smax[:, :]))
                chain.sync(dve.tensor_tensor(best, best, wide(smax[:, :]), ALU.mult))

            def bias_sums(g, p, chain):
                for e in range(NE):
                    for j in range(GT):
                        x = X[:, GT * g + j, :]
                        last = dve.scalar_tensor_tensor(out=x, in0=b2[:, e, :], scalar=gate[:, p, j, e:e + 1], in1=x,
                                                        op0=ALU.mult, op1=ALU.add)
                    chain.sync(last)

            def expert_sum(g, p, e, chain):
                wait(dve, down_done, NE * g + e + 1)
                for j in range(GT):
                    x = X[:, GT * g + j, :]
                    last = dve.scalar_tensor_tensor(out=x, in0=dn[e % 2][:, j * C:(j + 1) * C],
                                                    scalar=gate[:, p, j, e:e + 1], in1=x, op0=ALU.mult, op1=ALU.add)
                chain.sync(last)
                dve.sem_inc(added, 1)

            def step(g, p, last):
                chain = Chain(dve, dve_step, base + g * EACH)
                bias_sums(g, p, chain)
                if not last:
                    stats_of(g + 1, chain)
                expert_sum(g, p, 0, chain)
                if not last:
                    apply_of(g + 1, chain)
                expert_sum(g, p, 1, chain)
                if not last:
                    low_of(g + 1, 1 - p)
                    gates_of(g + 1, 1 - p, chain)
                expert_sum(g, p, 2, chain)
                expert_sum(g, p, 3, chain)
                assert chain.n == (2 * NE if last else EACH), chain.n

            dve.memset(xt[C:CB, :, :], 1.0)
            chain = Chain(dve, dve_step)
            stats_of(0, chain)
            dve.wait_ge(consts, 1)
            dve.tensor_copy(xh[C:CB, :, :], xt[C:CB, :, :])
            dve.tensor_tensor(xl[C:CB, :, :], xt[C:CB, :, :], xt[C:CB, :, :], ALU.subtract)
            apply_of(0, chain)
            for e in range(NE):
                dve.wait_ge(w_high, e + 1)
                dve.tensor_tensor(expert(w1l, e), expert(w1, e), expert(w1h, e).bitcast(F32), ALU.subtract
                                  ).then_inc(w_low, 1)
                if e == 0:
                    low_of(0, 0)
            gates_of(0, 0, chain)
            base = chain.n
            steps(dve, step)

        @block.scalar
        def _(act):
            def gelus(g, e):
                for k in range(KC):
                    n = e * KC + k
                    if k == 0:
                        wait(act, down_done, NE * (g - 1) + e + 1)
                    wait(act, up_done, NE * KC * g + n + 1)
                    act.activation(hid[:, n, :], up[n % UPS][:, :], ACT.Gelu).then_inc(hid_done, 1)

            def turned_out(g, p):
                wait(act, turned, g + 1)
                act.activation(xh[0:C, p, :], tp[0:C, :], ACT.Copy)
                act.activation(xt[0:C, p, :], tp[0:C, :], ACT.Copy).then_inc(xt_done, 1)

            act.wait_ge(T["moe_in"][layer], 64)
            act.activation(expert(w1h, 0), expert(w1, 0), ACT.Copy).then_inc(w_high, 1)
            turned_out(0, 0)
            for e in range(1, NE):
                act.activation(expert(w1h, e), expert(w1, e), ACT.Copy).then_inc(w_high, 1)
            gelus(0, 0)

            def step(g, p, last):
                gelus(g, 1)
                gelus(g, 2)
                if not last:
                    turned_out(g + 1, 1 - p)
                gelus(g, 3)
                if not last:
                    gelus(g + 1, 0)

            steps(act, step)

        @block.tensor
        def _(pe):
            def turn(g):
                wait(pe, xn_done, g + 1)
                wait(pe, xt_done, g)
                for j in range(GT):
                    last = pe.transpose(tp[0:C, j * P:(j + 1) * P], xn[:, j, :], ident[:, :])
                last.then_inc(turned, 1)

            def gates(g, p):
                wait(pe, xt_done, g + 1)
                wait(pe, gates_read, g)
                for j in range(GT):
                    last = pe.matmul(gp[:, j * NE:(j + 1) * NE], xt[:, p, j * P:(j + 1) * P], gw[:, :],
                                     start=True, stop=True)
                last.then_inc(gates_in, 1)

            def ups(g, p, e):
                if e == 0:
                    wait(pe, xl_done, g + 1)
                for k in range(KC):
                    n = e * KC + k
                    wait(pe, hid_done, NE * KC * g + n - UPS + 1)
                    bank = up[n % UPS][:, :]
                    pe.matmul(bank, w1h[:, n, :], xh[:, p, :], start=True, stop=False)
                    pe.matmul(bank, w1l[:, n, :], xh[:, p, :], start=False, stop=False)
                    pe.matmul(bank, w1h[:, n, :], xl[:, p, :], start=False, stop=True).then_inc(up_done, 1)

            def downs(g, e):
                wait(pe, hid_done, NE * KC * g + (e + 1) * KC)
                wait(pe, added, NE * g + e - 1)
                for j in range(GT):
                    for k in range(KC):
                        n = e * KC + k
                        last = pe.matmul(dn[e % 2][:, j * C:(j + 1) * C], hid[:, n, j * P:(j + 1) * P], w2[:, n, :],
                                         start=(k == 0), stop=(k == KC - 1))
                last.then_inc(down_done, 1)

            def step(g, p, last):
                for e in range(1, NE):
                    if isinstance(g, int) and g == 0:
                        wait(pe, w_low, e + 1)
                    ups(g, p, e)
                    if e == NE - 1 and not last:
                        gates(g + 1, 1 - p)
                    downs(g, e - 1)
                    if e == NE - 2 and not last:
                        turn(g + 1)
                if not last:
                    ups(g + 1, 1 - p, 0)
                downs(g, NE - 1)

            pe.wait_ge(T["moe_in"][layer], 64)
            turn(0)
            gates(0, 0)
            pe.wait_ge(w_low, 1)
            ups(0, 0, 0)
            steps(pe, step)


def l1_attention(nc, T, A):
    X, ident = T["X"], T["ident"]
    H, NB = HEADS, NI
    VW, VWIDE = DH + 1, 2 * DH
    VROW = (H - 1) * VW + VWIDE
    with ExitStack() as ctx:
        s = Scope(nc, ctx, "l1c")
        wqk, wv, wp, sp_, wo, wx, low, sel = (T[f"l1_{n}"] for n in ("wqk", "wv", "wp", "sp", "wo", "wx", "low", "sel"))
        selr = s.sb("selr", [P, H, P], F32R)
        xn = s.sb("xn", [P, 2, C])
        xi = s.sb("xi", [P, PIX])
        high = s.sb("high", [P, 3, 2 * PIX], F32R)
        qk = s.sb("qk", [P, 2, 3, 2 * PIX], F32R)
        vs = s.sb("vs", [P, 2, 2, VROW])
        nmax = s.sb("nmax", [P, 2, 2 * H])
        nmh = s.sb("nmh", [2 * H, PIX], F32R)
        nms = s.sb("nms", [P, PIX], F32R)
        pt = s.sb("pt", [P, 2, 2 * PIX])
        rinv = s.sb("rinv", [P, 2 * H])
        ro = s.sb("ro", [P, 2, H * DH])
        rt = s.sb("rt", [C, 2, PIX])
        u = s.sb("u", [DS, PIX])
        y0 = s.sb("y0", [P, 2, 2 * C])
        y1 = s.sb("y1", [P, 2 * C])
        stats = s.sb("stats", [P, 2, 6])
        mean = s.sb("mean", [P, 2])
        var = s.sb("var", [P, 2])
        rstd = s.sb("rstd", [P, 2])
        mhalf = s.sb("mhalf", [P, 2])
        sc_ps = [s.psum(f"sc{i}", [P, 512]) for i in range(2)]
        st_ps = [s.psum(f"st{i}", [P, 512]) for i in range(2)]
        o_ps = [s.psum(f"o{i}", [P, 512]) for i in range(2)]
        m1 = s.psum("m1", [P, 512])
        m2 = s.psum("m2", [P, 512])
        names = ("consts", "ready", "var_done", "rstd_done", "dve_step", "xn_done", "tok_in", "xi_done",
                 "unit_in", "unit_high", "unit_done", "v_in", "v_done", "x_in", "x_done", "scored", "maxed",
                 "max_done", "nm_in", "nm_high", "nm_done", "st_in", "exped", "valued", "ro_done", "ht_in",
                 "ht_done", "wp_in", "wp_done", "wo_in", "wo_done")
        S = {n: s.sem(n) for n in names}
        block = ctx.enter_context(nc.Block())
        def images(eng, body, tail=1):
            for b in range(3):
                body(b, b % 2)
            with eng.Fori(1, (NB - tail - 1) // 2) as i:
                body(2 * i + 1, 1)
                body(2 * i + 2, 0)
            for b in range(NB - tail, NB):
                body(b, b % 2)

        def is_last(b, n=1):
            return isinstance(b, int) and b >= NB - n

        def operand(kind, b_par, h):
            g, lo = h // 2, KS3 * (h % 2)
            unit, col = (kind, g * PIX) if g < 2 else (2, kind * PIX)
            return qk[lo:lo + KS3, b_par, unit, col:col + PIX]

        @block.gpsimd
        def _(pool):
            pool.memset(mhalf[:, :], -0.5).then_inc(S["consts"], 1)
            pool.wait_ge(S["consts"], 1)
            with pool.Fori(0, NB) as b:
                pool.wait_ge(S["var_done"], b + 1)
                pool.tensor_tensor(rstd[:, :], var[:, :], mhalf[:, :], ALU.pow).then_inc(S["rstd_done"], 1)

        @block.vector
        def _(dve):
            EACH = 4 + 2 + 2

            def ln_stats(b, chain):
                layernorm_stats(dve, chain, [X[:, 2 * b + t, :] for t in range(2)], stats, mean, var, 1e-6)
                dve.sem_inc(S["var_done"], 1)

            def ln_apply(b, chain):
                wait(dve, S["rstd_done"], b + 1)
                wait(dve, S["tok_in"], b)
                layernorm_apply(dve, chain, [X[:, 2 * b + t, :] for t in range(2)], [xn[:, t, :] for t in range(2)],
                                stats, mean, rstd).then_inc(S["xn_done"], 1)

            def row_max(b, h):
                wait(dve, S["scored"], H * b + h + 1)
                if h == 0:
                    wait(dve, S["nm_in"], b)
                dve.tensor_reduce(nmax[:, :, h], sc_ps[h % 2][:, :].rearrange("p (t m) -> p t m", t=2),
                                  AX.X, ALU.max, negate=True).then_inc(S["maxed"], 1)

            def maxima(b):
                wait(dve, S["maxed"], H * (b + 1))
                dve.tensor_scalar(nmax[:, :, H:2 * H], nmax[:, :, 0:H], 1.0, None, ALU.mult
                                  ).then_inc(S["max_done"], 1)

            def maxima_low(b):
                wait(dve, S["nm_high"], b + 1)
                wait(dve, S["st_in"], H * b)
                dve.scalar_tensor_tensor(out=nms[0:2 * H, :], in0=nmh[:, :].bitcast(F32), scalar=low[0:2 * H, 2:3],
                                         in1=m1[0:2 * H, 0:PIX], op0=ALU.mult, op1=ALU.add
                                         ).then_inc(S["nm_done"], 1)

            def unit_low(b, p, n):
                wait(dve, S["unit_high"], 3 * b + n + 1)
                if n == 0:
                    wait(dve, S["st_in"], H * (b - 1))
                bank = (m1, m2, m1)[n]
                for c in range(2) if n == 2 else (slice(0, 2),):
                    cols = slice(c * PIX, (c + 1) * PIX) if n == 2 else slice(0, 2 * PIX)
                    kind = c if n == 2 else n
                    last = dve.scalar_tensor_tensor(out=qk[:, p, n, cols], in0=high[:, n, cols].bitcast(F32),
                                                    scalar=low[:, kind:kind + 1], in1=bank[:, cols],
                                                    op0=ALU.mult, op1=ALU.add)
                last.then_inc(S["unit_done"], 1)

            def norm_heads(b, p, chain):
                wait(dve, S["valued"], H * (b + 1))
                wait(dve, S["ht_in"], b)
                o = o_ps[p][:, 0:2 * H * VW].rearrange("p (h d) -> p h d", d=VW)
                chain.sync(dve.reciprocal(rinv[:, :], o[:, :, DH]))
                for t in range(2):
                    half = slice(t, 2 * H, 2)
                    last = dve.scalar_tensor_tensor(out=ro[:, t, :].rearrange("p (h d) -> p h d", h=H),
                                                    in0=o[:, half, 0:DH], scalar=0.0,
                                                    in1=rinv[:, half].unsqueeze(2).broadcast_to([P, H, DH]),
                                                    op0=ALU.max, op1=ALU.mult)
                last.then_inc(S["ro_done"], 1)

            def wp_out(b):
                wait(dve, S["wp_in"], b + 1)
                dve.tensor_scalar(u[:, :], m2[0:DS, 0:PIX], sp_[:, 0:1], sp_[:, 1:2], ALU.mult, ALU.add
                                  ).then_inc(S["wp_done"], 1)

            def wo_out(b, p, chain):
                wait(dve, S["wo_in"], b + 1)
                wait(dve, S["x_done"], b + 1)
                chain.sync(dve.tensor_tensor(y1[:, :], m2[:, 0:2 * C], y0[:, p, :], ALU.add))
                x = X[:, bass.ds(2 * b, 2), :].rearrange("p t c -> p (t c)")
                dve.scalar_tensor_tensor(out=x, in0=y1[:, :], scalar=0.0, in1=x, op0=ALU.max, op1=ALU.add
                                         ).then_inc(S["wo_done"], 1)

            def body(b, p):
                first = isinstance(b, int) and b == 0
                chain = Chain(dve, S["dve_step"], base + b * EACH - (6 if is_last(b) else 0))
                maxima_low(b)
                if not first:
                    norm_heads(b - 1, 1 - p, chain)
                else:
                    chain.sync(dve.tensor_scalar(rinv[:, :], rinv[:, :], 1.0, None, ALU.mult))
                if not is_last(b):
                    unit_low(b + 1, 1 - p, 0)
                    unit_low(b + 1, 1 - p, 1)
                if not is_last(b, 2):
                    ln_stats(b + 2, chain)
                if not is_last(b):
                    unit_low(b + 1, 1 - p, 2)
                if not is_last(b, 2):
                    ln_apply(b + 2, chain)
                if not is_last(b):
                    row_max(b + 1, 0)
                    row_max(b + 1, 1)
                if not first:
                    wp_out(b - 1)
                if not is_last(b):
                    row_max(b + 1, 2)
                    row_max(b + 1, 3)
                if not first:
                    wo_out(b - 1, 1 - p, chain)
                else:
                    chain.sync(dve.tensor_scalar(rinv[:, :], rinv[:, :], 1.0, None, ALU.mult))
                if not is_last(b):
                    row_max(b + 1, 4)
                    row_max(b + 1, 5)
                    maxima(b + 1)

            dve.memset(rinv[:, :], 1.0)
            dve.memset(vs[:, :, :, :], 1.0)
            chain = Chain(dve, S["dve_step"])
            chain.sync(dve.memset(xi[C:P, :], 0.0))
            dve.memset(xi[C:CB, :], 1.0)
            ln_stats(0, chain)
            ln_apply(0, chain)
            dve.tensor_copy(selr[:, :, :], sel[:, :, :])
            dve.tensor_copy(nms[:, :], sel[:, 0:2, :].rearrange("p h n -> p (h n)")).then_inc(S["ready"], 1)
            for n in range(3):
                unit_low(0, 0, n)
            ln_stats(1, chain)
            ln_apply(1, chain)
            for h in range(H):
                row_max(0, h)
            maxima(0)
            base = chain.n
            images(dve, body, tail=3)
            last = Chain(dve, S["dve_step"], base + NB * EACH - 2 * 6)
            norm_heads(NB - 1, 1, last)
            wp_out(NB - 1)
            wo_out(NB - 1, 1, last)

        @block.scalar
        def _(act):
            def tokens_out(b):
                wait(act, S["tok_in"], b + 1)
                wait(act, S["x_in"], b)
                act.activation(xi[0:C, :], m2[0:C, 0:PIX], ACT.Copy).then_inc(S["xi_done"], 1)

            def unit_high(b, n):
                wait(act, S["unit_in"], 3 * b + n + 1)
                wait(act, S["unit_done"], 3 * (b - 1) + n + 1)
                act.activation(high[:, n, :], (m1, m2, m1)[n][:, :], ACT.Copy).then_inc(S["unit_high"], 1)

            def maxima_high(b):
                wait(act, S["nm_in"], b + 1)
                wait(act, S["nm_done"], b)
                act.activation(nmh[:, :], m1[0:2 * H, 0:PIX], ACT.Copy).then_inc(S["nm_high"], 1)

            def values_out(b, p):
                wait(act, S["v_in"], b + 1)
                wait(act, S["valued"], H * (b - 1))
                for m in range(2):
                    last = act.activation(vs[:, p, m, 0:H * VW].rearrange("p (h d) -> p h d", d=VW)[:, :, 0:DH],
                                          m2[:, m * H * DH:(m + 1) * H * DH].rearrange("p (h d) -> p h d", d=DH),
                                          ACT.Copy)
                last.then_inc(S["v_done"], 1)

            def residual_out(b, p):
                wait(act, S["x_in"], b + 1)
                wait(act, S["wo_done"], b - 1)
                act.activation(y0[:, p, :], m1[:, 0:2 * C], ACT.Copy).then_inc(S["x_done"], 1)

            def heads_out(b):
                wait(act, S["ht_in"], b + 1)
                wait(act, S["wp_in"], b)
                act.activation(rt[:, :, :].rearrange("p a n -> p (a n)"), m1[0:C, :], ACT.Copy
                               ).then_inc(S["ht_done"], 1)

            def exps(b, h):
                n = H * b + h
                wait(act, S["st_in"], n + 1)
                wait(act, S["valued"], n - 1)
                act.activation(pt[:, h % 2, :], st_ps[h % 2][:, :], ACT.Exp).then_inc(S["exped"], 1)

            def body(b, p):
                first = isinstance(b, int) and b == 0
                if not is_last(b):
                    tokens_out(b + 1)
                maxima_high(b)
                if not is_last(b):
                    unit_high(b + 1, 0)
                exps(b, 0)
                if not is_last(b):
                    unit_high(b + 1, 1)
                exps(b, 1)
                if not is_last(b):
                    unit_high(b + 1, 2)
                exps(b, 2)
                if not is_last(b):
                    values_out(b + 1, 1 - p)
                if not first:
                    heads_out(b - 1)
                exps(b, 3)
                exps(b, 4)
                exps(b, 5)
                if not is_last(b):
                    residual_out(b + 1, 1 - p)

            tokens_out(0)
            for n in range(3):
                unit_high(0, n)
            values_out(0, 0)
            residual_out(0, 0)
            images(act, body)
            heads_out(NB - 1)

        @block.tensor
        def _(pe):
            def turn_tokens(b):
                wait(pe, S["xn_done"], b + 1)
                wait(pe, S["v_done"], b)
                wait(pe, S["wo_done"], b - 2)
                for t in range(2):
                    last = pe.transpose(m2[0:C, t * P:(t + 1) * P], xn[:, t, :], ident[:, :])
                last.then_inc(S["tok_in"], 1)

            def unit(b, n):
                if n == 0:
                    wait(pe, S["xi_done"], b + 1)
                    wait(pe, S["nm_done"], b)
                else:
                    wait(pe, S["unit_done"], 3 * b + (n + 1) // 2 - (n == 1))
                for c in range(2):
                    kind, g = ((0, c), (1, c), (c, 2))[n]
                    last = pe.matmul((m1, m2, m1)[n][:, c * PIX:(c + 1) * PIX], wqk[:, kind, g, :], xi[:, :],
                                     start=True, stop=True)
                last.then_inc(S["unit_in"], 1)

            def value_tokens(b):
                wait(pe, S["unit_done"], 3 * b + 2)
                for t in range(2):
                    last = pe.matmul(m2[:, t * H * DH:(t + 1) * H * DH], xi[0:CB, t * P:(t + 1) * P], wv[:, :],
                                     start=True, stop=True)
                last.then_inc(S["v_in"], 1)

            def residual(b):
                wait(pe, S["unit_done"], 3 * (b + 1))
                wait(pe, S["ht_done"], b - 1)
                for t in range(2):
                    last = pe.matmul(m1[:, t * C:(t + 1) * C], xi[0:CB, t * P:(t + 1) * P], wx[:, :],
                                     start=True, stop=True)
                last.then_inc(S["x_in"], 1)

            def scores(b, p, h):
                if h == 0:
                    wait(pe, S["unit_done"], 3 * (b + 1))
                wait(pe, S["maxed"], H * b + h - 1)
                for t in range(2):
                    last = pe.matmul(sc_ps[h % 2][:, t * PIX:(t + 1) * PIX], operand(0, p, h)[:, t * P:(t + 1) * P],
                                     operand(1, p, h), start=True, stop=True)
                last.then_inc(S["scored"], 1)

            def turn_maxima(b):
                wait(pe, S["max_done"], b + 1)
                wait(pe, S["x_done"], b + 1)
                for t in range(2):
                    last = pe.transpose(m1[0:2 * H, t * P:(t + 1) * P], nmax[:, t, :], ident[:, :])
                last.then_inc(S["nm_in"], 1)

            def turned_scores(b, p, h):
                if h == 0:
                    wait(pe, S["nm_done"], b + 1)
                wait(pe, S["exped"], H * b + h - 1)
                for m in range(2):
                    out = st_ps[h % 2][:, m * PIX:(m + 1) * PIX]
                    pe.matmul(out, operand(1, p, h)[:, m * P:(m + 1) * P], operand(0, p, h), start=True, stop=False)
                    last = pe.matmul(out, selr[:, h, :], nms[:, :], start=False, stop=True)
                last.then_inc(S["st_in"], 1)

            def values(b, p, h):
                wait(pe, S["exped"], H * b + h + 1)
                if h == 0:
                    wait(pe, S["v_done"], b + 1)
                    wait(pe, S["ro_done"], b - 1)
                for t in range(2):
                    for m in range(2):
                        at = (2 * h + t) * VW
                        last = pe.matmul(o_ps[p][:, at:at + VWIDE], pt[:, h % 2, m * PIX + t * P:m * PIX + (t + 1) * P],
                                         vs[:, p, m, h * VW:h * VW + VWIDE], start=(m == 0), stop=(m == 1))
                last.then_inc(S["valued"], 1)

            def turn_heads(b):
                wait(pe, S["ro_done"], b + 1)
                wait(pe, S["nm_done"], min(b + 2, NB) if isinstance(b, int) else b + 2)
                wait(pe, S["unit_done"], 3 * min(b + 3, NB) if isinstance(b, int) else 3 * (b + 3))
                wait(pe, S["ht_done"], b)
                for a in range(2):
                    for t in range(2):
                        last = pe.transpose(m1[0:C, a * PIX + t * P:a * PIX + (t + 1) * P],
                                            ro[:, t, a * C:(a + 1) * C], ident[:, :])
                last.then_inc(S["ht_in"], 1)

            def mix_heads(b):
                wait(pe, S["ht_done"], b + 1)
                wait(pe, S["v_done"], min(b + 3, NB) if isinstance(b, int) else b + 3)
                wait(pe, S["wo_done"], b)
                for a in range(2):
                    last = pe.matmul(m2[0:DS, 0:PIX], wp[:, a, :], rt[:, a, :], start=(a == 0), stop=(a == 1))
                last.then_inc(S["wp_in"], 1)

            def mix_out(b):
                wait(pe, S["wp_done"], b + 1)
                for t in range(2):
                    last = pe.matmul(m2[:, t * C:(t + 1) * C], u[:, t * P:(t + 1) * P], wo[:, :], start=True,
                                     stop=True)
                last.then_inc(S["wo_in"], 1)

            def body(b, p):
                first, last = isinstance(b, int) and b == 0, is_last(b)
                if not last:
                    turn_tokens(b + 1)
                if not first:
                    values(b - 1, 1 - p, H - 1)
                turn_maxima(b)
                if not last:
                    unit(b + 1, 0)
                turned_scores(b, p, 0)
                if not last:
                    unit(b + 1, 1)
                turned_scores(b, p, 1)
                values(b, p, 0)
                if not last:
                    unit(b + 1, 2)
                turned_scores(b, p, 2)
                values(b, p, 1)
                if not last:
                    value_tokens(b + 1)
                if not first:
                    turn_heads(b - 1)
                turned_scores(b, p, 3)
                if not last:
                    scores(b + 1, 1 - p, 0)
                    scores(b + 1, 1 - p, 1)
                values(b, p, 2)
                if not first:
                    mix_heads(b - 1)
                turned_scores(b, p, 4)
                if not last:
                    scores(b + 1, 1 - p, 2)
                    scores(b + 1, 1 - p, 3)
                values(b, p, 3)
                if not first:
                    mix_out(b - 1)
                turned_scores(b, p, 5)
                if not last:
                    scores(b + 1, 1 - p, 4)
                    scores(b + 1, 1 - p, 5)
                values(b, p, 4)
                if not last:
                    residual(b + 1)

            turn_tokens(0)
            for n in range(3):
                unit(0, n)
            value_tokens(0)
            residual(0)
            for h in range(H):
                scores(0, 0, h)
            pe.wait_ge(S["ready"], 1)
            images(pe, body)
            values(NB - 1, 1, H - 1)
            turn_heads(NB - 1)
            mix_heads(NB - 1)
            mix_out(NB - 1)


NH2, HC2 = 12, 32
KSIDE = SIDE // 2
KPIX = KSIDE * KSIDE
QP = PIX // 4
KP = KPIX // 4
HG = P // HC2
N3 = NH2 // HG
PAD = SIDE + 2
L2_LN_EPS = 1e-5
L2_SCALE = HC2 ** -0.5


def l2_sample(nc, T, A, R):
    X, ident = T["X"], T["ident"]
    Q, K, V = R["Q"], R["K"], R["V"]
    TAPS = KS * KS
    with ExitStack() as ctx:
        s = Scope(nc, ctx, "l2s")
        taps, bias, lnp, woff, ref, coord = (T[f"l2_{n}"] for n in ("taps", "bias", "lnp", "woff", "ref", "coord"))
        diag = s.sb("diag", [C, 3, TAPS, C])
        xn = s.sb("xn", [P, 2, C])
        xp = s.sb("xp", [C, 2, PAD, PAD])
        val = s.sb("val", [C, PIX])
        off = s.sb("off", [C, P])
        on = s.sb("on", [P, C])
        og = s.sb("og", [C, KPIX])
        pos = s.sb("pos", [P, 2, KPIX])
        th = s.sb("th", [P, 2, KPIX])
        dist = s.sb("dist", [P, 3, KPIX])
        hat = s.sb("hat", [P, 3, KPIX])
        bil = s.sb("bil", [P, 2, KPIX])
        vt = s.sb("vt", [P, 2, C])
        stats = s.sb("stats", [P, 2, 6])
        mean = s.sb("mean", [P, 2])
        var = s.sb("var", [P, 2])
        rstd = s.sb("rstd", [P, 2])
        ostats = s.sb("ostats", [P, 1, 6])
        omean = s.sb("omean", [P, 1])
        ovar = s.sb("ovar", [P, 1])
        orstd = s.sb("orstd", [P, 1])
        mhalf = s.sb("mhalf", [P, 2])
        tp, qp, kp, op, fp, gp, vp, sp_ = (s.psum(n, [P, 512]) for n in
                                           ("tp", "qp", "kp", "op", "fp", "gp", "vp", "sp"))
        names = ("consts", "diag_done", "var_done", "rstd_done", "ovar_done", "orstd_done", "dve_step",
                 "xn_done", "turned", "xp_done", "q_in", "q_out", "k_in", "k_out", "off_in", "off_out",
                 "on_in", "on_done", "og_in", "og_out", "pos_in", "pos_out", "th_done", "dist_done", "hat_done",
                 "bil_done", "val_done", "vt_in", "vt_out", "smp_in", "smp_out")
        S = {n: s.sem(n) for n in names}
        block = ctx.enter_context(nc.Block())
        @block.gpsimd
        def _(pool):
            pool.memset(xp[:, :, :, :], 0.0)
            pool.memset(off[:, :], 0.0)
            pool.memset(on[:, :], 0.0)
            pool.memset(mhalf[:, :], -0.5).then_inc(S["consts"], 1)
            pool.wait_ge(S["consts"], 1)

            def tokens_rstd(b):
                wait(pool, S["var_done"], b + 1)
                pool.tensor_tensor(rstd[:, :], var[:, :], mhalf[:, :], ALU.pow).then_inc(S["rstd_done"], 1)

            def offsets_rstd(b):
                wait(pool, S["ovar_done"], b + 1)
                pool.tensor_tensor(orstd[0:KPIX, :], ovar[0:KPIX, :], mhalf[0:KPIX, 0:1], ALU.pow
                                   ).then_inc(S["orstd_done"], 1)

            tokens_rstd(0)
            with pool.Fori(0, NI - 1) as b:
                offsets_rstd(b)
                tokens_rstd(b + 1)
            offsets_rstd(NI - 1)

        STATS, APPLY, TAPS_A, TAPS_B = 4, 2, 5, 3
        EACH = TAPS_A + STATS + TAPS_B + APPLY

        def images(eng, body):
            body(0, 0, False)
            body(1, 1, False)
            body(2, 0, False)
            with eng.Fori(1, NI // 2 - 1) as i:
                body(2 * i + 1, 1, False)
                body(2 * i + 2, 0, False)
            body(NI - 1, 1, True)

        @block.vector
        def _(dve):
            def ln_stats(b, chain):
                layernorm_stats(dve, chain, [X[:, 2 * b + t, :] for t in range(2)], stats, mean, var, 1e-6)
                dve.sem_inc(S["var_done"], 1)

            def ln_apply(b, chain):
                wait(dve, S["rstd_done"], b + 1)
                wait(dve, S["turned"], b)
                layernorm_apply(dve, chain, [X[:, 2 * b + t, :] for t in range(2)], [xn[:, t, :] for t in range(2)],
                                stats, mean, rstd).then_inc(S["xn_done"], 1)

            def bilinear(b):
                wait(dve, S["hat_done"], b + 1)
                wait(dve, S["smp_in"], b)
                dve.tensor_tensor(bil[:, :, :], hat[:, 1:3, :],
                                  hat[:, 0, :].unsqueeze(1).broadcast_to([P, 2, KPIX]), ALU.mult
                                  ).then_inc(S["bil_done"], 1)

            def values_out(b):
                wait(dve, S["vt_in"], b + 1)
                wait(dve, S["smp_in"], b)
                dve.tensor_scalar(vt[:, :, :].rearrange("p t c -> p (t c)"), vp[:, 0:2 * C], 1.0, None, ALU.mult
                                  ).then_inc(S["vt_out"], 1)

            def body(b, p, last):
                chain = Chain(dve, S["dve_step"], STATS + APPLY + b * (STATS + APPLY + EACH))
                wait(dve, S["xp_done"], b + 1)
                wait(dve, S["vt_in"], b)
                v3 = val[:, :].rearrange("c (y x) -> c y x", x=SIDE)
                for t in range(TAPS):
                    image = xp[:, p, t // KS:t // KS + SIDE, t % KS:t % KS + SIDE]
                    if t == 0:
                        ins = dve.tensor_scalar(v3, image, taps[:, 3, 0:1], bias[:, 3:4], ALU.mult, ALU.add)
                    else:
                        ins = dve.scalar_tensor_tensor(out=v3, in0=image, scalar=taps[:, 3, t:t + 1], in1=v3,
                                                       op0=ALU.mult, op1=ALU.add)
                    if t < TAPS - 1:
                        chain.sync(ins)
                    if t == TAPS_A - 1:
                        if not (isinstance(b, int) and b == 0):
                            values_out(b - 1)
                            bilinear(b - 1)
                        wait(dve, S["on_in"], b + 1)
                        layernorm_stats(dve, chain, [fp[0:KPIX, 0:C]], ostats, omean, ovar, L2_LN_EPS, KPIX)
                        dve.sem_inc(S["ovar_done"], 1)
                        if not last:
                            ln_stats(b + 1, chain)
                        wait(dve, S["orstd_done"], b + 1)
                        layernorm_apply(dve, chain, [fp[0:KPIX, 0:C]], [on[0:KPIX, :]], ostats, omean, orstd, KPIX
                                        ).then_inc(S["on_done"], 1)
                        if not last:
                            ln_apply(b + 1, chain)
                ins.then_inc(S["val_done"], 1)
                wait(dve, S["pos_in"], b + 1)
                dve.tensor_tensor(pos[:, :, :], gp[:, 0:2 * KPIX].rearrange("p (a n) -> p a n", a=2), ref[:, :, :],
                                  ALU.add).then_inc(S["pos_out"], 1)
                assert chain.n == EACH + (0 if last else STATS + APPLY) - 0, chain.n

            dve.wait_ge(S["consts"], 1)
            chain = Chain(dve, S["dve_step"])
            ln_stats(0, chain)
            ln_apply(0, chain)
            for w in range(3):
                for t in range(TAPS):
                    ins = dve.tensor_scalar(diag[:, w, t, :], ident[0:C, 0:C], taps[:, w, t:t + 1], None, ALU.mult)
            ins.then_inc(S["diag_done"], 1)
            images(dve, body)
            values_out(NI - 1)
            bilinear(NI - 1)

        @block.scalar
        def _(act):
            def tokens_out(b, p):
                wait(act, S["turned"], b + 1)
                wait(act, S["k_in"], b - 1)
                wait(act, S["val_done"], b - 1)
                act.activation(xp[:, p, 1:SIDE + 1, 1:SIDE + 1],
                               tp[0:C, 0:PIX].rearrange("c (y x) -> c y x", x=SIDE), ACT.Copy
                               ).then_inc(S["xp_done"], 1)

            def sampled_out(b):
                wait(act, S["smp_in"], b + 1)
                act.activation(V[:, b, :], sp_[0:C, 0:KPIX], ACT.Copy).then_inc(S["smp_out"], 1)

            def body(b, p, last):
                wait(act, S["off_in"], b + 1)
                act.activation(off[:, 0:KPIX], op[0:C, 0:KPIX], ACT.Identity, bias=bias[:, 2:3]
                               ).then_inc(S["off_out"], 1)
                wait(act, S["k_in"], b + 1)
                act.activation(K[:, b, :], kp[0:C, 0:KPIX], ACT.Identity, bias=bias[:, 1:2]
                               ).then_inc(S["k_out"], 1)
                if not (isinstance(b, int) and b == 0):
                    sampled_out(b - 1)
                wait(act, S["q_in"], b + 1)
                act.activation(Q[:, b, :], qp[0:C, 0:PIX], ACT.Identity, bias=bias[:, 0:1]
                               ).then_inc(S["q_out"], 1)
                wait(act, S["og_in"], b + 1)
                act.activation(og[:, :], fp[0:C, 0:KPIX], ACT.Gelu, scale=lnp[:, 0:1], bias=lnp[:, 1:2]
                               ).then_inc(S["og_out"], 1)
                if not last:
                    tokens_out(b + 1, 1 - p)
                wait(act, S["pos_out"], b + 1)
                act.activation(th[:, :, :], pos[:, :, :], ACT.Tanh).then_inc(S["th_done"], 1)
                wait(act, S["th_done"], b + 1)
                for k, comp in enumerate((0, 1, 1)):
                    ins = act.activation(dist[:, k, :], th[:, comp, :], ACT.Abs, scale=(SIDE - 1) / 2,
                                         bias=coord[:, k:k + 1])
                ins.then_inc(S["dist_done"], 1)
                wait(act, S["dist_done"], b + 1)
                wait(act, S["bil_done"], b)
                act.activation(hat[:, :, :], dist[:, :, :], ACT.Relu, scale=-1.0, bias=1.0
                               ).then_inc(S["hat_done"], 1)

            act.wait_ge(S["consts"], 1)
            tokens_out(0, 0)
            images(act, body)
            sampled_out(NI - 1)

        @block.tensor
        def _(pe):
            def turn(b):
                wait(pe, S["xn_done"], b + 1)
                wait(pe, S["xp_done"], b)
                for t in range(2):
                    ins = pe.transpose(tp[0:C, t * P:(t + 1) * P], xn[:, t, :], ident[:, :])
                ins.then_inc(S["turned"], 1)

            def conv(out, w, p, stride, done):
                side = SIDE // stride
                o = out[0:C, 0:side * side].rearrange("c (y x) -> c y x", x=side)
                for t in range(TAPS):
                    dy, dx = t // KS, t % KS
                    ins = pe.matmul(o, diag[:, w, t, :], xp[:, p, dy:dy + SIDE:stride, dx:dx + SIDE:stride],
                                    start=(t == 0), stop=(t == TAPS - 1))
                ins.then_inc(done, 1)

            def sample(b):
                wait(pe, S["vt_out"], b + 1)
                wait(pe, S["bil_done"], b + 1)
                wait(pe, S["smp_out"], b)
                for t in range(2):
                    ins = pe.matmul(sp_[0:C, 0:KPIX], vt[:, t, :], bil[:, t, :], start=(t == 0), stop=(t == 1))
                ins.then_inc(S["smp_in"], 1)

            def turn_values(b):
                wait(pe, S["val_done"], b + 1)
                wait(pe, S["vt_out"], b)
                for t in range(2):
                    ins = pe.transpose(vp[:, t * C:(t + 1) * C], val[:, t * P:(t + 1) * P], ident[0:C, 0:C])
                ins.then_inc(S["vt_in"], 1)

            def body(b, p, last):
                if not (isinstance(b, int) and b == 0):
                    turn_values(b - 1)
                wait(pe, S["xp_done"], b + 1)
                wait(pe, S["off_out"], b)
                conv(op, 2, p, 2, S["off_in"])
                wait(pe, S["k_out"], b)
                conv(kp, 1, p, 2, S["k_in"])
                wait(pe, S["off_out"], b + 1)
                pe.transpose(fp[:, 0:C], off[:, :], ident[0:C, 0:C]).then_inc(S["on_in"], 1)
                if not (isinstance(b, int) and b == 0):
                    sample(b - 1)
                wait(pe, S["q_out"], b)
                conv(qp, 0, p, 1, S["q_in"])
                wait(pe, S["on_done"], b + 1)
                pe.transpose(fp[0:C, 0:P], on[:, :], ident[:, :]).then_inc(S["og_in"], 1)
                if not last:
                    turn(b + 1)
                wait(pe, S["og_out"], b + 1)
                wait(pe, S["pos_out"], b)
                for k in range(2):
                    ins = pe.matmul(gp[:, k * KPIX:(k + 1) * KPIX], woff[:, k, :], og[:, :], start=True, stop=True)
                ins.then_inc(S["pos_in"], 1)

            turn(0)
            pe.wait_ge(S["diag_done"], 1)
            images(pe, body)
            turn_values(NI - 1)
            sample(NI - 1)


def l2_mix(nc, T, A, R):
    X, ident = T["X"], T["ident"]
    Q, K, V = R["Q"], R["K"], R["V"]
    with ExitStack() as ctx:
        s = Scope(nc, ctx, "l2m")
        mask, wout = T["l2_mask"], T["l2_wout"]
        qr = s.sb("qr", [P, NI, N3, QP])
        kr = s.sb("kr", [P, NI, N3, KP])
        vr = s.sb("vr", [P, NI, N3, KP])
        orow = s.sb("orow", [P, NI, N3, QP])
        oc = s.sb("oc", [C, NI, PIX])
        kb = s.sb("kb", [P, 2, N3, HG, KP])
        vb = s.sb("vb", [P, 2, N3, HG, KP])
        vbt = s.sb("vbt", [HG * KP, 2, N3 * P])
        at = s.sb("at", [HG * KP, 2, N3 * QP])
        vp = [s.psum(f"vp{i}", [P, 512]) for i in range(2)]
        ap_ = [s.psum(f"ap{i}", [P, 512]) for i in range(2)]
        op = [s.psum(f"op{i}", [P, 512]) for i in range(2)]
        yp = [s.psum(f"yp{i}", [P, 512]) for i in range(2)]
        names = ("moved_dve", "moved_act", "moved_pool", "kb_done", "vb_done", "vbt_in", "vbt_out",
                 "at_in", "at_out", "o_in", "o_out", "back_dve", "back_act", "y_in", "y_out")
        S = {n: s.sem(n) for n in names}
        block = ctx.enter_context(nc.Block())
        PARTS = [(g, j) for g in range(N3) for j in range(4)]

        def rows(t, g, j, n):
            return t[HC2 * j:HC2 * (j + 1), :, g, 0:n]

        def chans(t, g, j, n):
            return t[HC2 * g:HC2 * (g + 1), :, n * j:n * (j + 1)]

        @block.gpsimd
        def _(pool):
            for g, j in PARTS:
                ins = pool.tensor_copy(rows(vr, g, j, KP), chans(V, g, j, KP))
            ins.then_inc(S["moved_pool"], 1)

        @block.vector
        def _(dve):
            for g, j in PARTS:
                dve.tensor_copy(rows(kr, g, j, KP), chans(K, g, j, KP))
            for g, j in PARTS[0:6]:
                ins = dve.tensor_copy(rows(qr, g, j, QP), chans(Q, g, j, QP))
            ins.then_inc(S["moved_dve"], 1)
            dve.wait_ge(S["moved_dve"], 1)
            dve.wait_ge(S["moved_pool"], 1)

            def block_diagonal(out, rows_, b, done):
                dve.tensor_tensor(out, rows_[:, b, :, :].unsqueeze(2).broadcast_to([P, N3, HG, KP]),
                                  mask[:, :].unsqueeze(1).unsqueeze(3).broadcast_to([P, N3, HG, KP]), ALU.mult
                                  ).then_inc(done, 1)

            def body(b, p):
                wait(dve, S["vbt_in"], b - 1)
                block_diagonal(vb[:, p, :, :, :], vr, b, S["vb_done"])
                wait(dve, S["at_in"], b - 1)
                block_diagonal(kb[:, p, :, :, :], kr, b, S["kb_done"])
                wait(dve, S["vbt_in"], b + 1)
                wait(dve, S["o_in"], b - 1)
                dve.tensor_scalar(vbt[:, p, :], vp[p][0:HG * KP, 0:N3 * P], L2_SCALE, None, ALU.mult
                                  ).then_inc(S["vbt_out"], 1)

            body(0, 0)
            body(1, 1)
            with dve.Fori(1, NI // 2) as i:
                body(2 * i, 0)
                body(2 * i + 1, 1)
            dve.wait_ge(S["o_out"], NI)
            for g, j in PARTS[0:7]:
                ins = dve.tensor_copy(chans(oc, g, j, QP), rows(orow, g, j, QP))
            ins.then_inc(S["back_dve"], 1)
            for n in range(NT // GT):
                dve.wait_ge(S["y_in"], n + 1)
                x = X[:, GT * n:GT * (n + 1), :].rearrange("p t c -> p (t c)")
                dve.tensor_tensor(x, yp[n % 2][:, 0:GT * C], x, ALU.add).then_inc(S["y_out"], 1)

        @block.scalar
        def _(act):
            for g, j in PARTS[6:]:
                ins = act.activation(rows(qr, g, j, QP), chans(Q, g, j, QP), ACT.Copy)
            ins.then_inc(S["moved_act"], 1)

            def body(b, p):
                wait(act, S["at_in"], b + 1)
                wait(act, S["o_in"], b - 1)
                act.activation(at[:, p, :], ap_[p][0:HG * KP, 0:N3 * QP], ACT.Copy).then_inc(S["at_out"], 1)
                wait(act, S["o_in"], b + 1)
                act.activation(orow[:, b, :, :], op[p][:, 0:N3 * QP].rearrange("p (g m) -> p g m", g=N3), ACT.Copy
                               ).then_inc(S["o_out"], 1)

            body(0, 0)
            body(1, 1)
            with act.Fori(1, NI // 2) as i:
                body(2 * i, 0)
                body(2 * i + 1, 1)
            act.wait_ge(S["o_out"], NI)
            for g, j in PARTS[7:]:
                ins = act.activation(chans(oc, g, j, QP), rows(orow, g, j, QP), ACT.Copy)
            ins.then_inc(S["back_act"], 1)

        @block.tensor
        def _(pe):
            pe.wait_ge(S["moved_act"], 1)
            pe.wait_ge(S["moved_dve"], 1)

            def body(b, p):
                wait(pe, S["vb_done"], b + 1)
                wait(pe, S["vbt_out"], b - 1)
                wait(pe, S["kb_done"], b + 1)
                wait(pe, S["at_out"], b - 1)
                for g in range(N3):
                    ins = pe.matmul(ap_[p][0:HG * KP, g * QP:(g + 1) * QP],
                                    kb[:, p, g, :, :].rearrange("p h n -> p (h n)"), qr[:, b, g, :],
                                    start=True, stop=True)
                ins.then_inc(S["at_in"], 1)
                for g in range(N3):
                    ins = pe.transpose(vp[p][0:HG * KP, g * P:(g + 1) * P],
                                       vb[:, p, g, :, :].rearrange("p h n -> p (h n)"), ident[:, :])
                ins.then_inc(S["vbt_in"], 1)
                wait(pe, S["at_out"], b + 1)
                wait(pe, S["vbt_out"], b + 1)
                wait(pe, S["o_out"], b - 1)
                for g in range(N3):
                    ins = pe.matmul(op[p][:, g * QP:(g + 1) * QP], vbt[:, p, g * P:(g + 1) * P],
                                    at[:, p, g * QP:(g + 1) * QP], start=True, stop=True)
                ins.then_inc(S["o_in"], 1)

            body(0, 0)
            body(1, 1)
            with pe.Fori(1, NI // 2) as i:
                body(2 * i, 0)
                body(2 * i + 1, 1)
            pe.wait_ge(S["back_dve"], 1)
            pe.wait_ge(S["back_act"], 1)
            flat = oc[:, :, :].rearrange("c b n -> c (b n)")
            for n in range(NT // GT):
                wait(pe, S["y_out"], n - 1)
                for j in range(GT):
                    t = GT * n + j
                    ins = pe.matmul(yp[n % 2][:, j * C:(j + 1) * C], flat[:, t * P:(t + 1) * P], wout[:, :],
                                    start=True, stop=True)
                ins.then_inc(S["y_in"], 1)


def l2_conv(nc, T, A):
    with ExitStack() as ctx:
        s = Scope(nc, ctx, "l2")
        R = {"Q": s.sb("Q", [C, NI, PIX]), "K": s.sb("K", [C, NI, KPIX]), "V": s.sb("V", [C, NI, KPIX])}
        l2_sample(nc, T, A, R)
        l2_mix(nc, T, A, R)


L3H, L3D = 8, 16
INNER = L3H * L3D
L3_SCALE = L3D ** -0.5
QG = 5
GI = NI // QG
TG = GI * PIX // P
QB, Q_EPS = 128.0, 1e-5


def l3_conv(nc, T, A):
    X, ident = T["X"], T["ident"]
    TAPS = KS * KS
    VW = INNER + INNER + C
    with ExitStack() as ctx:
        s = Scope(nc, ctx, "l3c")
        taps, bn, wq, wkv, wvt, wo, bo, mask = (T[f"l3_{n}"] for n in
                                                ("taps", "bn", "wq", "wkv", "wvt", "wo", "bo", "mask"))
        inv = s.sb("inv", [C, 2])
        shift = s.sb("shift", [C, 2])
        diag = s.sb("diag", [C, TAPS, C])
        ones = s.sb("ones", [P, P])
        xn = s.sb("xn", [P, 2, C])
        xp = s.sb("xp", [C, 2, PAD, PAD])
        yq = s.sb("yq", [C, PIX])
        ykv = s.sb("ykv", [C, PIX])
        q = s.sb("q", [INNER, PIX])
        kv = s.sb("kv", [P, 2, 2 * INNER])
        prod = s.sb("prod", [P, 2, INNER])
        dsum = s.sb("dsum", [P, NI, 2, L3H])
        dtot = s.sb("dtot", [P, 1])
        m0 = s.sb("m0", [P, 1])
        ktv = s.sb("ktv", [INNER, INNER])
        z = s.sb("z", [P, 2, INNER])
        zt = s.sb("zt", [INNER, 2, P])
        vw = s.sb("vw", [P, NT, C])
        stats = s.sb("stats", [P, 2, 6])
        mean = s.sb("mean", [P, 2])
        var = s.sb("var", [P, 2])
        rstd = s.sb("rstd", [P, 2])
        mhalf = s.sb("mhalf", [P, 2])
        tp, qp, cp, kv0, kv1, pp, zp, yp = (s.psum(n, [P, 512]) for n in
                                            ("tp", "qp", "cp", "kv0", "kv1", "pp", "zp", "yp"))
        names = ("consts", "v_eps", "bn_pow", "vw_in", "vw_out", "diag_done", "var_done", "rstd_done",
                 "dve_step", "xn_done", "turned", "xp_done", "yq_in", "yq_out", "ykv_done", "q_in", "q_out",
                 "qt_in", "qt_out", "kv_in", "kv_out", "ktv_in", "ktv_out", "qkv_in", "z_out", "zt_in", "zt_out",
                 "y_in", "y_out", "tot_done", "m0_in")
        S = {n: s.sem(n) for n in names}
        block = ctx.enter_context(nc.Block())

        def images(eng, body):
            body(0, 0, False)
            body(1, 1, False)
            body(2, 0, False)
            with eng.Fori(1, NI // 2 - 1) as i:
                body(2 * i + 1, 1, False)
                body(2 * i + 2, 0, False)
            body(NI - 1, 1, True)

        @block.gpsimd
        def _(pool):
            pool.memset(xp[:, :, :, :], 0.0)
            pool.memset(ones[:, :], 1.0)
            pool.memset(mhalf[:, :], -0.5).then_inc(S["consts"], 1)
            pool.wait_ge(S["consts"], 1)
            pool.wait_ge(S["v_eps"], 1)
            pool.tensor_tensor(inv[:, :], shift[:, :], mhalf[0:C, :], ALU.pow).then_inc(S["bn_pow"], 1)
            with pool.Fori(0, NI) as b:
                pool.wait_ge(S["var_done"], b + 1)
                pool.tensor_tensor(rstd[:, :], var[:, :], mhalf[:, :], ALU.pow).then_inc(S["rstd_done"], 1)

        LAST = 3
        EACH = LAST + 6 + TAPS - 1

        @block.vector
        def _(dve):
            def ln_stats(b, chain):
                layernorm_stats(dve, chain, [X[:, 2 * b + t, :] for t in range(2)], stats, mean, var, 1e-6)
                dve.sem_inc(S["var_done"], 1)

            def ln_apply(b, chain):
                wait(dve, S["rstd_done"], b + 1)
                wait(dve, S["turned"], b)
                layernorm_apply(dve, chain, [X[:, 2 * b + t, :] for t in range(2)], [xn[:, t, :] for t in range(2)],
                                stats, mean, rstd).then_inc(S["xn_done"], 1)

            def output(b):
                wait(dve, S["y_in"], b + 1)
                x = X[:, bass.ds(2 * b, 2), :].rearrange("p t c -> p (t c)")
                dve.tensor_tensor(x, yp[:, 0:2 * C], x, ALU.add).then_inc(S["y_out"], 1)

            def conv_kv(b, p, chain):
                wait(dve, S["xp_done"], b + 1)
                wait(dve, S["kv_in"], b)
                y3 = ykv[:, :].rearrange("c (y x) -> c y x", x=SIDE)
                for t in range(TAPS):
                    image = xp[:, p, t // KS:t // KS + SIDE, t % KS:t % KS + SIDE]
                    if t == 0:
                        ins = dve.tensor_scalar(y3, image, taps[:, 1, 0:1], shift[:, 1:2], ALU.mult, ALU.add)
                    else:
                        ins = dve.scalar_tensor_tensor(out=y3, in0=image, scalar=taps[:, 1, t:t + 1], in1=y3,
                                                       op0=ALU.mult, op1=ALU.add)
                    if t < TAPS - 1:
                        chain.sync(ins)
                ins.then_inc(S["ykv_done"], 1)

            def body(b, p, last):
                chain = Chain(dve, S["dve_step"], base + b * EACH)
                if not last:
                    ln_stats(b + 1, chain)
                    ln_apply(b + 1, chain)
                wait(dve, S["qt_in"], b + 1)
                wait(dve, S["kv_out"], b + 1)
                chain.sync(dve.tensor_tensor(prod[:, :, :], qp[:, 0:2 * INNER].rearrange("p (t c) -> p t c", t=2),
                                             kv[:, :, 0:INNER], ALU.mult))
                dve.sem_inc(S["qt_out"], 1)
                d = dsum[:, b, :, :].rearrange("p t h -> p (t h)")
                chain.sync(dve.tensor_reduce(d, prod[:, :, :].rearrange("p t (h d) -> p (t h) d", d=L3D), AX.X,
                                             ALU.add))
                wait(dve, S["ktv_in"], b + 1)
                dve.tensor_tensor(ktv[:, :].rearrange("p (h d) -> p h d", d=L3D),
                                  pp[:, 0:INNER].rearrange("p (h d) -> p h d", d=L3D),
                                  mask[:, :].unsqueeze(2).broadcast_to([INNER, L3H, L3D]), ALU.mult
                                  ).then_inc(S["ktv_out"], 1)
                chain.sync(dve.tensor_tensor(prod[:, :, :].rearrange("p t (h d) -> p (t h) d", d=L3D),
                                             kv[:, :, INNER:2 * INNER].rearrange("p t (h d) -> p t h d", d=L3D),
                                             d.unsqueeze(2).broadcast_to([P, 2 * L3H, L3D]), ALU.mult))
                if not last:
                    conv_kv(b + 1, 1 - p, chain)
                if not (isinstance(b, int) and b == 0):
                    output(b - 1)
                wait(dve, S["qkv_in"], b + 1)
                wait(dve, S["zt_in"], b)
                dve.tensor_tensor(z[:, :, :].rearrange("p t c -> p (t c)"), pp[:, INNER:3 * INNER],
                                  prod[:, :, :].rearrange("p t c -> p (t c)"), ALU.subtract).then_inc(S["z_out"], 1)
                assert chain.n == (LAST if last else EACH), chain.n

            chain = Chain(dve, S["dve_step"])
            chain.sync(dve.tensor_scalar(shift[:, :], bn[:, 3, :], BN_EPS, None, ALU.add))
            dve.sem_inc(S["v_eps"], 1)
            ln_stats(0, chain)
            dve.wait_ge(S["bn_pow"], 1)
            chain.sync(dve.tensor_tensor(inv[:, :], inv[:, :], bn[:, 0, :], ALU.mult))
            chain.sync(dve.tensor_tensor(shift[:, :], bn[:, 2, :], inv[:, :], ALU.mult))
            dve.tensor_tensor(shift[:, :], bn[:, 1, :], shift[:, :], ALU.subtract)
            chain.sync(dve.tensor_tensor(taps[:, :, :], taps[:, :, :], inv[:, :].unsqueeze(2)
                                         .broadcast_to([C, 2, TAPS]), ALU.mult))
            ln_apply(0, chain)
            for t in range(TAPS):
                ins = dve.tensor_scalar(diag[:, t, :], ident[0:C, 0:C], taps[:, 0, t:t + 1], None, ALU.mult)
            ins.then_inc(S["diag_done"], 1)
            dve.wait_ge(S["vw_in"], 1)
            dve.tensor_copy(wkv[:, 2 * INNER:VW], pp[0:C, 0:C]).then_inc(S["vw_out"], 1)
            conv_kv(0, 0, chain)
            base = chain.n
            images(dve, body)
            output(NI - 1)
            dve.tensor_reduce(dtot[:, :], dsum[:, :, :, :].rearrange("p b t h -> p (b t h)"), AX.X, ALU.add
                              ).then_inc(S["tot_done"], 1)
            dve.wait_ge(S["y_out"], NI)
            last = Chain(dve, S["dve_step"], base + (NI - 1) * EACH + LAST)
            last.sync(dve.tensor_tensor(X[:, :, :], X[:, :, :], bo[:, :].unsqueeze(1).broadcast_to([P, NT, C]),
                                        ALU.add))
            dve.wait_ge(S["m0_in"], 1)
            last.sync(dve.tensor_scalar(m0[:, :], pp[:, 0:1], L3_SCALE, None, ALU.mult))
            dve.scalar_tensor_tensor(out=X[:, :, :].rearrange("p t c -> p (t c)"),
                                     in0=vw[:, :, :].rearrange("p t c -> p (t c)"), scalar=m0[:, 0:1],
                                     in1=X[:, :, :].rearrange("p t c -> p (t c)"), op0=ALU.mult, op1=ALU.add)

        @block.scalar
        def _(act):
            def tokens_out(b, p):
                wait(act, S["turned"], b + 1)
                wait(act, S["yq_in"], b - 1)
                wait(act, S["ykv_done"], b - 1)
                act.activation(xp[:, p, 1:SIDE + 1, 1:SIDE + 1],
                               tp[0:C, 0:PIX].rearrange("c (y x) -> c y x", x=SIDE), ACT.Copy
                               ).then_inc(S["xp_done"], 1)

            def queries_out(b):
                wait(act, S["yq_in"], b + 1)
                act.activation(yq[:, :], cp[0:C, 0:PIX], ACT.Identity, bias=shift[:, 0:1]).then_inc(S["yq_out"], 1)
                wait(act, S["q_in"], b + 1)
                act.activation(q[:, :], tp[:, 0:PIX], ACT.Copy).then_inc(S["q_out"], 1)

            def kv_out(b):
                wait(act, S["kv_in"], b + 1)
                wait(act, S["z_out"], b)
                for t, bank in enumerate((kv0, kv1)):
                    act.activation(kv[:, t, :], bank[:, 0:2 * INNER], ACT.Copy)
                for t, bank in enumerate((kv0, kv1)):
                    ins = act.activation(vw[:, 2 * b + t, :], bank[:, 2 * INNER:VW], ACT.Copy)
                ins.then_inc(S["kv_out"], 1)

            def z_turned(b):
                wait(act, S["zt_in"], b + 1)
                act.activation(zt[:, :, :].rearrange("p t n -> p (t n)"), zp[:, 0:2 * P], ACT.Copy, scale=L3_SCALE
                               ).then_inc(S["zt_out"], 1)

            def body(b, p, last):
                kv_out(b)
                if not last:
                    tokens_out(b + 1, 1 - p)
                if not (isinstance(b, int) and b == 0):
                    z_turned(b - 1)
                if not last:
                    queries_out(b + 1)

            act.wait_ge(S["vw_out"], 1)
            tokens_out(0, 0)
            queries_out(0)
            images(act, body)
            z_turned(NI - 1)

        @block.tensor
        def _(pe):
            def turn(b):
                wait(pe, S["xn_done"], b + 1)
                wait(pe, S["q_out"], b)
                for t in range(2):
                    ins = pe.transpose(tp[0:C, t * P:(t + 1) * P], xn[:, t, :], ident[:, :])
                ins.then_inc(S["turned"], 1)

            def conv_q(b, p):
                wait(pe, S["xp_done"], b + 1)
                wait(pe, S["yq_out"], b)
                o = cp[0:C, 0:PIX].rearrange("c (y x) -> c y x", x=SIDE)
                for t in range(TAPS):
                    dy, dx = t // KS, t % KS
                    ins = pe.matmul(o, diag[:, t, :], xp[:, p, dy:dy + SIDE, dx:dx + SIDE],
                                    start=(t == 0), stop=(t == TAPS - 1))
                ins.then_inc(S["yq_in"], 1)

            def queries(b):
                wait(pe, S["yq_out"], b + 1)
                pe.matmul(tp[:, 0:PIX], wq[:, :], yq[:, :], start=True, stop=True).then_inc(S["q_in"], 1)
                wait(pe, S["qt_out"], b)
                for t in range(2):
                    ins = pe.matmul(qp[:, t * INNER:(t + 1) * INNER], yq[:, t * P:(t + 1) * P], wq[:, :],
                                    start=True, stop=True)
                ins.then_inc(S["qt_in"], 1)

            def keys_values(b):
                wait(pe, S["ykv_done"], b + 1)
                wait(pe, S["kv_out"], b)
                for t, bank in enumerate((kv0, kv1)):
                    ins = pe.matmul(bank[:, 0:VW], ykv[:, t * P:(t + 1) * P], wkv[:, :], start=True, stop=True)
                ins.then_inc(S["kv_in"], 1)

            def keys_by_values(b):
                wait(pe, S["kv_out"], b + 1)
                wait(pe, S["z_out"], b)
                for t in range(2):
                    ins = pe.matmul(pp[:, 0:INNER], kv[:, t, 0:INNER], kv[:, t, INNER:2 * INNER],
                                    start=(t == 0), stop=(t == 1))
                ins.then_inc(S["ktv_in"], 1)

            def queries_by_ktv(b):
                wait(pe, S["ktv_out"], b + 1)
                wait(pe, S["q_out"], b + 1)
                for t in range(2):
                    ins = pe.matmul(pp[:, (t + 1) * INNER:(t + 2) * INNER], q[:, t * P:(t + 1) * P], ktv[:, :],
                                    start=True, stop=True)
                ins.then_inc(S["qkv_in"], 1)

            def turn_z(b):
                wait(pe, S["z_out"], b + 1)
                wait(pe, S["zt_out"], b)
                for t in range(2):
                    ins = pe.transpose(zp[:, t * P:(t + 1) * P], z[:, t, :], ident[:, :])
                ins.then_inc(S["zt_in"], 1)

            def project(b):
                wait(pe, S["zt_out"], b + 1)
                wait(pe, S["y_out"], b)
                for t in range(2):
                    ins = pe.matmul(yp[:, t * C:(t + 1) * C], zt[:, t, :], wo[:, :], start=True, stop=True)
                ins.then_inc(S["y_in"], 1)

            def body(b, p, last):
                first = isinstance(b, int) and b == 0
                keys_values(b)
                if not last:
                    turn(b + 1)
                if not first:
                    turn_z(b - 1)
                keys_by_values(b)
                if not last:
                    conv_q(b + 1, 1 - p)
                if not first:
                    project(b - 1)
                queries_by_ktv(b)
                if not last:
                    queries(b + 1)

            pe.matmul(pp[0:C, 0:C], wvt[:, :], wo[:, :], start=True, stop=True).then_inc(S["vw_in"], 1)
            turn(0)
            pe.wait_ge(S["diag_done"], 1)
            pe.wait_ge(S["vw_out"], 1)
            conv_q(0, 0)
            queries(0)
            images(pe, body)
            turn_z(NI - 1)
            project(NI - 1)
            pe.wait_ge(S["tot_done"], 1)
            pe.wait_ge(S["consts"], 1)
            pe.matmul(pp[:, 0:1], ones[:, :], dtot[:, :], start=True, stop=True).then_inc(S["m0_in"], 1)


def l3_ffn(nc, T, A, out):
    X, ident = T["X"], T["ident"]
    TOKS = TG * P
    MS = 2 * KC
    UPS = 3
    with ExitStack() as ctx:
        s = Scope(nc, ctx, "l3f")
        w1, w2, b2 = T["l3_w1"], T["l3_w2"], T["l3_b2"]
        inv_qb = s.sb("inv_qb", [1, P])
        xn = s.sb("xn", [P, TG, C])
        xt = s.sb("xt", [CB, TOKS])
        hid = s.sb("hid", [P, KC, TOKS])
        y = s.sb("y", [P, TG, C])
        amax = s.sb("amax", [P, 2 * KC])
        bmax = s.sb("bmax", [P, 2])
        top = s.sb("top", [1, 2])
        gam = s.sb("gam", [P, 2])
        stats = s.sb("stats", [P, TG, 6])
        mean = s.sb("mean", [P, TG])
        var = s.sb("var", [P, TG])
        rstd = s.sb("rstd", [P, TG])
        mhalf = s.sb("mhalf", [P, TG])
        tp = [s.psum(f"tp{i}", [P, 512]) for i in range(2)]
        dn = [s.psum(f"dn{i}", [P, 512]) for i in range(2)]
        up = [s.psum(f"up{i}", [P, 512]) for i in range(UPS)]
        gp = s.psum("gp", [P, 512])
        names = ("consts", "var_done", "rstd_done", "dve_step",
                 "xn_done", "turned", "xt_done", "up_in", "up_max", "up_out", "max_done", "max_in", "top_done",
                 "top_in", "clipped", "hid_done", "down_in", "y_read", "y_done", "stored")
        S = {n: s.sem(n) for n in names}
        block = ctx.enter_context(nc.Block())
        LIM = float(np.float32(QB - Q_EPS))
        TB = TOKS - 512

        @block.sync
        def _(sp):
            with sp.Fori(0, QG) as g:
                sp.wait_ge(S["y_done"], g + 1)
                sp.dma_start(out[:, bass.ds(TG * g, TG), :], y[:, :, :]).then_inc(S["stored"], 16)
            sp.dma_start(out[:, TG * QG:NT, :], X[:, TG * QG:NT, :]).then_inc(S["stored"], 16)
            sp.wait_ge(S["stored"], 16 * (QG + 1))

        @block.gpsimd
        def _(pool):
            pool.memset(inv_qb[:, :], 1.0 / QB)
            pool.memset(mhalf[:, :], -0.5).then_inc(S["consts"], 1)
            pool.wait_ge(S["consts"], 1)
            with pool.Fori(0, QG) as g:
                pool.wait_ge(S["var_done"], g + 1)
                pool.tensor_tensor(rstd[:, :], var[:, :], mhalf[:, :], ALU.pow).then_inc(S["rstd_done"], 1)

        @block.vector
        def _(dve):
            LAST = 10
            EACH = LAST + 7

            def ln(g, chain):
                tiles = [X[:, TG * g + j, :] for j in range(TG)]
                layernorm_stats(dve, chain, tiles, stats, mean, var, 1e-5)
                dve.sem_inc(S["var_done"], 1)
                wait(dve, S["rstd_done"], g + 1)
                wait(dve, S["turned"], g)
                layernorm_apply(dve, chain, tiles, [xn[:, j, :] for j in range(TG)], stats, mean, rstd
                                ).then_inc(S["xn_done"], 1)

            def up_maxima(g, chain):
                for m in range(MS):
                    wait(dve, S["up_in"], MS * g + m + 1)
                    dve.tensor_reduce(amax[:, m:m + 1], up[m % UPS][:, 0:(512, TB)[m % 2]], AX.X, ALU.max,
                                      apply_absolute_value=True).then_inc(S["up_max"], 1)
                wait(dve, S["up_max"], MS * (g + 1))
                chain.sync(dve.tensor_reduce(bmax[:, 0:1], amax[:, :], AX.X, ALU.max))
                dve.sem_inc(S["max_done"], 1)

            def factor(g, chain, k):
                wait(dve, S["max_in"], 2 * g + k + 1)
                chain.sync(dve.tensor_reduce(top[:, k:k + 1], gp[0:1, 0:P], AX.X, ALU.max))
                dve.sem_inc(S["top_done"], 1)
                wait(dve, S["top_in"], 2 * g + k + 1)
                chain.sync(dve.tensor_scalar(gam[:, k:k + 1], gp[:, P:P + 1], Q_EPS / QB, None, ALU.add))
                chain.sync(dve.reciprocal(gam[:, k:k + 1], gam[:, k:k + 1]))

            def body(g, last):
                chain = Chain(dve, S["dve_step"], base + g * EACH)
                factor(g, chain, 0)
                wait(dve, S["up_out"], MS * (g + 1))
                for k in range(KC):
                    ins = dve.tensor_scalar(hid[:, k, :], hid[:, k, :], gam[:, 0:1], LIM, ALU.mult, ALU.min)
                chain.sync(ins)
                for k in range(KC):
                    dve.tensor_scalar(hid[:, k, :], hid[:, k, :], -LIM, None, ALU.max).then_inc(S["clipped"], 1)
                if not last:
                    ln(g + 1, chain)
                wait(dve, S["down_in"], g + 1)
                if not (isinstance(g, int) and g == 0):
                    wait(dve, S["stored"], 16 * g)
                for h, (lo, n) in enumerate(((0, 4), (4, 2))):
                    ins = dve.tensor_tensor(y[:, lo:lo + n, :], dn[h][:, 0:n * C].rearrange("p (t c) -> p t c", c=C),
                                            b2[:, :].unsqueeze(1).broadcast_to([P, n, C]), ALU.add)
                chain.sync(ins)
                dve.sem_inc(S["y_read"], 1)
                yf = y[:, :, :].rearrange("p t c -> p (t c)")
                chain.sync(dve.tensor_reduce(bmax[:, 1:2], yf, AX.X, ALU.max, apply_absolute_value=True))
                dve.sem_inc(S["max_done"], 1)
                factor(g, chain, 1)
                chain.sync(dve.tensor_scalar(yf, yf, gam[:, 1:2], LIM, ALU.mult, ALU.min))
                x = X[:, bass.ds(TG * g, TG), :].rearrange("p t c -> p (t c)")
                dve.scalar_tensor_tensor(out=yf, in0=yf, scalar=-LIM, in1=x, op0=ALU.max, op1=ALU.add
                                         ).then_inc(S["y_done"], 1)
                if not last:
                    up_maxima(g + 1, chain)
                assert chain.n == (LAST if last else EACH), chain.n

            dve.memset(xt[C:CB, :], 1.0)
            chain = Chain(dve, S["dve_step"])
            ln(0, chain)
            up_maxima(0, chain)
            base = chain.n
            body(0, False)
            with dve.Fori(1, QG - 1) as g:
                body(g, False)
            body(QG - 1, True)

        @block.scalar
        def _(act):
            def tokens_out(g):
                wait(act, S["turned"], g + 1)
                wait(act, S["up_in"], MS * g)
                act.activation(xt[0:C, 0:512], tp[0][0:C, :], ACT.Copy)
                act.activation(xt[0:C, 512:TOKS], tp[1][0:C, 0:TB], ACT.Copy).then_inc(S["xt_done"], 1)

            def ups_out(g):
                wait(act, S["down_in"], g)
                for m in range(MS):
                    wait(act, S["up_max"], MS * g + m + 1)
                    k, lo, n = m // 2, 512 * (m % 2), (512, TB)[m % 2]
                    act.activation(hid[:, k, lo:lo + n], up[m % UPS][:, 0:n], ACT.Copy).then_inc(S["up_out"], 1)

            def body(g, last):
                for k in range(KC):
                    wait(act, S["clipped"], KC * g + k + 1)
                    act.activation(hid[:, k, :], hid[:, k, :], ACT.Gelu).then_inc(S["hid_done"], 1)
                if not last:
                    tokens_out(g + 1)
                    ups_out(g + 1)

            tokens_out(0)
            ups_out(0)
            body(0, False)
            with act.Fori(1, QG - 1) as g:
                body(g, False)
            body(QG - 1, True)

        @block.tensor
        def _(pe):
            def top_in(g, k):
                wait(pe, S["max_done"], 2 * g + k + 1)
                pe.matmul(gp[0:1, 0:P], bmax[:, k:k + 1], ident[:, :], start=True, stop=True
                          ).then_inc(S["max_in"], 1)

            def top_out(g, k):
                wait(pe, S["top_done"], 2 * g + k + 1)
                pe.matmul(gp[:, P:P + 1], inv_qb[:, :], top[:, k:k + 1], start=True, stop=True
                          ).then_inc(S["top_in"], 1)

            def turn(g):
                wait(pe, S["xn_done"], g + 1)
                wait(pe, S["xt_done"], g)
                for j in range(TG):
                    ins = pe.transpose(tp[j // 4][0:C, (j % 4) * P:(j % 4 + 1) * P], xn[:, j, :], ident[:, :])
                ins.then_inc(S["turned"], 1)

            def ups(g, ms):
                wait(pe, S["xt_done"], g + 1)
                for m in ms:
                    wait(pe, S["up_out"], MS * g + m - UPS + 1)
                    k, lo, n = m // 2, 512 * (m % 2), (512, TB)[m % 2]
                    pe.matmul(up[m % UPS][:, 0:n], w1[:, k * P:(k + 1) * P], xt[:, lo:lo + n], start=True, stop=True
                              ).then_inc(S["up_in"], 1)

            def body(g, last):
                top_in(g, 0)
                top_out(g, 0)
                wait(pe, S["hid_done"], KC * (g + 1))
                wait(pe, S["y_read"], g)
                for j in range(TG):
                    for k in range(KC):
                        ins = pe.matmul(dn[j // 4][:, (j % 4) * C:(j % 4 + 1) * C], hid[:, k, j * P:(j + 1) * P],
                                        w2[:, k, :], start=(k == 0), stop=(k == KC - 1))
                ins.then_inc(S["down_in"], 1)
                if not last:
                    turn(g + 1)
                top_in(g, 1)
                if not last:
                    ups(g + 1, range(2))
                top_out(g, 1)
                if not last:
                    ups(g + 1, range(2, MS))

            pe.wait_ge(S["consts"], 1)
            turn(0)
            ups(0, range(MS))
            body(0, False)
            with pe.Fori(1, QG - 1) as g:
                body(g, False)
            body(QG - 1, True)


PHASES = ("l0c", "m0", "l1c", "m1", "l2c", "m2", "l3c", "l3f")


def build(nc, A, out, phases=PHASES, load_x=False):
    with ExitStack() as ctx:
        s = Scope(nc, ctx, "all")
        T = {"X": s.sb("X", [P, NT, C]), "ident": s.sb("ident", [P, P])}
        T["scratch"] = nc.dram_tensor("conv_scratch", [NT * P, C], F32).ap()
        T["moe"] = [(s.sb(f"w1_{n}", [CB, NE * KC, P]), s.sb(f"w2_{n}", [P, NE * KC, C]),
                     s.sb(f"gw_{n}", [CB, NE]), s.sb(f"b2_{n}", [P, NE, C])) for n in range(3)]
        for name in LATE:
            shape = list(A[name].shape)
            T[name] = s.sb(name, [C, 2 * INNER + C] if name == "l3_wkv" else shape)
        T["late_in"] = s.sem("late_in")
        T["moe_in"] = [s.sem(f"moe_in{n}") for n in range(3)]
        if load_x:
            ld = s.sem("ld")
            with nc.Block() as block:
                @block.sync
                def _(sp):
                    sp.dma_start(T["ident"][:, :], A["ident"]).then_inc(ld, 16)
                    sp.dma_start(T["X"][:, :, :], A["x_tokens"]).then_inc(ld, 16)
                    load_weights(sp, T, A)
                    sp.wait_ge(ld, 32)
                    for m in T["moe_in"]:
                        sp.wait_ge(m, 64)
                    sp.wait_ge(T["late_in"], 16 * len(LATE))
            with ExitStack() as c2:
                s2 = Scope(nc, c2, "prep")
                work = WeightWork(s2, T, s2.psum("pb", [P, 512]))
                st2 = s2.sem("st2")
                block = c2.enter_context(nc.Block())
                @block.vector
                def _(dve):
                    chain = Chain(dve, st2)
                    work.dve_sums(dve, chain)
                    work.dve_centre(dve, chain)
                    work.dve_binarise(dve, chain)
                @block.scalar
                def _(act):
                    work.act_signs(act)
                @block.tensor
                def _(pe):
                    work.pe_means(pe)
        for ph in phases:
            before = nc.snapshot_sems()
            if ph == "l0c":
                l0_conv(nc, T, A)
            elif ph in ("m0", "m1", "m2"):
                moe(nc, T, A, int(ph[1]))
            elif ph == "l1c":
                l1_attention(nc, T, A)
            elif ph == "l2c":
                l2_conv(nc, T, A)
            elif ph == "l3c":
                l3_conv(nc, T, A)
            elif ph == "l3f":
                l3_ffn(nc, T, A, out)
            nc.clear_and_free_semaphores(nc.allocated_since(before))
            nc.all_engine_barrier()
        if "l3f" not in phases:
            st = s.sem("st")
            with nc.Block() as block:
                @block.sync
                def _(sp):
                    for m in T["moe_in"]:
                        sp.wait_ge(m, 64)
                    sp.dma_start(out, T["X"][:, :, :]).then_inc(st, 16)
                    sp.wait_ge(st, 16)


def tokens(x):
    return np.ascontiguousarray(np.transpose(x.reshape(NI, C, 2, P), (3, 0, 2, 1)).reshape(P, NT, C))


def layouts(v):
    f = np.float32
    v = {k: np.asarray(a) for k, a in v.items()}
    x = v["x"]
    A = {"x_tokens": tokens(x), "ident": np.eye(P, dtype=f)}
    A["x_rows"] = np.ascontiguousarray(
        np.transpose(x.reshape(2, 8, C, SIDE, SIDE), (1, 3, 0, 4, 2)).reshape(P, NT, C))

    def band(w):
        k = w.shape[-1]
        out = np.zeros((GC, SIDE, NG, k, SIDE), f)
        wg = w.reshape(NG, GC, k, k)
        for xi in range(SIDE):
            for xo in range(SIDE):
                d = xi - xo + k // 2
                if 0 <= d < k:
                    out[:, xi, :, :, xo] = np.transpose(wg[:, :, :, d], (1, 0, 2))
        return out.reshape(P, NG, k, SIDE)

    A["band"] = band(v["L0_conv_w_large"])
    A["band_s"] = band(v["L0_conv_w_small"])
    bn = np.stack([np.stack([v[f"L0_conv_{a}_{b}"] for b in "lsi"]) for a in "gbmv"])
    bn = np.transpose(bn.reshape(4, 3, NG, GC), (3, 0, 1, 2))
    A["bn"] = np.ascontiguousarray(np.repeat(bn, SIDE, axis=0))
    A["eye"] = np.tile(np.eye(SIDE, dtype=f), (GC, 1))
    A["own"] = np.repeat(np.eye(GC, dtype=f), SIDE, axis=0)
    for n in range(3):
        g = lambda name: v[f"L{n}_ffn_{name}"]
        w1 = np.concatenate([np.transpose(g("w1"), (1, 0, 2)).reshape(C, NE * HID), g("b1").reshape(1, -1)])
        A[f"w1_{n}"] = w1.reshape(CB, NE * KC, P)
        A[f"w2_{n}"] = np.ascontiguousarray(
            np.transpose(g("w2").reshape(NE * KC, P, C), (1, 0, 2)))
        A[f"gw_{n}"] = np.concatenate([g("gate_w"), g("gate_b").reshape(1, -1)])
        A[f"b2_{n}"] = np.ascontiguousarray(np.broadcast_to(g("b2")[None], (P, NE, C)))
    def stacked(w):
        w = w.reshape(w.shape[:-1] + (SG, 2, 1, KD))
        out = np.zeros(w.shape[:-4] + (SG, 2, KS3 // KD, KD), f)
        out[..., 0:3, :] = w
        return out.reshape(w.shape[:-4] + (SG, P))

    c = {k[8:]: a for k, a in v.items() if k.startswith("L1_conv_")}
    wq = np.zeros((CB, HEADS * KD), f)
    wq[C - DS:C] = c["Wq"].T
    wq[C] = c["q_bias"]
    wk = np.concatenate([c["Wk"].T, c["k_bias"][None]])
    A["l1_wqk"] = np.zeros((P, 2, SG, P), f)
    A["l1_wqk"][0:CB] = stacked(np.stack([wq, wk], axis=1))
    A["l1_sqk"] = np.broadcast_to(stacked(np.stack([c["q_scale"], c["k_scale"]]))[None], (C, 2, SG, P))
    low = np.zeros((P, 3), f)
    low[np.arange(P) // KD % 4 == 1, 0] = -1
    low[np.arange(P) // KD % 4 == 2, 1] = -1
    low[HEADS:2 * HEADS, 2] = -1
    A["l1_low"] = low
    A["l1_sel"] = np.zeros((P, HEADS, P), f)
    A["l1_sel"][0:2 * HEADS] = np.tile(np.eye(HEADS, dtype=f), (2, 1))[:, :, None]
    A["l1_wv"] = np.concatenate([c["Wv"].T, c["v_bias"][None]])
    A["l1_sv"] = np.broadcast_to(c["v_scale"][None], (C, HEADS * DH))
    A["l1_wp"] = np.transpose(c["Wp"].T.reshape(2, C, DS), (1, 0, 2))
    A["l1_sp"] = np.stack([c["p_scale"], c["p_bias"]], axis=1)
    A["l1_wo"] = c["Wo"].T
    wx = np.zeros((CB, C), f)
    wx[C - DS:C] = c["Wo"].T
    wx[C] = c["o_bias"]
    A["l1_wx"] = wx
    A["l1_so"] = np.broadcast_to(c["o_scale"][None], (C, C))
    c = {k[8:]: a for k, a in v.items() if k.startswith("L2_conv_")}
    kinds = ("q", "k", "off1", "v")
    A["l2_taps"] = np.stack([c[f"w_{k}"].reshape(C, KS * KS) for k in kinds], axis=1)
    A["l2_bias"] = np.stack([c[f"b_{k}"] for k in kinds], axis=1)
    A["l2_lnp"] = np.stack([c["ln_g"], c["ln_b"]], axis=1)
    A["l2_woff"] = np.repeat(c["w_off2"][::-1].T[:, :, None], P, axis=2)
    line = (np.linspace(0.5, KSIDE - 0.5, KSIDE) / KSIDE * 2 - 1).astype(f)
    ref = np.stack([np.tile(line, KSIDE), np.repeat(line, KSIDE)])
    A["l2_ref"] = np.broadcast_to(ref[None], (P, 2, KPIX))
    px, py = np.arange(P) % SIDE, np.arange(P) // SIDE
    A["l2_coord"] = ((SIDE - 1) / 2 - np.stack([px, py, py + SIDE // 2], axis=1)).astype(f)
    A["l2_mask"] = (np.arange(P)[:, None] % HC2 // (HC2 // 4) == np.arange(HG)[None]).astype(f)
    A["l2_wout"] = c["w_out"].T
    c = {k[8:]: a for k, a in v.items() if k.startswith("L3_conv_")}
    A["l3_taps"] = np.stack([c["wq_dw"].reshape(C, KS * KS), c["wkv_dw"].reshape(C, KS * KS)], axis=1)
    A["l3_bn"] = np.transpose(np.stack([np.stack([c[f"{w}_bn_{a}"] for w in ("wq", "wkv")]) for a in "gbmv"]),
                              (2, 0, 1))
    A["l3_wq"], A["l3_wkv"], A["l3_wo"] = c["wq_pw"].T, c["wkv_pw"].T, c["wo"].T
    A["l3_wvt"] = c["wkv_pw"][INNER:]
    A["l3_bo"] = np.broadcast_to(c["bo"][None], (P, C))
    A["l3_mask"] = np.repeat(np.eye(L3H, dtype=f), L3D, axis=0)
    A["l3_w1"] = np.concatenate([v["L3_ffn_W1"].T, v["L3_ffn_b1"][None]])
    A["l3_w2"] = np.transpose(v["L3_ffn_W2"].T.reshape(KC, P, C), (1, 0, 2))
    A["l3_b2"] = np.broadcast_to(v["L3_ffn_b2"][None], (P, C))
    return {k: np.ascontiguousarray(a) for k, a in A.items()}


def kernel(**inputs):
    import concourse.bacc as bacc
    from concourse.bass_utils import run_bass_kernel_spmd

    arrays = layouts(inputs)
    nc = bacc.Bacc("TRN2", target_bir_lowering=False, num_devices=1)
    A = {name: nc.dram_tensor(name, a.shape, F32, kind="ExternalInput").ap() for name, a in arrays.items()}
    out = nc.dram_tensor("out_tokens", (P, NT, C), F32, kind="ExternalOutput").ap()
    build(nc, A, out, PHASES)
    y = run_bass_kernel_spmd(nc, [arrays], core_ids=[0]).results[0]["out_tokens"]
    return np.ascontiguousarray(y.reshape(P, NI, 2, C).transpose(1, 3, 2, 0).reshape(NI, C, SIDE, SIDE))
```

```python
from contextlib import ExitStack

import numpy as np

import concourse.bass as bass
from concourse import mybir

F32 = mybir.dt.float32
F32R = mybir.dt.float32r
ALU = mybir.AluOpType
ACT = mybir.ActivationFunctionType
AX = mybir.AxisListType

P = 128
C = 96
CB = C + 1
NI = 16
SIDE = 16
PIX = SIDE * SIDE
NT = NI * PIX // P
HALF = C // 2
KL, KS = 13, 3
GC = P // SIDE
NG = C // GC
NE, HID = 4, 4 * C
KC = HID // P
GT = 4
GW = GT * P
HEADS, KD, DH = 6, 16, 32
DS = C // 4
SG = HEADS // 2
CT = C + DS
KS3 = 4 * KD
BN_EPS = 1e-5


def wait(eng, sem, count):
    if isinstance(count, int) and count <= 0:
        return
    eng.wait_ge(sem, count)


class Chain:

    def __init__(self, eng, sem, start=0):
        self.eng, self.sem, self.start, self.n = eng, sem, start, 0

    def sync(self, ins):
        ins.then_inc(self.sem, 1)
        self.n += 1
        self.eng.wait_ge(self.sem, self.start + self.n)


def layernorm_stats(dve, chain, tiles, stats, mean, var, eps, rows=P):
    n = len(tiles)
    for j, tile in enumerate(tiles):
        last = dve.bn_stats(stats[0:rows, j, :], tile)
    chain.sync(last)
    s = stats[0:rows, 0:n, :]
    dve.tensor_tensor(mean[0:rows, 0:n], s[:, :, 1], s[:, :, 4], ALU.subtract)
    chain.sync(dve.tensor_tensor(var[0:rows, 0:n], s[:, :, 2], s[:, :, 5], ALU.add))
    dve.scalar_tensor_tensor(out=mean[0:rows, 0:n], in0=mean[0:rows, 0:n], scalar=0.25,
                             in1=mean[0:rows, 0:n], op0=ALU.mult, op1=ALU.mult)
    chain.sync(dve.tensor_scalar(var[0:rows, 0:n], var[0:rows, 0:n], 1.0 / C, eps, ALU.mult, ALU.add))
    chain.sync(dve.tensor_tensor(var[0:rows, 0:n], var[0:rows, 0:n], mean[0:rows, 0:n], ALU.add))


def layernorm_apply(dve, chain, tiles, outs, stats, mean, rstd, rows=P):
    n = len(tiles)
    s = stats[0:rows, 0:n, :]
    chain.sync(dve.tensor_tensor(mean[0:rows, 0:n], s[:, :, 1], s[:, :, 4], ALU.add))
    chain.sync(dve.tensor_scalar(mean[0:rows, 0:n], mean[0:rows, 0:n], 0.5, None, ALU.mult))
    for j, (tile, out) in enumerate(zip(tiles, outs)):
        last = dve.tensor_scalar(out, tile, mean[0:rows, j:j + 1], rstd[0:rows, j:j + 1],
                                 ALU.subtract, ALU.mult)
    return last


class Scope:

    def __init__(self, nc, ctx, tag):
        self.nc, self.ctx, self.tag = nc, ctx, tag

    def sb(self, name, shape, dtype=F32):
        return self.ctx.enter_context(self.nc.sbuf_tensor(f"{self.tag}_{name}", shape, dtype))

    def psum(self, name, shape):
        return self.ctx.enter_context(self.nc.psum_tensor(f"{self.tag}_{name}", shape, F32))

    def sem(self, name):
        return self.nc.alloc_semaphore(name=f"{self.tag}_{name}")


LATE = ("l3_w1", "l3_w2", "l3_b2", "l1_wqk", "l1_sqk", "l1_wv", "l1_sv", "l1_wp", "l1_sp", "l1_wo", "l1_wx", "l1_so",
        "l1_low", "l1_sel", "l2_taps", "l2_bias", "l2_lnp", "l2_woff", "l2_ref", "l2_coord", "l2_mask", "l2_wout",
        "l3_taps", "l3_bn", "l3_wq", "l3_wkv", "l3_wvt", "l3_wo", "l3_bo", "l3_mask")


def load_weights(sp, T, A):
    def moe_weights(n):
        for t, name in zip(T["moe"][n], ("w1", "w2", "gw", "b2")):
            sp.dma_start(t[tuple(slice(None) for _ in t.shape)], A[f"{name}_{n}"]).then_inc(T["moe_in"][n], 16)

    moe_weights(0)
    for name in LATE:
        t = T[name]
        if name == "l3_wkv":
            sp.dma_start(t[:, 0:2 * INNER], A[name]).then_inc(T["late_in"], 16)
        else:
            sp.dma_start(t[tuple(slice(None) for _ in t.shape)], A[name]).then_inc(T["late_in"], 16)
    moe_weights(1)
    moe_weights(2)


class WeightWork:

    def __init__(self, s, T, bank):
        self.T, self.bank = T, bank
        self.w1, self.w2 = T["l3_w1"], T["l3_w2"]
        self.w2f = self.w2[:, :, :].rearrange("p k c -> p (k c)")
        self.ones = s.sb("ones", [P, P])
        self.rs = s.sb("rs", [P, 2, QG])
        self.mu = s.sb("mu", [P, 2, QG])
        self.sg = s.sb("sg", [P, 2, HID])
        self.rs_done, self.mu_in, self.centred, self.signs = (
            s.sem(n) for n in ("rs_done", "mu_in", "centred", "signs"))

    def w2_groups(self, k):
        return self.w2[:, k, 0:QG * (C // QG)].rearrange("p (g r) -> p g r", g=QG)

    def dve_sums(self, dve, chain):
        T, rs, mu = self.T, self.rs, self.mu
        dve.memset(self.ones[:, :], 1.0)
        dve.memset(rs[:, :, :], 0.0)
        chain.sync(dve.memset(self.sg[:, :, :], 0.0))
        dve.wait_ge(T["late_in"], 16 * len(LATE))
        wqk, wv, wx, wo = T["l1_wqk"], T["l1_wv"], T["l1_wx"], T["l1_wo"]
        dve.tensor_tensor(wqk[:, :, :, :], wqk[:, :, :, :], T["l1_sqk"][:, :, :, :], ALU.mult)
        dve.tensor_tensor(wv[0:C, :], wv[0:C, :], T["l1_sv"][:, :], ALU.mult)
        dve.tensor_tensor(wx[0:C, :], wx[0:C, :], T["l1_so"][:, :], ALU.mult)
        dve.tensor_tensor(wo[:, :], wo[:, :], T["l1_so"][0:DS, :], ALU.mult)
        g1 = self.w1[0:C, 0:QG * (HID // QG)].rearrange("c (g r) -> c g r", g=QG)
        dve.tensor_reduce(rs[0:C, 0, :], g1, AX.X, ALU.add)
        for k in range(KC):
            chain.sync(dve.tensor_reduce(mu[:, 0, :], self.w2_groups(k), AX.X, ALU.add))
            chain.sync(dve.tensor_tensor(rs[:, 1, :], rs[:, 1, :], mu[:, 0, :], ALU.add))
        dve.sem_inc(self.rs_done, 1)

    def pe_means(self, pe):
        pe.wait_ge(self.rs_done, 1)
        pe.matmul(self.bank[:, 0:2 * QG], self.ones[:, :], self.rs[:, :, :].rearrange("p a g -> p (a g)"),
                  start=True, stop=True).then_inc(self.mu_in, 1)

    def dve_centre(self, dve, chain):
        w1, w2, mu = self.w1, self.w2, self.mu
        R1, R2 = HID // QG, C // QG
        dve.wait_ge(self.mu_in, 1)
        dve.tensor_scalar(mu[:, 0, :], self.bank[:, 0:QG], 1.0 / (R1 * C), None, ALU.mult)
        chain.sync(dve.tensor_scalar(mu[:, 1, :], self.bank[:, QG:2 * QG], 1.0 / (R2 * HID), None, ALU.mult))
        g1 = w1[0:C, 0:QG * R1].rearrange("c (g r) -> c g r", g=QG)
        dve.tensor_tensor(g1, g1, mu[0:C, 0, :].unsqueeze(2).broadcast_to([C, QG, R1]), ALU.subtract)
        for k in range(KC):
            part = self.w2_groups(k)
            dve.tensor_tensor(part, part, mu[:, 1, :].unsqueeze(2).broadcast_to([P, QG, R2]), ALU.subtract)
        dve.memset(w1[0:C, QG * R1:HID], 0.0)
        chain.sync(dve.memset(w2[:, :, QG * R2:C], 0.0))
        dve.sem_inc(self.centred, 1)

    def act_signs(self, act):
        act.wait_ge(self.centred, 1)
        act.activation(self.sg[0:C, 0, :], self.w1[0:C, :], ACT.Sign)
        act.activation(self.sg[:, 1, 0:KC * C], self.w2f, ACT.Sign).then_inc(self.signs, 1)

    def dve_binarise(self, dve, chain):
        w1, w2f, sg = self.w1, self.w2f, self.sg
        dve.wait_ge(self.signs, 1)
        dve.tensor_tensor(sg[0:C, 0, :], sg[0:C, 0, :], w1[0:C, :], ALU.subtract)
        chain.sync(dve.tensor_tensor(sg[:, 1, 0:KC * C], sg[:, 1, 0:KC * C], w2f, ALU.subtract))
        dve.tensor_tensor(w1[0:C, :], w1[0:C, :], sg[0:C, 0, :], ALU.add)
        dve.tensor_tensor(w2f, w2f, sg[:, 1, 0:KC * C], ALU.add)


def l0_conv(nc, T, A):
    with ExitStack() as ctx:
        s = Scope(nc, ctx, "l0c")
        x0 = s.sb("x0", [P, NT, C])
        xn = s.sb("xn", [P, 2, C, SIDE])
        xt = s.sb("xt", [P, NG, NI, SIDE])
        band = s.sb("band", [P, NG, KL, SIDE])
        band_s = s.sb("band_s", [P, NG, KS, SIDE])
        full = s.sb("full", [P, NG * KL, GC, SIDE])
        bn = s.sb("bn", [P, 4, 3, NG])
        inv = s.sb("inv", [P, 3, NG])
        shift = s.sb("shift", [P, 3, NG])
        eye = s.sb("eye", [P, SIDE])
        eyes = s.sb("eyes", [P, NG, SIDE])
        own = s.sb("own", [P, GC])
        mhalf = s.sb("mhalf", [P, 3 * NG])
        stats = s.sb("stats", [P, NT, 6])
        mean = s.sb("mean", [P, NT])
        var = s.sb("var", [P, NT])
        rstd = s.sb("rstd", [P, NT])
        conv = s.sb("conv", [P, 2, PIX])
        back = x0[:, :, :].rearrange("p (h x) c -> p h x c", h=2)
        backB = xn[:, :, :, :].rearrange("p h c x -> p (h c x)").rearrange("p (t c) -> p t c", c=C)
        tp = [s.psum(f"tp{i}", [P, 512]) for i in range(2)]
        cp = [s.psum(f"cp{i}", [P, 512]) for i in range(2)]
        bp = [s.psum(f"bp{i}", [P, 512]) for i in range(2)]
        x0_in = [s.sem(f"x0_in{h}") for h in range(2)]
        bn_in, w_in, res_in, ident_in = (s.sem(n) for n in ("bn_in", "w_in", "res_in", "ident_in"))
        mhalf_set, v_eps, bn_pow, ln_var, ln_rstd = (s.sem(n) for n in
            ("mhalf_set", "v_eps", "bn_pow", "ln_var", "ln_rstd"))
        dve_step, band_done, full_done, xn_done = (s.sem(n) for n in
            ("dve_step", "band_done", "full_done", "xn_done"))
        turned, xt_done, conv_done, conv_out, back_done, back_out = (s.sem(n) for n in
            ("turned", "xt_done", "conv_done", "conv_out", "back_done", "back_out"))
        stored = [[s.sem(f"stored{k}{h}") for h in range(2)] for k in range(2)]
        reread = [[s.sem(f"reread{k}{h}") for h in range(2)] for k in range(2)]
        FG = 3
        work = WeightWork(s, T, tp[0])
        block = ctx.enter_context(nc.Block())

        @block.sync
        def _(sp):
            for h in range(2):
                half = slice(h * SIDE, (h + 1) * SIDE)
                sp.dma_start(x0[:, half, :], A["x_rows"][:, half, :]).then_inc(x0_in[h], 16)
            sp.dma_start(T["ident"][:, :], A["ident"]).then_inc(ident_in, 16)
            sp.wait_ge(w_in, 64)
            sp.dma_start(T["X"][:, :, :], A["x_tokens"]).then_inc(res_in, 16)
            load_weights(sp, T, A)
            for k in range(2):
                chans = slice(k * HALF, (k + 1) * HALF)
                sp.wait_ge(back_out, (k + 1) * NG // 2)
                rows = [T["scratch"][h * (NI // 2) * PIX:(h + 1) * (NI // 2) * PIX, chans] for h in range(2)]
                for h in range(2):
                    sp.dma_start(rows[h].rearrange("(p x) c -> p x c", x=SIDE), back[:, h, :, chans]
                                 ).then_inc(stored[k][h], 16)
                for h in range(2):
                    sp.wait_ge(stored[k][h], 16)
                    sp.dma_start(backB[:, h * NT // 2:(h + 1) * NT // 2, chans],
                                 rows[h].rearrange("(t p) c -> p t c", p=P)).then_inc(reread[k][h], 16)

        @block.gpsimd
        def _(pool):
            pool.memset(mhalf[:, :], -0.5).then_inc(mhalf_set, 1)
            pool.wait_ge(mhalf_set, 1)
            pool.wait_ge(v_eps, 1)
            pool.tensor_tensor(inv[:, :, :], shift[:, :, :], mhalf[:, :].rearrange("p (k g) -> p k g", k=3),
                               ALU.pow).then_inc(bn_pow, 1)
            for h in range(2):
                half = slice(h * SIDE, (h + 1) * SIDE)
                pool.wait_ge(ln_var, h + 1)
                pool.tensor_tensor(rstd[:, half], var[:, half], mhalf[:, 0:SIDE], ALU.pow).then_inc(ln_rstd, 1)

        @block.scalar
        def _(act):
            act.dma_start(bn[:, :, :, :], A["bn"]).then_inc(bn_in, 16)
            act.dma_start(band[:, :, :, :], A["band"]).then_inc(w_in, 16)
            act.dma_start(band_s[:, :, :, :], A["band_s"]).then_inc(w_in, 16)
            act.dma_start(eye[:, :], A["eye"]).then_inc(w_in, 16)
            act.dma_start(own[:, :], A["own"]).then_inc(w_in, 16)

            def fill(chunk):
                groups = slice(chunk * FG, (chunk + 1) * FG)
                rows = slice(chunk * FG * KL, (chunk + 1) * FG * KL)
                for k in range(GC):
                    last = act.activation(full[:, rows, k, :], band[:, groups, :, :].rearrange("p g r x -> p (g r) x"),
                                          ACT.Copy, scale=own[:, k:k + 1])
                last.then_inc(full_done, 1)

            act.wait_ge(band_done, 1)
            fill(0)
            for g2 in range(NG // 2):
                act.wait_ge(turned, g2 + 1)
                act.activation(xt[:, 2 * g2:2 * g2 + 2, :, :].rearrange("p g i r -> p (g i r)"), tp[g2 % 2][:, :],
                               ACT.Copy).then_inc(xt_done, 1)
            act.wait_ge(band_done, 2)
            fill(1)
            for g in range(NG):
                act.wait_ge(conv_done, g + 1)
                if g >= 2:
                    act.wait_ge(back_done, g - 1)
                act.activation(conv[:, g % 2, :], cp[g % 2][:, 0:PIX], ACT.Identity,
                               bias=shift[:, 0, g:g + 1]).then_inc(conv_out, 1)
                if g in (1, 3):
                    fill(2 + g // 2)
            work.act_signs(act)

        @block.vector
        def _(dve):
            chain = Chain(dve, dve_step)
            dve.wait_ge(bn_in, 16)
            chain.sync(dve.tensor_scalar(shift[:, :, :], bn[:, 3, :, :], BN_EPS, None, ALU.add))
            dve.sem_inc(v_eps, 1)
            tiles = [x0[:, t, :] for t in range(NT)]
            halves = [slice(h * SIDE, (h + 1) * SIDE) for h in range(2)]
            for h, half in enumerate(halves):
                dve.wait_ge(x0_in[h], 16)
                layernorm_stats(dve, chain, tiles[half], stats[:, half, :], mean[:, half], var[:, half], 1e-6)
                dve.sem_inc(ln_var, 1)
            dve.wait_ge(bn_pow, 1)
            chain.sync(dve.tensor_tensor(inv[:, :, :], inv[:, :, :], bn[:, 0, :, :], ALU.mult))
            chain.sync(dve.tensor_tensor(shift[:, :, :], bn[:, 2, :, :], inv[:, :, :], ALU.mult))
            chain.sync(dve.tensor_tensor(shift[:, :, :], bn[:, 1, :, :], shift[:, :, :], ALU.subtract))
            chain.sync(dve.tensor_tensor(shift[:, 0, :], shift[:, 0, :], shift[:, 1, :], ALU.add))
            chain.sync(dve.tensor_tensor(shift[:, 0, :], shift[:, 0, :], shift[:, 2, :], ALU.add))
            dve.wait_ge(w_in, 64)

            def merge_bands(lo, hi):
                gs, n = slice(lo, hi), hi - lo
                bv = band[:, gs, :, :].rearrange("p g r x -> p g (r x)")
                sv = band_s[:, gs, :, :].rearrange("p g r x -> p g (r x)")
                dve.tensor_tensor(bv, bv, inv[:, 0, gs].unsqueeze(2).broadcast_to([P, n, KL * SIDE]), ALU.mult)
                dve.tensor_tensor(sv, sv, inv[:, 1, gs].unsqueeze(2).broadcast_to([P, n, KS * SIDE]), ALU.mult)
                chain.sync(dve.tensor_tensor(eyes[:, gs, :], eye[:, :].unsqueeze(1).broadcast_to([P, n, SIDE]),
                                             inv[:, 2, gs].unsqueeze(2).broadcast_to([P, n, SIDE]), ALU.mult))
                mid = (KL - KS) // 2
                inner = band[:, gs, mid:mid + KS, :].rearrange("p g r x -> p g (r x)")
                chain.sync(dve.tensor_tensor(inner, inner, sv, ALU.add))
                chain.sync(dve.tensor_tensor(band[:, gs, KL // 2, :], band[:, gs, KL // 2, :], eyes[:, gs, :],
                                             ALU.add))
                dve.sem_inc(band_done, 1)

            merge_bands(0, FG)
            for h, half in enumerate(halves):
                dve.wait_ge(ln_rstd, h + 1)
                layernorm_apply(dve, chain, tiles[half], [xn[:, h, :, t] for t in range(SIDE)],
                                stats[:, half, :], mean[:, half], rstd[:, half]).then_inc(xn_done, 1)
            merge_bands(FG, NG)
            for g in range(NG):
                dve.wait_ge(back_done, g + 1)
                dve.tensor_copy(back[:, :, :, GC * g:GC * (g + 1)],
                                bp[g % 2][:, 0:PIX].rearrange("p (h c x) -> p h x c", h=2, x=SIDE)
                                ).then_inc(back_out, 1)
                if g == NG - 7:
                    work.dve_sums(dve, chain)
                if g == NG - 3:
                    work.dve_centre(dve, chain)
            work.dve_binarise(dve, chain)
            dve.wait_ge(res_in, 16)
            for k in range(2):
                chans = slice(k * HALF, (k + 1) * HALF)
                for h in range(2):
                    dve.wait_ge(reread[k][h], 16)
                    x = T["X"][:, h * NT // 2:(h + 1) * NT // 2, chans]
                    dve.tensor_tensor(x, x, backB[:, h * NT // 2:(h + 1) * NT // 2, chans], ALU.add)

        @block.tensor
        def _(pe):
            ident = T["ident"]
            pe.wait_ge(ident_in, 16)
            pe.wait_ge(xn_done, 2)
            for g2 in range(NG // 2):
                if g2 >= 2:
                    pe.wait_ge(xt_done, g2 - 1)
                for k in range(4):
                    g, h = 2 * g2 + k // 2, k % 2
                    last = pe.transpose(tp[g2 % 2][:, k * P:(k + 1) * P], xn[:, h, GC * g:GC * (g + 1), :]
                                        .rearrange("p c x -> p (c x)"), ident[:, :])
                last.then_inc(turned, 1)

            def conv_group(g):
                pe.wait_ge(xt_done, g // 2 + 1)
                pe.wait_ge(full_done, g // FG + 1)
                if g >= 2:
                    pe.wait_ge(conv_out, g - 1)
                out = cp[g % 2][:, 0:PIX].rearrange("p (i r) -> p i r", r=SIDE)
                order = [KL // 2] + [r for r in range(KL) if r != KL // 2]
                for n, r in enumerate(order):
                    d = r - KL // 2
                    lo, hi = max(0, -d), min(SIDE, SIDE - d)
                    last = pe.matmul(out[:, :, lo:hi], full[:, g * KL + r, :, :].rearrange("p c x -> p (c x)"),
                                     xt[:, g, :, lo + d:hi + d], start=(n == 0), stop=(n == KL - 1))
                last.then_inc(conv_done, 1)

            def turn_back(g):
                pe.wait_ge(conv_out, g + 1)
                if g >= 2:
                    pe.wait_ge(back_out, g - 1)
                for h in range(2):
                    last = pe.transpose(bp[g % 2][:, h * P:(h + 1) * P], conv[:, g % 2, h * P:(h + 1) * P],
                                        ident[:, :])
                last.then_inc(back_done, 1)

            conv_group(0)
            for g in range(NG):
                if g + 1 < NG:
                    conv_group(g + 1)
                turn_back(g)
                if g == NG - 4:
                    work.pe_means(pe)


def moe(nc, T, A, layer):
    w1, w2, gw, b2 = T["moe"][layer]
    X, ident = T["X"], T["ident"]
    STEPS = NT // GT
    UPS = 4
    with ExitStack() as ctx:
        s = Scope(nc, ctx, f"moe{layer}")
        w1h = s.sb("w1h", [CB, NE * KC, P], F32R)
        w1l = s.sb("w1l", [CB, NE * KC, P], F32R)
        xn = s.sb("xn", [P, GT, C])
        xt = s.sb("xt", [CB, 2, GW])
        xh = s.sb("xh", [CB, 2, GW], F32R)
        xl = s.sb("xl", [CB, 2, GW], F32R)
        hid = s.sb("hid", [P, NE * KC, GW])
        stats = s.sb("stats", [P, GT, 6])
        mean = s.sb("mean", [P, GT])
        var = s.sb("var", [P, GT])
        rstd = s.sb("rstd", [P, GT])
        mhalf = s.sb("mhalf", [P, GT])
        euler = s.sb("euler", [P, GT * NE])
        smax = s.sb("smax", [P, GT])
        logit = s.sb("logit", [P, GT, NE])
        prob = s.sb("prob", [P, GT, NE])
        ge = s.sb("ge", [P, 3, GT, NE])
        rank = s.sb("rank", [P, GT, NE])
        gate = s.sb("gate", [P, 2, GT, NE])
        up = [s.psum(f"up{i}", [P, 512]) for i in range(UPS)]
        tp = s.psum("tp", [P, 512])
        gp = s.psum("gp", [P, 512])
        dn = [s.psum(f"dn{i}", [P, 512]) for i in range(2)]
        names = ("consts", "var_done", "rstd_done", "logit_done", "exp_done", "dve_step", "xn_done", "turned",
                 "xt_done", "xl_done", "w_high", "w_low", "gates_in", "gates_read", "up_done", "hid_done",
                 "down_done", "added")
        (consts, var_done, rstd_done, logit_done, exp_done, dve_step, xn_done, turned, xt_done, xl_done, w_high,
         w_low, gates_in, gates_read, up_done, hid_done, down_done, added) = (s.sem(n) for n in names)
        block = ctx.enter_context(nc.Block())

        def steps(eng, step):
            step(0, 0, False)
            with eng.Fori(1, STEPS // 2) as i:
                step(2 * i - 1, 1, False)
                step(2 * i, 0, False)
            step(STEPS - 1, 1, True)

        def expert(t, e):
            return t[:, e * KC:(e + 1) * KC, :]

        @block.gpsimd
        def _(pool):
            pool.memset(mhalf[:, :], -0.5)
            pool.memset(euler[:, :], float(np.e)).then_inc(consts, 1)
            pool.wait_ge(consts, 1)
            pool.memset(xt[C:CB, :, :], 1.0).then_inc(consts, 1)
            pool.wait_ge(consts, 2)

            def rstd_of(g):
                pool.wait_ge(var_done, g + 1)
                pool.tensor_tensor(rstd[:, :], var[:, :], mhalf[:, :], ALU.pow).then_inc(rstd_done, 1)

            def exp_of(g):
                pool.wait_ge(logit_done, g + 1)
                pool.tensor_tensor(prob[:, :, :], euler[:, :].rearrange("p (t e) -> p t e", e=NE),
                                   logit[:, :, :], ALU.pow).then_inc(exp_done, 1)

            with pool.Fori(0, STEPS) as g:
                rstd_of(g)
                exp_of(g)

        @block.vector
        def _(dve):
            STATS, APPLY, GATES = 4, 2, 15
            EACH = STATS + APPLY + GATES + 2 * NE

            def stats_of(g, chain):
                layernorm_stats(dve, chain, [X[:, GT * g + j, :] for j in range(GT)], stats, mean, var, 1e-5)
                dve.sem_inc(var_done, 1)

            def apply_of(g, chain):
                wait(dve, rstd_done, g + 1)
                wait(dve, turned, g)
                layernorm_apply(dve, chain, [X[:, GT * g + j, :] for j in range(GT)],
                                [xn[:, j, :] for j in range(GT)], stats, mean, rstd).then_inc(xn_done, 1)

            def low_of(g, p):
                wait(dve, xt_done, g + 1)
                dve.tensor_tensor(xl[0:C, p, :], xt[0:C, p, :], xh[0:C, p, :].bitcast(F32), ALU.subtract
                                  ).then_inc(xl_done, 1)

            def gates_of(g, p, chain):
                wide = lambda a: a.unsqueeze(2).broadcast_to([P, GT, NE])
                scores = gp[:, 0:GT * NE].rearrange("p (t e) -> p t e", e=NE)
                wait(dve, gates_in, g + 1)
                chain.sync(dve.tensor_reduce(smax[:, :], scores, AX.X, ALU.max))
                chain.sync(dve.tensor_tensor(logit[:, :, :], scores, wide(smax[:, :]), ALU.subtract))
                dve.sem_inc(logit_done, 1)
                dve.sem_inc(gates_read, 1)
                for e in range(NE):
                    dve.memset(rank[:, :, e], float(NE - 1 - e))
                wait(dve, exp_done, g + 1)
                chain.sync(dve.tensor_reduce(smax[:, :], prob[:, :, :], AX.X, ALU.add))
                chain.sync(dve.reciprocal(smax[:, :], smax[:, :]))
                chain.sync(dve.tensor_tensor(prob[:, :, :], prob[:, :, :], wide(smax[:, :]), ALU.mult))
                for d in range(1, NE):
                    last = dve.tensor_tensor(ge[:, d - 1, :, 0:NE - d], prob[:, :, 0:NE - d], prob[:, :, d:NE],
                                             ALU.is_ge)
                chain.sync(last)
                for d in range(1, NE):
                    ahead = ge[:, d - 1, :, 0:NE - d]
                    last = dve.tensor_tensor(rank[:, :, d:NE], rank[:, :, d:NE], ahead, ALU.add)
                    if d < NE / 2:
                        chain.sync(last)
                    chain.sync(dve.tensor_tensor(rank[:, :, 0:NE - d], rank[:, :, 0:NE - d], ahead, ALU.subtract))
                best = gate[:, p, :, :]
                chain.sync(dve.scalar_tensor_tensor(
                    out=best.rearrange("p t e -> p (t e)"), in0=rank[:, :, :].rearrange("p t e -> p (t e)"),
                    scalar=2.0, in1=prob[:, :, :].rearrange("p t e -> p (t e)"), op0=ALU.is_lt, op1=ALU.mult))
                chain.sync(dve.tensor_reduce(smax[:, :], best, AX.X, ALU.add))
                chain.sync(dve.tensor_scalar(smax[:, :], smax[:, :], 1e-9, None, ALU.add))
                chain.sync(dve.reciprocal(smax[:, :], smax[:, :]))
                chain.sync(dve.tensor_tensor(best, best, wide(smax[:, :]), ALU.mult))

            def bias_sums(g, p, chain):
                for e in range(NE):
                    for j in range(GT):
                        x = X[:, GT * g + j, :]
                        last = dve.scalar_tensor_tensor(out=x, in0=b2[:, e, :], scalar=gate[:, p, j, e:e + 1], in1=x,
                                                        op0=ALU.mult, op1=ALU.add)
                    chain.sync(last)

            def expert_sum(g, p, e, chain):
                wait(dve, down_done, NE * g + e + 1)
                for j in range(GT):
                    x = X[:, GT * g + j, :]
                    last = dve.scalar_tensor_tensor(out=x, in0=dn[e % 2][:, j * C:(j + 1) * C],
                                                    scalar=gate[:, p, j, e:e + 1], in1=x, op0=ALU.mult, op1=ALU.add)
                chain.sync(last)
                dve.sem_inc(added, 1)

            def step(g, p, last):
                chain = Chain(dve, dve_step, base + g * EACH)
                bias_sums(g, p, chain)
                if not last:
                    stats_of(g + 1, chain)
                expert_sum(g, p, 0, chain)
                if not last:
                    apply_of(g + 1, chain)
                expert_sum(g, p, 1, chain)
                if not last:
                    low_of(g + 1, 1 - p)
                    gates_of(g + 1, 1 - p, chain)
                expert_sum(g, p, 2, chain)
                expert_sum(g, p, 3, chain)
                assert chain.n == (2 * NE if last else EACH), chain.n

            chain = Chain(dve, dve_step)
            stats_of(0, chain)
            apply_of(0, chain)
            for e in range(NE):
                dve.wait_ge(w_high, e + 1)
                dve.tensor_tensor(expert(w1l, e), expert(w1, e), expert(w1h, e).bitcast(F32), ALU.subtract
                                  ).then_inc(w_low, 1)
                if e == 0:
                    low_of(0, 0)
            gates_of(0, 0, chain)
            base = chain.n
            steps(dve, step)

        @block.scalar
        def _(act):
            def gelus(g, e):
                for k in range(KC):
                    n = e * KC + k
                    if k == 0:
                        wait(act, down_done, NE * (g - 1) + e + 1)
                    wait(act, up_done, NE * KC * g + n + 1)
                    act.activation(hid[:, n, :], up[n % UPS][:, :], ACT.Gelu).then_inc(hid_done, 1)

            def turned_out(g, p):
                wait(act, turned, g + 1)
                act.activation(xh[0:C, p, :], tp[0:C, :], ACT.Copy)
                act.activation(xt[0:C, p, :], tp[0:C, :], ACT.Copy).then_inc(xt_done, 1)

            act.wait_ge(T["moe_in"][layer], 64)
            act.wait_ge(consts, 2)
            act.activation(xh[C:CB, :, :], xt[C:CB, :, :], ACT.Copy)
            act.activation(xl[C:CB, :, :], xt[C:CB, :, :], ACT.Copy, scale=0.0)
            act.activation(expert(w1h, 0), expert(w1, 0), ACT.Copy).then_inc(w_high, 1)
            turned_out(0, 0)
            for e in range(1, NE):
                act.activation(expert(w1h, e), expert(w1, e), ACT.Copy).then_inc(w_high, 1)
            gelus(0, 0)

            def step(g, p, last):
                gelus(g, 1)
                gelus(g, 2)
                if not last:
                    turned_out(g + 1, 1 - p)
                gelus(g, 3)
                if not last:
                    gelus(g + 1, 0)

            steps(act, step)

        @block.tensor
        def _(pe):
            def turn(g):
                wait(pe, xn_done, g + 1)
                wait(pe, xt_done, g)
                for j in range(GT):
                    last = pe.transpose(tp[0:C, j * P:(j + 1) * P], xn[:, j, :], ident[:, :])
                last.then_inc(turned, 1)

            def gates(g, p):
                wait(pe, xt_done, g + 1)
                wait(pe, gates_read, g)
                for j in range(GT):
                    last = pe.matmul(gp[:, j * NE:(j + 1) * NE], xt[:, p, j * P:(j + 1) * P], gw[:, :],
                                     start=True, stop=True)
                last.then_inc(gates_in, 1)

            def ups(g, p, e):
                if e == 0:
                    wait(pe, xl_done, g + 1)
                for k in range(KC):
                    n = e * KC + k
                    wait(pe, hid_done, NE * KC * g + n - UPS + 1)
                    bank = up[n % UPS][:, :]
                    pe.matmul(bank, w1h[:, n, :], xh[:, p, :], start=True, stop=False)
                    pe.matmul(bank, w1l[:, n, :], xh[:, p, :], start=False, stop=False)
                    pe.matmul(bank, w1h[:, n, :], xl[:, p, :], start=False, stop=True).then_inc(up_done, 1)

            def downs(g, e):
                wait(pe, hid_done, NE * KC * g + (e + 1) * KC)
                wait(pe, added, NE * g + e - 1)
                for j in range(GT):
                    for k in range(KC):
                        n = e * KC + k
                        last = pe.matmul(dn[e % 2][:, j * C:(j + 1) * C], hid[:, n, j * P:(j + 1) * P], w2[:, n, :],
                                         start=(k == 0), stop=(k == KC - 1))
                last.then_inc(down_done, 1)

            def step(g, p, last):
                for e in range(1, NE):
                    if isinstance(g, int) and g == 0:
                        wait(pe, w_low, e + 1)
                    ups(g, p, e)
                    if e == NE - 1 and not last:
                        gates(g + 1, 1 - p)
                    downs(g, e - 1)
                    if e == NE - 2 and not last:
                        turn(g + 1)
                if not last:
                    ups(g + 1, 1 - p, 0)
                downs(g, NE - 1)

            pe.wait_ge(T["moe_in"][layer], 64)
            turn(0)
            gates(0, 0)
            pe.wait_ge(w_low, 1)
            ups(0, 0, 0)
            steps(pe, step)


def l1_attention(nc, T, A):
    X, ident = T["X"], T["ident"]
    H, NB = HEADS, NI
    VW, VWIDE = DH + 1, 2 * DH
    VROW = (H - 1) * VW + VWIDE
    with ExitStack() as ctx:
        s = Scope(nc, ctx, "l1c")
        wqk, wv, wp, sp_, wo, wx, low, sel = (T[f"l1_{n}"] for n in ("wqk", "wv", "wp", "sp", "wo", "wx", "low", "sel"))
        selr = s.sb("selr", [P, H, P], F32R)
        wh, wl = (s.sb(n, [P, 2, SG, P], F32R) for n in ("wh", "wl"))
        xn = s.sb("xn", [P, 2, P])
        xi = s.sb("xi", [P, PIX])
        xh, xs, xl = (s.sb(n, [P, PIX], F32R) for n in ("xh", "xs", "xl"))
        high = s.sb("high", [P, 3, 2 * PIX], F32R)
        qk = s.sb("qk", [P, 2, 3, 2 * PIX], F32R)
        vs = s.sb("vs", [P, 2, 2, VROW])
        nmax = s.sb("nmax", [P, 2, 2 * H])
        nmh = s.sb("nmh", [2 * H, PIX], F32R)
        nms = s.sb("nms", [P, PIX], F32R)
        pt = s.sb("pt", [P, 2, 2 * PIX])
        rinv = s.sb("rinv", [P, 2 * H])
        ro = s.sb("ro", [P, 2, H * DH])
        rt = s.sb("rt", [C, 2, PIX])
        u = s.sb("u", [DS, PIX])
        y0 = s.sb("y0", [P, 2, 2 * C])
        y1 = s.sb("y1", [P, 2 * C])
        stats = s.sb("stats", [P, 2, 6])
        mean = s.sb("mean", [P, 2])
        var = s.sb("var", [P, 2])
        rstd = s.sb("rstd", [P, 2])
        mhalf = s.sb("mhalf", [P, 2])
        sc_ps = [s.psum(f"sc{i}", [P, 512]) for i in range(2)]
        st_ps = [s.psum(f"st{i}", [P, 512]) for i in range(2)]
        o_ps = [s.psum(f"o{i}", [P, 512]) for i in range(2)]
        m1 = s.psum("m1", [P, 512])
        m2 = s.psum("m2", [P, 512])
        names = ("consts", "ready", "w_high", "w_low", "x_high", "x_low",
                 "var_done", "rstd_done", "dve_step", "xn_done", "tok_in", "xi_done",
                 "unit_in", "unit_high", "unit_done", "v_in", "v_done", "x_in", "x_done", "scored", "maxed",
                 "max_done", "nm_in", "nm_high", "nm_done", "st_in", "exped", "valued", "ro_done", "ht_in",
                 "ht_done", "wp_in", "wp_done", "wo_in", "wo_done")
        S = {n: s.sem(n) for n in names}
        block = ctx.enter_context(nc.Block())
        def images(eng, body, tail=1):
            for b in range(3):
                body(b, b % 2)
            with eng.Fori(1, (NB - tail - 1) // 2) as i:
                body(2 * i + 1, 1)
                body(2 * i + 2, 0)
            for b in range(NB - tail, NB):
                body(b, b % 2)

        def is_last(b, n=1):
            return isinstance(b, int) and b >= NB - n

        def operand(kind, b_par, h):
            g, lo = h // 2, KS3 * (h % 2)
            unit, col = (kind, g * PIX) if g < 2 else (2, kind * PIX)
            return qk[lo:lo + KS3, b_par, unit, col:col + PIX]

        @block.gpsimd
        def _(pool):
            pool.memset(mhalf[:, :], -0.5).then_inc(S["consts"], 1)
            pool.wait_ge(S["consts"], 1)
            with pool.Fori(0, NB) as b:
                pool.wait_ge(S["var_done"], b + 1)
                pool.tensor_tensor(rstd[:, :], var[:, :], mhalf[:, :], ALU.pow).then_inc(S["rstd_done"], 1)

        @block.vector
        def _(dve):
            EACH = 5 + 2 + 2

            def ln_stats(b, chain):
                layernorm_stats(dve, chain, [X[:, 2 * b + t, :] for t in range(2)], stats, mean, var, 1e-6)
                dve.sem_inc(S["var_done"], 1)

            def ln_apply(b, chain):
                wait(dve, S["rstd_done"], b + 1)
                wait(dve, S["tok_in"], b)
                chain.sync(layernorm_apply(dve, chain, [X[:, 2 * b + t, :] for t in range(2)],
                                           [xn[:, t, 0:C] for t in range(2)], stats, mean, rstd))
                dve.tensor_scalar(xn[:, :, C:CT], xn[:, :, C - DS:C], 1.0, None, ALU.mult
                                  ).then_inc(S["xn_done"], 1)

            def tokens_low(b):
                wait(dve, S["x_high"], b + 1)
                wait(dve, S["x_in"], b)
                dve.scalar_tensor_tensor(out=xs[:, :], in0=xh[:, :].bitcast(F32), scalar=low[:, 3:4],
                                         in1=xi[:, :], op0=ALU.mult, op1=ALU.add)
                dve.scalar_tensor_tensor(out=xl[:, :], in0=xh[:, :].bitcast(F32), scalar=-1.0,
                                         in1=xi[:, :], op0=ALU.mult, op1=ALU.add).then_inc(S["x_low"], 1)

            def row_max(b, h):
                wait(dve, S["scored"], H * b + h + 1)
                if h == 0:
                    wait(dve, S["nm_in"], b)
                dve.tensor_reduce(nmax[:, :, h], sc_ps[h % 2][:, :].rearrange("p (t m) -> p t m", t=2),
                                  AX.X, ALU.max, negate=True).then_inc(S["maxed"], 1)

            def maxima(b):
                wait(dve, S["maxed"], H * (b + 1))
                dve.tensor_scalar(nmax[:, :, H:2 * H], nmax[:, :, 0:H], 1.0, None, ALU.mult
                                  ).then_inc(S["max_done"], 1)

            def maxima_low(b):
                wait(dve, S["nm_high"], b + 1)
                wait(dve, S["st_in"], H * b)
                dve.scalar_tensor_tensor(out=nms[0:2 * H, :], in0=nmh[:, :].bitcast(F32), scalar=low[0:2 * H, 2:3],
                                         in1=m1[0:2 * H, 0:PIX], op0=ALU.mult, op1=ALU.add
                                         ).then_inc(S["nm_done"], 1)

            def unit_low(b, p, n):
                wait(dve, S["unit_high"], 3 * b + n + 1)
                if n == 0:
                    wait(dve, S["st_in"], H * (b - 1))
                bank = (m2, m1, m2)[n]
                for c in range(2) if n == 2 else (slice(0, 2),):
                    cols = slice(c * PIX, (c + 1) * PIX) if n == 2 else slice(0, 2 * PIX)
                    kind = c if n == 2 else n
                    last = dve.scalar_tensor_tensor(out=qk[:, p, n, cols], in0=high[:, n, cols].bitcast(F32),
                                                    scalar=low[:, kind:kind + 1], in1=bank[:, cols],
                                                    op0=ALU.mult, op1=ALU.add)
                last.then_inc(S["unit_done"], 1)

            def norm_heads(b, p, chain):
                wait(dve, S["valued"], H * (b + 1))
                wait(dve, S["ht_in"], b)
                o = o_ps[p][:, 0:2 * H * VW].rearrange("p (h d) -> p h d", d=VW)
                chain.sync(dve.reciprocal(rinv[:, :], o[:, :, DH]))
                for t in range(2):
                    half = slice(t, 2 * H, 2)
                    last = dve.scalar_tensor_tensor(out=ro[:, t, :].rearrange("p (h d) -> p h d", h=H),
                                                    in0=o[:, half, 0:DH], scalar=0.0,
                                                    in1=rinv[:, half].unsqueeze(2).broadcast_to([P, H, DH]),
                                                    op0=ALU.max, op1=ALU.mult)
                last.then_inc(S["ro_done"], 1)

            def wp_out(b):
                wait(dve, S["wp_in"], b + 1)
                dve.tensor_scalar(u[:, :], m2[0:DS, 0:PIX], sp_[:, 0:1], sp_[:, 1:2], ALU.mult, ALU.add
                                  ).then_inc(S["wp_done"], 1)

            def wo_out(b, p, chain):
                wait(dve, S["wo_in"], b + 1)
                wait(dve, S["x_done"], b + 1)
                chain.sync(dve.tensor_tensor(y1[:, :], m2[:, 0:2 * C], y0[:, p, :], ALU.add))
                x = X[:, bass.ds(2 * b, 2), :].rearrange("p t c -> p (t c)")
                dve.scalar_tensor_tensor(out=x, in0=y1[:, :], scalar=0.0, in1=x, op0=ALU.max, op1=ALU.add
                                         ).then_inc(S["wo_done"], 1)

            def body(b, p):
                first = isinstance(b, int) and b == 0
                chain = Chain(dve, S["dve_step"], base + b * EACH - (7 if is_last(b) else 0))
                maxima_low(b)
                if not is_last(b):
                    unit_low(b + 1, 1 - p, 0)
                if not first:
                    norm_heads(b - 1, 1 - p, chain)
                else:
                    chain.sync(dve.tensor_scalar(rinv[:, :], rinv[:, :], 1.0, None, ALU.mult))
                if not is_last(b):
                    unit_low(b + 1, 1 - p, 1)
                    unit_low(b + 1, 1 - p, 2)
                if not is_last(b, 2):
                    ln_stats(b + 2, chain)
                if not is_last(b, 2):
                    ln_apply(b + 2, chain)
                if not is_last(b):
                    row_max(b + 1, 0)
                    row_max(b + 1, 1)
                if not first:
                    wp_out(b - 1)
                if not is_last(b):
                    row_max(b + 1, 2)
                    row_max(b + 1, 3)
                if not first:
                    wo_out(b - 1, 1 - p, chain)
                else:
                    chain.sync(dve.tensor_scalar(rinv[:, :], rinv[:, :], 1.0, None, ALU.mult))
                if not is_last(b):
                    row_max(b + 1, 4)
                    row_max(b + 1, 5)
                    maxima(b + 1)
                if not is_last(b, 2):
                    tokens_low(b + 2)

            dve.memset(rinv[:, :], 1.0)
            dve.memset(vs[:, :, :, :], 1.0)
            chain = Chain(dve, S["dve_step"])
            chain.sync(dve.memset(xn[:, :, CT:P], 0.0))
            dve.memset(xn[:, :, CT:CT + 1], 1.0)
            ln_stats(0, chain)
            dve.wait_ge(S["w_high"], 1)
            dve.scalar_tensor_tensor(out=wl[:, :, :, :].rearrange("p a g n -> p (a g n)"),
                                     in0=wh[:, :, :, :].rearrange("p a g n -> p (a g n)").bitcast(F32), scalar=-1.0,
                                     in1=wqk[:, :, :, :].rearrange("p a g n -> p (a g n)"),
                                     op0=ALU.mult, op1=ALU.add).then_inc(S["w_low"], 1)
            ln_apply(0, chain)
            tokens_low(0)
            dve.tensor_copy(selr[:, :, :], sel[:, :, :])
            dve.tensor_copy(nms[:, :], sel[:, 0:2, :].rearrange("p h n -> p (h n)")).then_inc(S["ready"], 1)
            for n in range(3):
                unit_low(0, 0, n)
            ln_stats(1, chain)
            ln_apply(1, chain)
            for h in range(H):
                row_max(0, h)
            maxima(0)
            tokens_low(1)
            base = chain.n
            images(dve, body, tail=3)
            last = Chain(dve, S["dve_step"], base + NB * EACH - 2 * 7)
            norm_heads(NB - 1, 1, last)
            wp_out(NB - 1)
            wo_out(NB - 1, 1, last)

        @block.scalar
        def _(act):
            def tokens_out(b):
                wait(act, S["tok_in"], b + 1)
                wait(act, S["x_low"], b)
                wait(act, S["x_in"], b)
                act.activation(xi[:, :], m2[:, 0:PIX], ACT.Copy).then_inc(S["xi_done"], 1)
                wait(act, S["xi_done"], b + 1)
                act.activation(xh[:, :], xi[:, :], ACT.Copy).then_inc(S["x_high"], 1)

            def unit_high(b, n):
                wait(act, S["unit_in"], 3 * b + n + 1)
                wait(act, S["unit_done"], 3 * (b - 1) + n + 1)
                act.activation(high[:, n, :], (m2, m1, m2)[n][:, :], ACT.Copy).then_inc(S["unit_high"], 1)

            def maxima_high(b):
                wait(act, S["nm_in"], b + 1)
                wait(act, S["nm_done"], b)
                act.activation(nmh[:, :], m1[0:2 * H, 0:PIX], ACT.Copy).then_inc(S["nm_high"], 1)

            def values_out(b, p):
                wait(act, S["v_in"], b + 1)
                wait(act, S["valued"], H * (b - 1))
                for m in range(2):
                    last = act.activation(vs[:, p, m, 0:H * VW].rearrange("p (h d) -> p h d", d=VW)[:, :, 0:DH],
                                          m2[:, m * H * DH:(m + 1) * H * DH].rearrange("p (h d) -> p h d", d=DH),
                                          ACT.Copy)
                last.then_inc(S["v_done"], 1)

            def residual_out(b, p):
                wait(act, S["x_in"], b + 1)
                wait(act, S["wo_done"], b - 1)
                act.activation(y0[:, p, :], m1[:, 0:2 * C], ACT.Copy).then_inc(S["x_done"], 1)

            def heads_out(b):
                wait(act, S["ht_in"], b + 1)
                wait(act, S["wp_in"], b)
                act.activation(rt[:, :, :].rearrange("p a n -> p (a n)"), m1[0:C, :], ACT.Copy
                               ).then_inc(S["ht_done"], 1)

            def exps(b, h):
                n = H * b + h
                wait(act, S["st_in"], n + 1)
                wait(act, S["valued"], n - 1)
                act.activation(pt[:, h % 2, :], st_ps[h % 2][:, :], ACT.Exp).then_inc(S["exped"], 1)

            def body(b, p):
                first = isinstance(b, int) and b == 0
                maxima_high(b)
                if not is_last(b):
                    unit_high(b + 1, 0)
                exps(b, 0)
                if not is_last(b):
                    unit_high(b + 1, 1)
                exps(b, 1)
                if not is_last(b):
                    unit_high(b + 1, 2)
                exps(b, 2)
                if not is_last(b):
                    values_out(b + 1, 1 - p)
                if not first:
                    heads_out(b - 1)
                exps(b, 3)
                exps(b, 4)
                exps(b, 5)
                if not is_last(b):
                    residual_out(b + 1, 1 - p)
                if not is_last(b, 2):
                    tokens_out(b + 2)

            act.activation(wh[:, :, :, :].rearrange("p a g n -> p (a g n)"),
                           wqk[:, :, :, :].rearrange("p a g n -> p (a g n)"), ACT.Copy).then_inc(S["w_high"], 1)
            tokens_out(0)
            for n in range(3):
                unit_high(0, n)
            values_out(0, 0)
            residual_out(0, 0)
            tokens_out(1)
            images(act, body, tail=3)
            heads_out(NB - 1)

        @block.tensor
        def _(pe):
            def turn_tokens(b):
                wait(pe, S["xn_done"], b + 1)
                wait(pe, S["v_done"], b)
                wait(pe, S["wo_done"], b - 2)
                for t in range(2):
                    last = pe.transpose(m2[:, t * P:(t + 1) * P], xn[:, t, :], ident[:, :])
                last.then_inc(S["tok_in"], 1)

            def unit(b, n):
                if n == 0:
                    wait(pe, S["w_low"], 1)
                    wait(pe, S["x_low"], b + 1)
                elif n == 1:
                    wait(pe, S["nm_done"], b)
                else:
                    wait(pe, S["unit_done"], 3 * b + 1)
                for c in range(2):
                    kind, g = ((0, c), (1, c), (c, 2))[n]
                    passes = [(wh, xs), (wl, xs), (wh, xl)][0:2 + kind]
                    for i, (w, x) in enumerate(passes):
                        last = pe.matmul((m2, m1, m2)[n][:, c * PIX:(c + 1) * PIX], w[:, kind, g, :], x[:, :],
                                         start=(i == 0), stop=(i == len(passes) - 1))
                last.then_inc(S["unit_in"], 1)

            def value_tokens(b):
                wait(pe, S["unit_done"], 3 * (b + 1))
                for t in range(2):
                    last = pe.matmul(m2[:, t * H * DH:(t + 1) * H * DH], xi[0:CT + 1, t * P:(t + 1) * P], wv[:, :],
                                     start=True, stop=True)
                last.then_inc(S["v_in"], 1)

            def residual(b):
                wait(pe, S["unit_done"], 3 * (b + 1))
                wait(pe, S["ht_done"], b - 1)
                for t in range(2):
                    last = pe.matmul(m1[:, t * C:(t + 1) * C], xi[0:CT + 1, t * P:(t + 1) * P], wx[:, :],
                                     start=True, stop=True)
                last.then_inc(S["x_in"], 1)

            def scores(b, p, h):
                if h == 0:
                    wait(pe, S["unit_done"], 3 * (b + 1))
                wait(pe, S["maxed"], H * b + h - 1)
                for t in range(2):
                    last = pe.matmul(sc_ps[h % 2][:, t * PIX:(t + 1) * PIX], operand(0, p, h)[:, t * P:(t + 1) * P],
                                     operand(1, p, h), start=True, stop=True)
                last.then_inc(S["scored"], 1)

            def turn_maxima(b):
                wait(pe, S["max_done"], b + 1)
                wait(pe, S["x_done"], b + 1)
                for t in range(2):
                    last = pe.transpose(m1[0:2 * H, t * P:(t + 1) * P], nmax[:, t, :], ident[:, :])
                last.then_inc(S["nm_in"], 1)

            def turned_scores(b, p, h):
                if h == 0:
                    wait(pe, S["nm_done"], b + 1)
                wait(pe, S["exped"], H * b + h - 1)
                for m in range(2):
                    out = st_ps[h % 2][:, m * PIX:(m + 1) * PIX]
                    pe.matmul(out, operand(1, p, h)[:, m * P:(m + 1) * P], operand(0, p, h), start=True, stop=False)
                    last = pe.matmul(out, selr[:, h, :], nms[:, :], start=False, stop=True)
                last.then_inc(S["st_in"], 1)

            def values(b, p, h):
                wait(pe, S["exped"], H * b + h + 1)
                if h == 0:
                    wait(pe, S["v_done"], b + 1)
                    wait(pe, S["ro_done"], b - 1)
                for t in range(2):
                    for m in range(2):
                        at = (2 * h + t) * VW
                        last = pe.matmul(o_ps[p][:, at:at + VWIDE], pt[:, h % 2, m * PIX + t * P:m * PIX + (t + 1) * P],
                                         vs[:, p, m, h * VW:h * VW + VWIDE], start=(m == 0), stop=(m == 1))
                last.then_inc(S["valued"], 1)

            def turn_heads(b):
                wait(pe, S["ro_done"], b + 1)
                wait(pe, S["nm_done"], min(b + 2, NB) if isinstance(b, int) else b + 2)
                wait(pe, S["unit_done"], 3 * min(b + 3, NB) if isinstance(b, int) else 3 * (b + 3))
                wait(pe, S["ht_done"], b)
                for a in range(2):
                    for t in range(2):
                        last = pe.transpose(m1[0:C, a * PIX + t * P:a * PIX + (t + 1) * P],
                                            ro[:, t, a * C:(a + 1) * C], ident[:, :])
                last.then_inc(S["ht_in"], 1)

            def mix_heads(b):
                wait(pe, S["ht_done"], b + 1)
                wait(pe, S["v_done"], min(b + 3, NB) if isinstance(b, int) else b + 3)
                wait(pe, S["wo_done"], b)
                for a in range(2):
                    last = pe.matmul(m2[0:DS, 0:PIX], wp[:, a, :], rt[:, a, :], start=(a == 0), stop=(a == 1))
                last.then_inc(S["wp_in"], 1)

            def mix_out(b):
                wait(pe, S["wp_done"], b + 1)
                for t in range(2):
                    last = pe.matmul(m2[:, t * C:(t + 1) * C], u[:, t * P:(t + 1) * P], wo[:, :], start=True,
                                     stop=True)
                last.then_inc(S["wo_in"], 1)

            def body(b, p):
                first, last = isinstance(b, int) and b == 0, is_last(b)
                turn_maxima(b)
                if not first:
                    values(b - 1, 1 - p, H - 1)
                if not last:
                    unit(b + 1, 0)
                turned_scores(b, p, 0)
                if not last:
                    unit(b + 1, 1)
                turned_scores(b, p, 1)
                if not last:
                    unit(b + 1, 2)
                values(b, p, 0)
                turned_scores(b, p, 2)
                values(b, p, 1)
                if not last:
                    value_tokens(b + 1)
                if not first:
                    turn_heads(b - 1)
                turned_scores(b, p, 3)
                if not last:
                    scores(b + 1, 1 - p, 0)
                    scores(b + 1, 1 - p, 1)
                values(b, p, 2)
                if not first:
                    mix_heads(b - 1)
                turned_scores(b, p, 4)
                if not last:
                    scores(b + 1, 1 - p, 2)
                    scores(b + 1, 1 - p, 3)
                values(b, p, 3)
                if not first:
                    mix_out(b - 1)
                turned_scores(b, p, 5)
                if not last:
                    scores(b + 1, 1 - p, 4)
                    scores(b + 1, 1 - p, 5)
                    residual(b + 1)
                if not is_last(b, 2):
                    turn_tokens(b + 2)
                values(b, p, 4)

            turn_tokens(0)
            for n in range(3):
                unit(0, n)
            value_tokens(0)
            residual(0)
            turn_tokens(1)
            for h in range(H):
                scores(0, 0, h)
            pe.wait_ge(S["ready"], 1)
            images(pe, body, tail=3)
            values(NB - 1, 1, H - 1)
            turn_heads(NB - 1)
            mix_heads(NB - 1)
            mix_out(NB - 1)


NH2, HC2 = 12, 32
KSIDE = SIDE // 2
KPIX = KSIDE * KSIDE
QP = PIX // 4
KP = KPIX // 4
HG = P // HC2
N3 = NH2 // HG
PAD = SIDE + 2
L2_LN_EPS = 1e-5
L2_SCALE = HC2 ** -0.5


def l2_sample(nc, T, A, R):
    X, ident = T["X"], T["ident"]
    Q, K, V = R["Q"], R["K"], R["V"]
    TAPS = KS * KS
    with ExitStack() as ctx:
        s = Scope(nc, ctx, "l2s")
        taps, bias, lnp, woff, ref, coord = (T[f"l2_{n}"] for n in ("taps", "bias", "lnp", "woff", "ref", "coord"))
        diag = s.sb("diag", [P, 3, TAPS, C])
        xn = s.sb("xn", [P, 2, C])
        xp = s.sb("xp", [P, 2, PAD, PAD])
        val = s.sb("val", [C, 2, PIX])
        off = s.sb("off", [C, P])
        on = s.sb("on", [P, C])
        og = s.sb("og", [C, KPIX])
        pos = s.sb("pos", [P, 2, KPIX])
        th = s.sb("th", [P, 2, KPIX])
        dist = s.sb("dist", [P, 3, KPIX])
        hat = s.sb("hat", [P, 3, KPIX])
        bil = s.sb("bil", [P, 2, KPIX])
        vt = s.sb("vt", [P, 2, C])
        stats = s.sb("stats", [P, 2, 6])
        mean = s.sb("mean", [P, 2])
        var = s.sb("var", [P, 2])
        rstd = s.sb("rstd", [P, 2])
        ostats = s.sb("ostats", [P, 1, 6])
        omean = s.sb("omean", [P, 1])
        ovar = s.sb("ovar", [P, 1])
        orstd = s.sb("orstd", [P, 1])
        mhalf = s.sb("mhalf", [P, 2])
        tp, qp, kp, op, fp, gp, vp, sp_ = (s.psum(n, [P, 512]) for n in
                                           ("tp", "qp", "kp", "op", "fp", "gp", "vp", "sp"))
        names = ("consts", "tap_done", "diag_done", "var_done", "rstd_done", "ovar_done", "orstd_done", "dve_step",
                 "xn_done", "turned", "xp_done", "q_in", "q_out", "k_in", "k_out", "off_in", "off_out",
                 "on_in", "on_done", "og_in", "og_out", "pos_in", "pos_out", "th_done", "dist_done", "hat_done",
                 "bil_done", "val_done", "vt_in", "vt_out", "smp_in", "smp_out")
        S = {n: s.sem(n) for n in names}
        block = ctx.enter_context(nc.Block())
        @block.gpsimd
        def _(pool):
            pool.memset(xp[:, :, :, :], 0.0)
            pool.memset(off[:, :], 0.0)
            pool.memset(on[:, :], 0.0)
            pool.memset(mhalf[:, :], -0.5).then_inc(S["consts"], 1)
            pool.wait_ge(S["consts"], 1)
            pool.memset(diag[C:P, :, :, :], 0.0).then_inc(S["consts"], 1)
            pool.wait_ge(S["consts"], 2)

            def tokens_rstd(b):
                wait(pool, S["var_done"], b + 1)
                pool.tensor_tensor(rstd[:, :], var[:, :], mhalf[:, :], ALU.pow).then_inc(S["rstd_done"], 1)

            def offsets_rstd(b):
                wait(pool, S["ovar_done"], b + 1)
                pool.tensor_tensor(orstd[0:KPIX, :], ovar[0:KPIX, :], mhalf[0:KPIX, 0:1], ALU.pow
                                   ).then_inc(S["orstd_done"], 1)

            tokens_rstd(0)
            with pool.Fori(0, NI - 1) as b:
                offsets_rstd(b)
                tokens_rstd(b + 1)
            offsets_rstd(NI - 1)

        STATS, APPLY, TAPS_A, TAPS_B = 4, 2, 4, 3
        EACH = TAPS_A + STATS + TAPS_B + APPLY

        def images(eng, body):
            body(0, 0, False)
            body(1, 1, False)
            body(2, 0, False)
            with eng.Fori(1, NI // 2 - 1) as i:
                body(2 * i + 1, 1, False)
                body(2 * i + 2, 0, False)
            body(NI - 1, 1, True)

        @block.vector
        def _(dve):
            def ln_stats(b, chain):
                layernorm_stats(dve, chain, [X[:, 2 * b + t, :] for t in range(2)], stats, mean, var, 1e-6)
                dve.sem_inc(S["var_done"], 1)

            def ln_apply(b, chain):
                wait(dve, S["rstd_done"], b + 1)
                wait(dve, S["turned"], b)
                layernorm_apply(dve, chain, [X[:, 2 * b + t, :] for t in range(2)], [xn[:, t, :] for t in range(2)],
                                stats, mean, rstd).then_inc(S["xn_done"], 1)

            def bilinear(b):
                wait(dve, S["hat_done"], b + 1)
                wait(dve, S["smp_in"], b)
                dve.tensor_tensor(bil[:, :, :], hat[:, 1:3, :],
                                  hat[:, 0, :].unsqueeze(1).broadcast_to([P, 2, KPIX]), ALU.mult
                                  ).then_inc(S["bil_done"], 1)

            def values_out(b):
                wait(dve, S["vt_in"], b + 1)
                wait(dve, S["smp_in"], b)
                dve.tensor_scalar(vt[:, :, :].rearrange("p t c -> p (t c)"), vp[:, 0:2 * C], 1.0, None, ALU.mult
                                  ).then_inc(S["vt_out"], 1)

            def body(b, p, last):
                chain = Chain(dve, S["dve_step"], STATS + APPLY + b * (STATS + APPLY + EACH))
                wait(dve, S["tap_done"], b + 1)
                v3 = val[:, p, :].rearrange("c (y x) -> c y x", x=SIDE)
                for t in range(1, TAPS):
                    image = xp[0:C, p, t // KS:t // KS + SIDE, t % KS:t % KS + SIDE]
                    ins = dve.scalar_tensor_tensor(out=v3, in0=image, scalar=taps[:, 3, t:t + 1], in1=v3,
                                                   op0=ALU.mult, op1=ALU.add)
                    if t < TAPS - 1:
                        chain.sync(ins)
                    if t == TAPS_A:
                        if not (isinstance(b, int) and b == 0):
                            values_out(b - 1)
                            bilinear(b - 1)
                        wait(dve, S["on_in"], b + 1)
                        layernorm_stats(dve, chain, [fp[0:KPIX, 0:C]], ostats, omean, ovar, L2_LN_EPS, KPIX)
                        dve.sem_inc(S["ovar_done"], 1)
                        if not last:
                            ln_stats(b + 1, chain)
                        wait(dve, S["orstd_done"], b + 1)
                        layernorm_apply(dve, chain, [fp[0:KPIX, 0:C]], [on[0:KPIX, :]], ostats, omean, orstd, KPIX
                                        ).then_inc(S["on_done"], 1)
                        if not last:
                            ln_apply(b + 1, chain)
                ins.then_inc(S["val_done"], 1)
                wait(dve, S["pos_in"], b + 1)
                dve.tensor_tensor(pos[:, :, :], gp[:, 0:2 * KPIX].rearrange("p (a n) -> p a n", a=2), ref[:, :, :],
                                  ALU.add).then_inc(S["pos_out"], 1)
                assert chain.n == EACH + (0 if last else STATS + APPLY) - 0, chain.n

            dve.wait_ge(S["consts"], 1)
            chain = Chain(dve, S["dve_step"])
            ln_stats(0, chain)
            ln_apply(0, chain)
            for w in range(3):
                for t in range(TAPS):
                    ins = dve.tensor_scalar(diag[0:C, w, t, :], ident[0:C, 0:C], taps[:, w, t:t + 1], None, ALU.mult)
            ins.then_inc(S["diag_done"], 1)
            images(dve, body)
            values_out(NI - 1)
            bilinear(NI - 1)

        @block.scalar
        def _(act):
            def tokens_out(b, p):
                wait(act, S["turned"], b + 1)
                wait(act, S["k_in"], b - 1)
                wait(act, S["val_done"], b - 1)
                act.activation(xp[0:C, p, 1:SIDE + 1, 1:SIDE + 1],
                               tp[0:C, 0:PIX].rearrange("c (y x) -> c y x", x=SIDE), ACT.Copy
                               ).then_inc(S["xp_done"], 1)

            def first_tap(b, p):
                wait(act, S["xp_done"], b + 1)
                wait(act, S["vt_in"], b - 1)
                act.activation(val[:, p, :].rearrange("c (y x) -> c y x", x=SIDE), xp[0:C, p, 0:SIDE, 0:SIDE],
                               ACT.Identity, scale=taps[:, 3, 0:1], bias=bias[:, 3:4]).then_inc(S["tap_done"], 1)

            def sampled_out(b):
                wait(act, S["smp_in"], b + 1)
                act.activation(V[:, b, :], sp_[0:C, 0:KPIX], ACT.Copy).then_inc(S["smp_out"], 1)

            def body(b, p, last):
                wait(act, S["off_in"], b + 1)
                act.activation(off[:, 0:KPIX], op[0:C, 0:KPIX], ACT.Identity, bias=bias[:, 2:3]
                               ).then_inc(S["off_out"], 1)
                wait(act, S["k_in"], b + 1)
                act.activation(K[:, b, :], kp[0:C, 0:KPIX], ACT.Identity, bias=bias[:, 1:2]
                               ).then_inc(S["k_out"], 1)
                if not (isinstance(b, int) and b == 0):
                    sampled_out(b - 1)
                wait(act, S["q_in"], b + 1)
                act.activation(Q[:, b, :], qp[0:C, 0:PIX], ACT.Identity, bias=bias[:, 0:1]
                               ).then_inc(S["q_out"], 1)
                wait(act, S["og_in"], b + 1)
                act.activation(og[:, :], fp[0:C, 0:KPIX], ACT.Gelu, scale=lnp[:, 0:1], bias=lnp[:, 1:2]
                               ).then_inc(S["og_out"], 1)
                if not last:
                    tokens_out(b + 1, 1 - p)
                    first_tap(b + 1, 1 - p)
                wait(act, S["pos_out"], b + 1)
                act.activation(th[:, :, :], pos[:, :, :], ACT.Tanh).then_inc(S["th_done"], 1)
                wait(act, S["th_done"], b + 1)
                for k, comp in enumerate((0, 1, 1)):
                    ins = act.activation(dist[:, k, :], th[:, comp, :], ACT.Abs, scale=(SIDE - 1) / 2,
                                         bias=coord[:, k:k + 1])
                ins.then_inc(S["dist_done"], 1)
                wait(act, S["dist_done"], b + 1)
                wait(act, S["bil_done"], b)
                act.activation(hat[:, :, :], dist[:, :, :], ACT.Relu, scale=-1.0, bias=1.0
                               ).then_inc(S["hat_done"], 1)

            act.wait_ge(S["consts"], 1)
            tokens_out(0, 0)
            first_tap(0, 0)
            images(act, body)
            sampled_out(NI - 1)

        @block.tensor
        def _(pe):
            def turn(b):
                wait(pe, S["xn_done"], b + 1)
                wait(pe, S["xp_done"], b)
                for t in range(2):
                    ins = pe.transpose(tp[0:C, t * P:(t + 1) * P], xn[:, t, :], ident[:, :])
                ins.then_inc(S["turned"], 1)

            def conv(out, w, p, stride, done):
                side = SIDE // stride
                o = out[0:C, 0:side * side].rearrange("c (y x) -> c y x", x=side)
                for t in range(TAPS):
                    dy, dx = t // KS, t % KS
                    ins = pe.matmul(o, diag[:, w, t, :], xp[:, p, dy:dy + SIDE:stride, dx:dx + SIDE:stride],
                                    start=(t == 0), stop=(t == TAPS - 1))
                ins.then_inc(done, 1)

            def sample(b):
                wait(pe, S["vt_out"], b + 1)
                wait(pe, S["bil_done"], b + 1)
                wait(pe, S["smp_out"], b)
                for t in range(2):
                    ins = pe.matmul(sp_[0:C, 0:KPIX], vt[:, t, :], bil[:, t, :], start=(t == 0), stop=(t == 1))
                ins.then_inc(S["smp_in"], 1)

            def turn_values(b, p):
                wait(pe, S["val_done"], b + 1)
                wait(pe, S["vt_out"], b)
                for t in range(2):
                    ins = pe.transpose(vp[:, t * C:(t + 1) * C], val[:, p, t * P:(t + 1) * P], ident[0:C, 0:C])
                ins.then_inc(S["vt_in"], 1)

            def body(b, p, last):
                if not (isinstance(b, int) and b == 0):
                    turn_values(b - 1, 1 - p)
                wait(pe, S["xp_done"], b + 1)
                wait(pe, S["off_out"], b)
                conv(op, 2, p, 2, S["off_in"])
                wait(pe, S["k_out"], b)
                conv(kp, 1, p, 2, S["k_in"])
                wait(pe, S["off_out"], b + 1)
                pe.transpose(fp[:, 0:C], off[:, :], ident[0:C, 0:C]).then_inc(S["on_in"], 1)
                if not (isinstance(b, int) and b == 0):
                    sample(b - 1)
                wait(pe, S["q_out"], b)
                conv(qp, 0, p, 1, S["q_in"])
                wait(pe, S["on_done"], b + 1)
                pe.transpose(fp[0:C, 0:P], on[:, :], ident[:, :]).then_inc(S["og_in"], 1)
                if not last:
                    turn(b + 1)
                wait(pe, S["og_out"], b + 1)
                wait(pe, S["pos_out"], b)
                for k in range(2):
                    ins = pe.matmul(gp[:, k * KPIX:(k + 1) * KPIX], woff[:, k, :], og[:, :], start=True, stop=True)
                ins.then_inc(S["pos_in"], 1)

            turn(0)
            pe.wait_ge(S["diag_done"], 1)
            pe.wait_ge(S["consts"], 2)
            images(pe, body)
            turn_values(NI - 1, 1)
            sample(NI - 1)


def l2_mix(nc, T, A, R):
    X, ident = T["X"], T["ident"]
    Q, K, V = R["Q"], R["K"], R["V"]
    with ExitStack() as ctx:
        s = Scope(nc, ctx, "l2m")
        mask, wout = T["l2_mask"], T["l2_wout"]
        qr = s.sb("qr", [P, NI, N3, QP])
        kr = s.sb("kr", [P, NI, N3, KP])
        vr = s.sb("vr", [P, NI, N3, KP])
        orow = s.sb("orow", [P, NI, N3, QP])
        oc = s.sb("oc", [C, NI, PIX])
        kb = s.sb("kb", [P, 2, N3, HG, KP])
        vb = s.sb("vb", [P, 2, N3, HG, KP])
        vbt = s.sb("vbt", [HG * KP, 2, N3 * P])
        at = s.sb("at", [HG * KP, 2, N3 * QP])
        vp = [s.psum(f"vp{i}", [P, 512]) for i in range(2)]
        ap_ = [s.psum(f"ap{i}", [P, 512]) for i in range(2)]
        op = [s.psum(f"op{i}", [P, 512]) for i in range(2)]
        yp = [s.psum(f"yp{i}", [P, 512]) for i in range(2)]
        names = ("moved_dve", "moved_act", "moved_pool", "kb_done", "vb_done", "vbt_in", "vbt_out",
                 "at_in", "at_out", "o_in", "o_out", "back_dve", "back_act", "y_in", "y_out")
        S = {n: s.sem(n) for n in names}
        block = ctx.enter_context(nc.Block())
        PARTS = [(g, j) for g in range(N3) for j in range(4)]

        def rows(t, g, j, n):
            return t[HC2 * j:HC2 * (j + 1), :, g, 0:n]

        def chans(t, g, j, n):
            return t[HC2 * g:HC2 * (g + 1), :, n * j:n * (j + 1)]

        @block.gpsimd
        def _(pool):
            for g, j in PARTS[0:6]:
                ins = pool.tensor_copy(rows(vr, g, j, KP), chans(V, g, j, KP))
            ins.then_inc(S["moved_pool"], 1)

        @block.vector
        def _(dve):
            for g, j in PARTS:
                dve.tensor_copy(rows(kr, g, j, KP), chans(K, g, j, KP))
            for g, j in PARTS[6:]:
                dve.tensor_copy(rows(vr, g, j, KP), chans(V, g, j, KP))
            for g, j in PARTS[0:5]:
                ins = dve.tensor_copy(rows(qr, g, j, QP), chans(Q, g, j, QP))
            ins.then_inc(S["moved_dve"], 1)
            dve.wait_ge(S["moved_dve"], 1)
            dve.wait_ge(S["moved_pool"], 1)

            def block_diagonal(out, rows_, b, done):
                dve.tensor_tensor(out, rows_[:, b, :, :].unsqueeze(2).broadcast_to([P, N3, HG, KP]),
                                  mask[:, :].unsqueeze(1).unsqueeze(3).broadcast_to([P, N3, HG, KP]), ALU.mult
                                  ).then_inc(done, 1)

            def blocks(b, p):
                wait(dve, S["vbt_in"], b - 1)
                block_diagonal(vb[:, p, :, :, :], vr, b, S["vb_done"])
                wait(dve, S["at_in"], b - 1)
                block_diagonal(kb[:, p, :, :, :], kr, b, S["kb_done"])

            def values_out(b, p):
                wait(dve, S["vbt_in"], b + 1)
                wait(dve, S["o_in"], b - 1)
                dve.tensor_scalar(vbt[:, p, :], vp[p][0:HG * KP, 0:N3 * P], L2_SCALE, None, ALU.mult
                                  ).then_inc(S["vbt_out"], 1)

            blocks(0, 0)
            for b in range(1, 4):
                blocks(b, b % 2)
                values_out(b - 1, (b - 1) % 2)
            with dve.Fori(2, NI // 2) as i:
                blocks(2 * i, 0)
                values_out(2 * i - 1, 1)
                blocks(2 * i + 1, 1)
                values_out(2 * i, 0)
            values_out(NI - 1, 1)
            dve.wait_ge(S["o_out"], NI)
            for g, j in PARTS[0:7]:
                ins = dve.tensor_copy(chans(oc, g, j, QP), rows(orow, g, j, QP))
            ins.then_inc(S["back_dve"], 1)
            for n in range(NT // GT):
                dve.wait_ge(S["y_in"], n + 1)
                x = X[:, GT * n:GT * (n + 1), :].rearrange("p t c -> p (t c)")
                dve.tensor_tensor(x, yp[n % 2][:, 0:GT * C], x, ALU.add).then_inc(S["y_out"], 1)

        @block.scalar
        def _(act):
            for g, j in PARTS[5:]:
                ins = act.activation(rows(qr, g, j, QP), chans(Q, g, j, QP), ACT.Copy)
            ins.then_inc(S["moved_act"], 1)

            def scores_out(b, p):
                wait(act, S["at_in"], b + 1)
                wait(act, S["o_in"], b - 1)
                act.activation(at[:, p, :], ap_[p][0:HG * KP, 0:N3 * QP], ACT.Copy).then_inc(S["at_out"], 1)

            def outputs_out(b, p):
                wait(act, S["o_in"], b + 1)
                act.activation(orow[:, b, :, :], op[p][:, 0:N3 * QP].rearrange("p (g m) -> p g m", g=N3), ACT.Copy
                               ).then_inc(S["o_out"], 1)

            scores_out(0, 0)
            for b in range(1, 4):
                scores_out(b, b % 2)
                outputs_out(b - 1, (b - 1) % 2)
            with act.Fori(2, NI // 2) as i:
                scores_out(2 * i, 0)
                outputs_out(2 * i - 1, 1)
                scores_out(2 * i + 1, 1)
                outputs_out(2 * i, 0)
            outputs_out(NI - 1, 1)
            act.wait_ge(S["o_out"], NI)
            for g, j in PARTS[7:]:
                ins = act.activation(chans(oc, g, j, QP), rows(orow, g, j, QP), ACT.Copy)
            ins.then_inc(S["back_act"], 1)

        @block.tensor
        def _(pe):
            pe.wait_ge(S["moved_act"], 1)
            pe.wait_ge(S["moved_dve"], 1)

            def scores(b, p):
                wait(pe, S["vb_done"], b + 1)
                wait(pe, S["vbt_out"], b - 1)
                wait(pe, S["kb_done"], b + 1)
                wait(pe, S["at_out"], b - 1)
                for g in range(N3):
                    ins = pe.matmul(ap_[p][0:HG * KP, g * QP:(g + 1) * QP],
                                    kb[:, p, g, :, :].rearrange("p h n -> p (h n)"), qr[:, b, g, :],
                                    start=True, stop=True)
                ins.then_inc(S["at_in"], 1)
                for g in range(N3):
                    ins = pe.transpose(vp[p][0:HG * KP, g * P:(g + 1) * P],
                                       vb[:, p, g, :, :].rearrange("p h n -> p (h n)"), ident[:, :])
                ins.then_inc(S["vbt_in"], 1)

            def outputs(b, p):
                wait(pe, S["at_out"], b + 1)
                wait(pe, S["vbt_out"], b + 1)
                wait(pe, S["o_out"], b - 1)
                for g in range(N3):
                    ins = pe.matmul(op[p][:, g * QP:(g + 1) * QP], vbt[:, p, g * P:(g + 1) * P],
                                    at[:, p, g * QP:(g + 1) * QP], start=True, stop=True)
                ins.then_inc(S["o_in"], 1)

            scores(0, 0)
            for b in range(1, 4):
                scores(b, b % 2)
                outputs(b - 1, (b - 1) % 2)
            with pe.Fori(2, NI // 2) as i:
                scores(2 * i, 0)
                outputs(2 * i - 1, 1)
                scores(2 * i + 1, 1)
                outputs(2 * i, 0)
            outputs(NI - 1, 1)
            pe.wait_ge(S["back_dve"], 1)
            pe.wait_ge(S["back_act"], 1)
            flat = oc[:, :, :].rearrange("c b n -> c (b n)")
            for n in range(NT // GT):
                wait(pe, S["y_out"], n - 1)
                for j in range(GT):
                    t = GT * n + j
                    ins = pe.matmul(yp[n % 2][:, j * C:(j + 1) * C], flat[:, t * P:(t + 1) * P], wout[:, :],
                                    start=True, stop=True)
                ins.then_inc(S["y_in"], 1)


def l2_conv(nc, T, A):
    with ExitStack() as ctx:
        s = Scope(nc, ctx, "l2")
        R = {"Q": s.sb("Q", [C, NI, PIX]), "K": s.sb("K", [C, NI, KPIX]), "V": s.sb("V", [C, NI, KPIX])}
        l2_sample(nc, T, A, R)
        l2_mix(nc, T, A, R)


L3H, L3D = 8, 16
INNER = L3H * L3D
L3_SCALE = L3D ** -0.5
QG = 5
GI = NI // QG
TG = GI * PIX // P
QB, Q_EPS = 128.0, 1e-5


def l3_conv(nc, T, A):
    X, ident = T["X"], T["ident"]
    TAPS = KS * KS
    VW = INNER + INNER + C
    with ExitStack() as ctx:
        s = Scope(nc, ctx, "l3c")
        taps, bn, wq, wkv, wvt, wo, bo, mask = (T[f"l3_{n}"] for n in
                                                ("taps", "bn", "wq", "wkv", "wvt", "wo", "bo", "mask"))
        inv = s.sb("inv", [C, 2])
        shift = s.sb("shift", [C, 2])
        diag = s.sb("diag", [P, TAPS, C])
        ones = s.sb("ones", [P, P])
        xn = s.sb("xn", [P, 2, C])
        xp = s.sb("xp", [P, 2, PAD, PAD])
        yq = s.sb("yq", [C, PIX])
        ykv = s.sb("ykv", [C, PIX])
        q = s.sb("q", [INNER, PIX])
        kv = s.sb("kv", [P, 2, 2 * INNER])
        prod = s.sb("prod", [P, 2, INNER])
        dsum = s.sb("dsum", [P, NI, 2, L3H])
        dtot = s.sb("dtot", [P, 1])
        m0 = s.sb("m0", [P, 1])
        ktv = s.sb("ktv", [INNER, INNER])
        z = s.sb("z", [P, 2, INNER])
        zt = s.sb("zt", [INNER, 2, P])
        vw = s.sb("vw", [P, NT, C])
        stats = s.sb("stats", [P, 2, 6])
        mean = s.sb("mean", [P, 2])
        var = s.sb("var", [P, 2])
        rstd = s.sb("rstd", [P, 2])
        mhalf = s.sb("mhalf", [P, 2])
        tp, qp, cp, kv0, kv1, pp, zp, yp = (s.psum(n, [P, 512]) for n in
                                            ("tp", "qp", "cp", "kv0", "kv1", "pp", "zp", "yp"))
        names = ("consts", "bias_done", "tap_done", "v_eps", "bn_pow", "vw_in", "vw_out", "diag_done",
                 "var_done", "rstd_done",
                 "dve_step", "xn_done", "turned", "xp_done", "yq_in", "yq_out", "ykv_done", "q_in", "q_out",
                 "qt_in", "qt_out", "kv_in", "kv_out", "ktv_in", "ktv_out", "qkv_in", "z_out", "zt_in", "zt_out",
                 "y_in", "y_out", "tot_done", "m0_in")
        S = {n: s.sem(n) for n in names}
        block = ctx.enter_context(nc.Block())

        def images(eng, body):
            body(0, 0, False)
            body(1, 1, False)
            body(2, 0, False)
            with eng.Fori(1, NI // 2 - 1) as i:
                body(2 * i + 1, 1, False)
                body(2 * i + 2, 0, False)
            body(NI - 1, 1, True)

        @block.gpsimd
        def _(pool):
            pool.memset(xp[:, :, :, :], 0.0)
            pool.memset(ones[:, :], 1.0)
            pool.memset(mhalf[:, :], -0.5).then_inc(S["consts"], 1)
            pool.wait_ge(S["consts"], 1)
            pool.memset(diag[C:P, :, :], 0.0).then_inc(S["consts"], 1)
            pool.wait_ge(S["consts"], 2)
            pool.wait_ge(S["v_eps"], 1)
            pool.tensor_tensor(inv[:, :], shift[:, :], mhalf[0:C, :], ALU.pow).then_inc(S["bn_pow"], 1)
            with pool.Fori(0, NI) as b:
                pool.wait_ge(S["var_done"], b + 1)
                pool.tensor_tensor(rstd[:, :], var[:, :], mhalf[:, :], ALU.pow).then_inc(S["rstd_done"], 1)
                pool.wait_ge(S["xn_done"], b + 1)
                x = X[:, bass.ds(2 * b, 2), :]
                pool.tensor_tensor(x, x, bo[:, :].unsqueeze(1).broadcast_to([P, 2, C]), ALU.add
                                   ).then_inc(S["bias_done"], 1)

        LAST = 3
        EACH = LAST + 6 + TAPS - 2

        @block.vector
        def _(dve):
            def ln_stats(b, chain):
                layernorm_stats(dve, chain, [X[:, 2 * b + t, :] for t in range(2)], stats, mean, var, 1e-6)
                dve.sem_inc(S["var_done"], 1)

            def ln_apply(b, chain):
                wait(dve, S["rstd_done"], b + 1)
                wait(dve, S["turned"], b)
                layernorm_apply(dve, chain, [X[:, 2 * b + t, :] for t in range(2)], [xn[:, t, :] for t in range(2)],
                                stats, mean, rstd).then_inc(S["xn_done"], 1)

            def output(b):
                wait(dve, S["y_in"], b + 1)
                wait(dve, S["bias_done"], b + 1)
                x = X[:, bass.ds(2 * b, 2), :].rearrange("p t c -> p (t c)")
                dve.tensor_tensor(x, yp[:, 0:2 * C], x, ALU.add).then_inc(S["y_out"], 1)

            def conv_kv(b, p, chain):
                wait(dve, S["tap_done"], b + 1)
                y3 = ykv[:, :].rearrange("c (y x) -> c y x", x=SIDE)
                for t in range(1, TAPS):
                    image = xp[0:C, p, t // KS:t // KS + SIDE, t % KS:t % KS + SIDE]
                    ins = dve.scalar_tensor_tensor(out=y3, in0=image, scalar=taps[:, 1, t:t + 1], in1=y3,
                                                   op0=ALU.mult, op1=ALU.add)
                    if t < TAPS - 1:
                        chain.sync(ins)
                ins.then_inc(S["ykv_done"], 1)

            def body(b, p, last):
                chain = Chain(dve, S["dve_step"], base + b * EACH)
                if not last:
                    ln_stats(b + 1, chain)
                    ln_apply(b + 1, chain)
                wait(dve, S["qt_in"], b + 1)
                wait(dve, S["kv_out"], b + 1)
                chain.sync(dve.tensor_tensor(prod[:, :, :], qp[:, 0:2 * INNER].rearrange("p (t c) -> p t c", t=2),
                                             kv[:, :, 0:INNER], ALU.mult))
                dve.sem_inc(S["qt_out"], 1)
                d = dsum[:, b, :, :].rearrange("p t h -> p (t h)")
                chain.sync(dve.tensor_reduce(d, prod[:, :, :].rearrange("p t (h d) -> p (t h) d", d=L3D), AX.X,
                                             ALU.add))
                wait(dve, S["ktv_in"], b + 1)
                dve.tensor_tensor(ktv[:, :].rearrange("p (h d) -> p h d", d=L3D),
                                  pp[:, 0:INNER].rearrange("p (h d) -> p h d", d=L3D),
                                  mask[:, :].unsqueeze(2).broadcast_to([INNER, L3H, L3D]), ALU.mult
                                  ).then_inc(S["ktv_out"], 1)
                chain.sync(dve.tensor_tensor(prod[:, :, :].rearrange("p t (h d) -> p (t h) d", d=L3D),
                                             kv[:, :, INNER:2 * INNER].rearrange("p t (h d) -> p t h d", d=L3D),
                                             d.unsqueeze(2).broadcast_to([P, 2 * L3H, L3D]), ALU.mult))
                if not last:
                    conv_kv(b + 1, 1 - p, chain)
                if not (isinstance(b, int) and b == 0):
                    output(b - 1)
                wait(dve, S["qkv_in"], b + 1)
                wait(dve, S["zt_in"], b)
                dve.tensor_tensor(z[:, :, :].rearrange("p t c -> p (t c)"), pp[:, INNER:3 * INNER],
                                  prod[:, :, :].rearrange("p t c -> p (t c)"), ALU.subtract).then_inc(S["z_out"], 1)
                assert chain.n == (LAST if last else EACH), chain.n

            chain = Chain(dve, S["dve_step"])
            chain.sync(dve.tensor_scalar(shift[:, :], bn[:, 3, :], BN_EPS, None, ALU.add))
            dve.sem_inc(S["v_eps"], 1)
            ln_stats(0, chain)
            dve.wait_ge(S["bn_pow"], 1)
            chain.sync(dve.tensor_tensor(inv[:, :], inv[:, :], bn[:, 0, :], ALU.mult))
            chain.sync(dve.tensor_tensor(shift[:, :], bn[:, 2, :], inv[:, :], ALU.mult))
            dve.tensor_tensor(shift[:, :], bn[:, 1, :], shift[:, :], ALU.subtract)
            chain.sync(dve.tensor_tensor(taps[:, :, :], taps[:, :, :], inv[:, :].unsqueeze(2)
                                         .broadcast_to([C, 2, TAPS]), ALU.mult))
            ln_apply(0, chain)
            for t in range(TAPS):
                ins = dve.tensor_scalar(diag[0:C, t, :], ident[0:C, 0:C], taps[:, 0, t:t + 1], None, ALU.mult)
            ins.then_inc(S["diag_done"], 1)
            dve.wait_ge(S["vw_in"], 1)
            dve.tensor_copy(wkv[:, 2 * INNER:VW], pp[0:C, 0:C]).then_inc(S["vw_out"], 1)
            conv_kv(0, 0, chain)
            base = chain.n
            images(dve, body)
            output(NI - 1)
            dve.tensor_reduce(dtot[:, :], dsum[:, :, :, :].rearrange("p b t h -> p (b t h)"), AX.X, ALU.add
                              ).then_inc(S["tot_done"], 1)
            dve.wait_ge(S["y_out"], NI)
            last = Chain(dve, S["dve_step"], base + (NI - 1) * EACH + LAST)
            dve.wait_ge(S["m0_in"], 1)
            last.sync(dve.tensor_scalar(m0[:, :], pp[:, 0:1], L3_SCALE, None, ALU.mult))
            dve.scalar_tensor_tensor(out=X[:, :, :].rearrange("p t c -> p (t c)"),
                                     in0=vw[:, :, :].rearrange("p t c -> p (t c)"), scalar=m0[:, 0:1],
                                     in1=X[:, :, :].rearrange("p t c -> p (t c)"), op0=ALU.mult, op1=ALU.add)

        @block.scalar
        def _(act):
            def tokens_out(b, p):
                wait(act, S["turned"], b + 1)
                wait(act, S["yq_in"], b - 1)
                wait(act, S["ykv_done"], b - 1)
                act.activation(xp[0:C, p, 1:SIDE + 1, 1:SIDE + 1],
                               tp[0:C, 0:PIX].rearrange("c (y x) -> c y x", x=SIDE), ACT.Copy
                               ).then_inc(S["xp_done"], 1)

            def first_tap(b, p):
                wait(act, S["xp_done"], b + 1)
                wait(act, S["kv_in"], b)
                act.activation(ykv[:, :].rearrange("c (y x) -> c y x", x=SIDE), xp[0:C, p, 0:SIDE, 0:SIDE],
                               ACT.Identity, scale=taps[:, 1, 0:1], bias=shift[:, 1:2]).then_inc(S["tap_done"], 1)

            def queries_out(b):
                wait(act, S["yq_in"], b + 1)
                act.activation(yq[:, :], cp[0:C, 0:PIX], ACT.Identity, bias=shift[:, 0:1]).then_inc(S["yq_out"], 1)
                wait(act, S["q_in"], b + 1)
                act.activation(q[:, :], tp[:, 0:PIX], ACT.Copy).then_inc(S["q_out"], 1)

            def kv_out(b):
                wait(act, S["kv_in"], b + 1)
                wait(act, S["z_out"], b)
                for t, bank in enumerate((kv0, kv1)):
                    act.activation(kv[:, t, :], bank[:, 0:2 * INNER], ACT.Copy)
                for t, bank in enumerate((kv0, kv1)):
                    ins = act.activation(vw[:, 2 * b + t, :], bank[:, 2 * INNER:VW], ACT.Copy)
                ins.then_inc(S["kv_out"], 1)

            def z_turned(b):
                wait(act, S["zt_in"], b + 1)
                act.activation(zt[:, :, :].rearrange("p t n -> p (t n)"), zp[:, 0:2 * P], ACT.Copy, scale=L3_SCALE
                               ).then_inc(S["zt_out"], 1)

            def body(b, p, last):
                kv_out(b)
                if not last:
                    tokens_out(b + 1, 1 - p)
                    first_tap(b + 1, 1 - p)
                if not (isinstance(b, int) and b == 0):
                    z_turned(b - 1)
                if not last:
                    queries_out(b + 1)

            act.wait_ge(S["vw_out"], 1)
            tokens_out(0, 0)
            first_tap(0, 0)
            queries_out(0)
            images(act, body)
            z_turned(NI - 1)

        @block.tensor
        def _(pe):
            def turn(b):
                wait(pe, S["xn_done"], b + 1)
                wait(pe, S["q_out"], b)
                for t in range(2):
                    ins = pe.transpose(tp[0:C, t * P:(t + 1) * P], xn[:, t, :], ident[:, :])
                ins.then_inc(S["turned"], 1)

            def conv_q(b, p):
                wait(pe, S["xp_done"], b + 1)
                wait(pe, S["yq_out"], b)
                o = cp[0:C, 0:PIX].rearrange("c (y x) -> c y x", x=SIDE)
                for t in range(TAPS):
                    dy, dx = t // KS, t % KS
                    ins = pe.matmul(o, diag[:, t, :], xp[:, p, dy:dy + SIDE, dx:dx + SIDE],
                                    start=(t == 0), stop=(t == TAPS - 1))
                ins.then_inc(S["yq_in"], 1)

            def queries(b):
                wait(pe, S["yq_out"], b + 1)
                pe.matmul(tp[:, 0:PIX], wq[:, :], yq[:, :], start=True, stop=True).then_inc(S["q_in"], 1)
                wait(pe, S["qt_out"], b)
                for t in range(2):
                    ins = pe.matmul(qp[:, t * INNER:(t + 1) * INNER], yq[:, t * P:(t + 1) * P], wq[:, :],
                                    start=True, stop=True)
                ins.then_inc(S["qt_in"], 1)

            def keys_values(b):
                wait(pe, S["ykv_done"], b + 1)
                wait(pe, S["kv_out"], b)
                for t, bank in enumerate((kv0, kv1)):
                    ins = pe.matmul(bank[:, 0:VW], ykv[:, t * P:(t + 1) * P], wkv[:, :], start=True, stop=True)
                ins.then_inc(S["kv_in"], 1)

            def keys_by_values(b):
                wait(pe, S["kv_out"], b + 1)
                wait(pe, S["z_out"], b)
                for t in range(2):
                    ins = pe.matmul(pp[:, 0:INNER], kv[:, t, 0:INNER], kv[:, t, INNER:2 * INNER],
                                    start=(t == 0), stop=(t == 1))
                ins.then_inc(S["ktv_in"], 1)

            def queries_by_ktv(b):
                wait(pe, S["ktv_out"], b + 1)
                wait(pe, S["q_out"], b + 1)
                for t in range(2):
                    ins = pe.matmul(pp[:, (t + 1) * INNER:(t + 2) * INNER], q[:, t * P:(t + 1) * P], ktv[:, :],
                                    start=True, stop=True)
                ins.then_inc(S["qkv_in"], 1)

            def turn_z(b):
                wait(pe, S["z_out"], b + 1)
                wait(pe, S["zt_out"], b)
                for t in range(2):
                    ins = pe.transpose(zp[:, t * P:(t + 1) * P], z[:, t, :], ident[:, :])
                ins.then_inc(S["zt_in"], 1)

            def project(b):
                wait(pe, S["zt_out"], b + 1)
                wait(pe, S["y_out"], b)
                for t in range(2):
                    ins = pe.matmul(yp[:, t * C:(t + 1) * C], zt[:, t, :], wo[:, :], start=True, stop=True)
                ins.then_inc(S["y_in"], 1)

            def body(b, p, last):
                first = isinstance(b, int) and b == 0
                keys_values(b)
                if not last:
                    turn(b + 1)
                if not first:
                    turn_z(b - 1)
                keys_by_values(b)
                if not last:
                    conv_q(b + 1, 1 - p)
                if not first:
                    project(b - 1)
                queries_by_ktv(b)
                if not last:
                    queries(b + 1)

            pe.matmul(pp[0:C, 0:C], wvt[:, :], wo[:, :], start=True, stop=True).then_inc(S["vw_in"], 1)
            turn(0)
            pe.wait_ge(S["diag_done"], 1)
            pe.wait_ge(S["consts"], 2)
            pe.wait_ge(S["vw_out"], 1)
            conv_q(0, 0)
            queries(0)
            images(pe, body)
            turn_z(NI - 1)
            project(NI - 1)
            pe.wait_ge(S["tot_done"], 1)
            pe.matmul(pp[:, 0:1], ones[:, :], dtot[:, :], start=True, stop=True).then_inc(S["m0_in"], 1)


def l3_ffn(nc, T, A, out):
    X, ident = T["X"], T["ident"]
    TOKS = TG * P
    MS = 2 * KC
    UPS = 3
    with ExitStack() as ctx:
        s = Scope(nc, ctx, "l3f")
        w1, w2, b2 = T["l3_w1"], T["l3_w2"], T["l3_b2"]
        inv_qb = s.sb("inv_qb", [2, P])
        xn = s.sb("xn", [P, TG, C])
        xt = s.sb("xt", [CB, TOKS])
        hid = s.sb("hid", [P, 2, KC, TOKS])
        y = s.sb("y", [P, TG, C])
        amax = s.sb("amax", [P, 2 * KC])
        bmax = s.sb("bmax", [P, 2])
        top = s.sb("top", [2, 1])
        tops = s.sb("tops", [2, 2])
        gam = s.sb("gam", [P, 2])
        stats = s.sb("stats", [P, TG, 6])
        mean = s.sb("mean", [P, TG])
        var = s.sb("var", [P, TG])
        rstd = s.sb("rstd", [P, TG])
        mhalf = s.sb("mhalf", [P, TG])
        tp = [s.psum(f"tp{i}", [P, 512]) for i in range(2)]
        dn = [s.psum(f"dn{i}", [P, 512]) for i in range(2)]
        up = [s.psum(f"up{i}", [P, 512]) for i in range(UPS)]
        gp = s.psum("gp", [P, 512])
        names = ("consts", "var_done", "rstd_done", "dve_step",
                 "xn_done", "turned", "xt_done", "up_in", "up_max", "up_out", "max_done", "max_in", "top_done",
                 "top_in", "gam_done", "clipped", "hid_done", "down_in", "y_read", "y_done", "stored")
        S = {n: s.sem(n) for n in names}
        block = ctx.enter_context(nc.Block())
        LIM = float(np.float32(QB - Q_EPS))
        TB = TOKS - 512

        @block.sync
        def _(sp):
            for g in range(QG):
                sp.wait_ge(S["y_done"], g + 1)
                sp.dma_start(out[:, TG * g:TG * (g + 1), :], y[:, :, :]).then_inc(S["stored"], 16)
            sp.dma_start(out[:, TG * QG:NT, :], X[:, TG * QG:NT, :]).then_inc(S["stored"], 16)
            sp.wait_ge(S["stored"], 16 * (QG + 1))

        @block.gpsimd
        def _(pool):
            pool.memset(inv_qb[:, :], 1.0 / QB)
            pool.memset(mhalf[:, :], -0.5).then_inc(S["consts"], 1)
            pool.wait_ge(S["consts"], 1)
            with pool.Fori(0, QG) as g:
                pool.wait_ge(S["var_done"], g + 1)
                pool.tensor_tensor(rstd[:, :], var[:, :], mhalf[:, :], ALU.pow).then_inc(S["rstd_done"], 1)

        @block.vector
        def _(dve):
            def ln(g, chain):
                tiles = [X[:, TG * g + j, :] for j in range(TG)]
                layernorm_stats(dve, chain, tiles, stats, mean, var, 1e-5)
                dve.sem_inc(S["var_done"], 1)
                wait(dve, S["rstd_done"], g + 1)
                wait(dve, S["turned"], g)
                layernorm_apply(dve, chain, tiles, [xn[:, j, :] for j in range(TG)], stats, mean, rstd
                                ).then_inc(S["xn_done"], 1)

            def up_maxima(g, ms):
                for m in ms:
                    wait(dve, S["up_in"], MS * g + m + 1)
                    dve.tensor_reduce(amax[:, m:m + 1], up[m % UPS][:, 0:(512, TB)[m % 2]], AX.X, ALU.max,
                                      apply_absolute_value=True).then_inc(S["up_max"], 1)

            def up_maximum(g, chain):
                wait(dve, S["up_max"], MS * (g + 1))
                chain.sync(dve.tensor_reduce(bmax[:, 0:1], amax[:, :], AX.X, ALU.max))

            def factors(g, chain):
                wait(dve, S["max_in"], g + 1)
                chain.sync(dve.tensor_reduce(top[:, :], gp[0:2, 0:P], AX.X, ALU.max))
                chain.sync(dve.tensor_scalar(tops[:, :], ident[0:2, 0:2], top[:, 0:1], None, ALU.mult))
                dve.sem_inc(S["top_done"], 1)
                wait(dve, S["top_in"], g + 1)
                chain.sync(dve.tensor_scalar(gam[:, :], gp[:, P:P + 2], Q_EPS / QB, None, ALU.add))
                dve.sem_inc(S["gam_done"], 1)
                chain.sync(dve.reciprocal(gam[:, :], gam[:, :]))

            def clip(g, chain):
                wait(dve, S["up_out"], MS * (g + 1))
                h = hid[:, g % 2, :, :]

                def scale(k):
                    return dve.tensor_scalar(h[:, k, :], h[:, k, :], gam[:, 0:1], LIM, ALU.mult, ALU.min)

                scale(0)
                for k in range(KC):
                    if k + 1 < KC:
                        chain.sync(scale(k + 1))
                    dve.tensor_scalar(h[:, k, :], h[:, k, :], -LIM, None, ALU.max).then_inc(S["clipped"], 1)

            yf = y[:, :, :].rearrange("p t c -> p (t c)")

            def results(g, chain):
                wait(dve, S["down_in"], g + 1)
                wait(dve, S["stored"], 16 * g)
                for h, (lo, n) in enumerate(((0, 4), (4, 2))):
                    ins = dve.tensor_tensor(y[:, lo:lo + n, :], dn[h][:, 0:n * C].rearrange("p (t c) -> p t c", c=C),
                                            b2[:, :].unsqueeze(1).broadcast_to([P, n, C]), ALU.add)
                chain.sync(ins)
                dve.sem_inc(S["y_read"], 1)
                chain.sync(dve.tensor_reduce(bmax[:, 1:2], yf, AX.X, ALU.max, apply_absolute_value=True))

            def add_results(g, chain):
                chain.sync(dve.tensor_scalar(yf, yf, gam[:, 1:2], LIM, ALU.mult, ALU.min))
                x = X[:, TG * g:TG * (g + 1), :].rearrange("p t c -> p (t c)")
                dve.scalar_tensor_tensor(out=yf, in0=yf, scalar=-LIM, in1=x, op0=ALU.max, op1=ALU.add
                                         ).then_inc(S["y_done"], 1)

            dve.memset(xt[C:CB, :], 1.0)
            dve.memset(bmax[:, :], 0.0)
            chain = Chain(dve, S["dve_step"])
            ln(0, chain)
            ln(1, chain)
            up_maxima(0, range(MS))
            up_maximum(0, chain)
            dve.sem_inc(S["max_done"], 1)
            for g in range(QG):
                factors(g, chain)
                clip(g, chain)
                if g > 0:
                    add_results(g - 1, chain)
                if g + 1 < QG:
                    up_maxima(g + 1, range(UPS))
                if g + 2 < QG:
                    ln(g + 2, chain)
                results(g, chain)
                if g + 1 < QG:
                    up_maxima(g + 1, range(UPS, MS))
                    up_maximum(g + 1, chain)
                dve.sem_inc(S["max_done"], 1)
            factors(QG, chain)
            add_results(QG - 1, chain)

        @block.scalar
        def _(act):
            def tokens_out(g):
                wait(act, S["turned"], g + 1)
                wait(act, S["up_in"], MS * g)
                act.activation(xt[0:C, 0:512], tp[0][0:C, :], ACT.Copy)
                act.activation(xt[0:C, 512:TOKS], tp[1][0:C, 0:TB], ACT.Copy).then_inc(S["xt_done"], 1)

            def ups_out(g):
                for m in range(MS):
                    wait(act, S["up_max"], MS * g + m + 1)
                    k, lo, n = m // 2, 512 * (m % 2), (512, TB)[m % 2]
                    act.activation(hid[:, g % 2, k, lo:lo + n], up[m % UPS][:, 0:n], ACT.Copy
                                   ).then_inc(S["up_out"], 1)

            tokens_out(0)
            ups_out(0)
            for g in range(QG):
                if g + 1 < QG:
                    tokens_out(g + 1)
                for k in range(KC):
                    wait(act, S["clipped"], KC * g + k + 1)
                    h = hid[:, g % 2, k, :]
                    act.activation(h, h, ACT.Gelu).then_inc(S["hid_done"], 1)
                if g + 1 < QG:
                    ups_out(g + 1)

        @block.tensor
        def _(pe):
            def top_in(g):
                wait(pe, S["max_done"], g + 1)
                wait(pe, S["gam_done"], g)
                pe.matmul(gp[0:2, 0:P], bmax[:, :], ident[:, :], start=True, stop=True).then_inc(S["max_in"], 1)

            def top_out(g):
                wait(pe, S["top_done"], g + 1)
                pe.matmul(gp[:, P:P + 2], inv_qb[:, :], tops[:, :], start=True, stop=True).then_inc(S["top_in"], 1)

            def turn(g):
                wait(pe, S["xn_done"], g + 1)
                wait(pe, S["xt_done"], g)
                for j in range(TG):
                    ins = pe.transpose(tp[j // 4][0:C, (j % 4) * P:(j % 4 + 1) * P], xn[:, j, :], ident[:, :])
                ins.then_inc(S["turned"], 1)

            def ups(g, ms):
                wait(pe, S["xt_done"], g + 1)
                for m in ms:
                    wait(pe, S["up_out"], MS * g + m - UPS + 1)
                    k, lo, n = m // 2, 512 * (m % 2), (512, TB)[m % 2]
                    pe.matmul(up[m % UPS][:, 0:n], w1[:, k * P:(k + 1) * P], xt[:, lo:lo + n], start=True, stop=True
                              ).then_inc(S["up_in"], 1)

            def downs(g):
                wait(pe, S["y_read"], g)
                for k in range(KC):
                    wait(pe, S["hid_done"], KC * g + k + 1)
                    for j in range(TG):
                        ins = pe.matmul(dn[j // 4][:, (j % 4) * C:(j % 4 + 1) * C],
                                        hid[:, g % 2, k, j * P:(j + 1) * P], w2[:, k, :],
                                        start=(k == 0 and j % 4 == 0),
                                        stop=(k == KC - 1 and j in (3, TG - 1)))
                ins.then_inc(S["down_in"], 1)

            pe.wait_ge(S["consts"], 1)
            turn(0)
            ups(0, range(MS))
            for g in range(QG):
                top_in(g)
                top_out(g)
                if g + 1 < QG:
                    turn(g + 1)
                    ups(g + 1, range(UPS))
                downs(g)
                if g + 1 < QG:
                    ups(g + 1, range(UPS, MS))
            top_in(QG)
            top_out(QG)


def build(nc, A, out):
    with ExitStack() as ctx:
        s = Scope(nc, ctx, "all")
        T = {"X": s.sb("X", [P, NT, C]), "ident": s.sb("ident", [P, P])}
        T["scratch"] = nc.dram_tensor("conv_scratch", [NT * P, C], F32).ap()
        T["moe"] = [(s.sb(f"w1_{n}", [CB, NE * KC, P]), s.sb(f"w2_{n}", [P, NE * KC, C]),
                     s.sb(f"gw_{n}", [CB, NE]), s.sb(f"b2_{n}", [P, NE, C])) for n in range(3)]
        for name in LATE:
            shape = list(A[name].shape)
            T[name] = s.sb(name, [C, 2 * INNER + C] if name == "l3_wkv" else shape)
        T["late_in"] = s.sem("late_in")
        T["moe_in"] = [s.sem(f"moe_in{n}") for n in range(3)]
        before = nc.snapshot_sems()
        l0_conv(nc, T, A)
        moe(nc, T, A, 0)
        l1_attention(nc, T, A)
        moe(nc, T, A, 1)
        nc.clear_and_free_semaphores(nc.allocated_since(before))
        nc.all_engine_barrier()
        l2_conv(nc, T, A)
        moe(nc, T, A, 2)
        l3_conv(nc, T, A)
        l3_ffn(nc, T, A, out)


def tokens(x):
    return np.ascontiguousarray(np.transpose(x.reshape(NI, C, 2, P), (3, 0, 2, 1)).reshape(P, NT, C))


def layouts(v):
    f = np.float32
    v = {k: np.asarray(a) for k, a in v.items()}
    x = v["x"]
    A = {"x_tokens": tokens(x), "ident": np.eye(P, dtype=f)}
    A["x_rows"] = np.ascontiguousarray(
        np.transpose(x.reshape(2, 8, C, SIDE, SIDE), (1, 3, 0, 4, 2)).reshape(P, NT, C))

    def band(w):
        k = w.shape[-1]
        out = np.zeros((GC, SIDE, NG, k, SIDE), f)
        wg = w.reshape(NG, GC, k, k)
        for xi in range(SIDE):
            for xo in range(SIDE):
                d = xi - xo + k // 2
                if 0 <= d < k:
                    out[:, xi, :, :, xo] = np.transpose(wg[:, :, :, d], (1, 0, 2))
        return out.reshape(P, NG, k, SIDE)

    A["band"] = band(v["L0_conv_w_large"])
    A["band_s"] = band(v["L0_conv_w_small"])
    bn = np.stack([np.stack([v[f"L0_conv_{a}_{b}"] for b in "lsi"]) for a in "gbmv"])
    bn = np.transpose(bn.reshape(4, 3, NG, GC), (3, 0, 1, 2))
    A["bn"] = np.ascontiguousarray(np.repeat(bn, SIDE, axis=0))
    A["eye"] = np.tile(np.eye(SIDE, dtype=f), (GC, 1))
    A["own"] = np.repeat(np.eye(GC, dtype=f), SIDE, axis=0)
    for n in range(3):
        g = lambda name: v[f"L{n}_ffn_{name}"]
        w1 = np.concatenate([np.transpose(g("w1"), (1, 0, 2)).reshape(C, NE * HID), g("b1").reshape(1, -1)])
        A[f"w1_{n}"] = w1.reshape(CB, NE * KC, P)
        A[f"w2_{n}"] = np.ascontiguousarray(
            np.transpose(g("w2").reshape(NE * KC, P, C), (1, 0, 2)))
        A[f"gw_{n}"] = np.concatenate([g("gate_w"), g("gate_b").reshape(1, -1)])
        A[f"b2_{n}"] = np.ascontiguousarray(np.broadcast_to(g("b2")[None], (P, NE, C)))
    def stacked(w):
        w = w.reshape(w.shape[:-1] + (SG, 2, 1, KD))
        out = np.zeros(w.shape[:-4] + (SG, 2, KS3 // KD, KD), f)
        out[..., 0:3, :] = w
        return out.reshape(w.shape[:-4] + (SG, P))

    c = {k[8:]: a for k, a in v.items() if k.startswith("L1_conv_")}
    def rows(w, bias):
        out = np.zeros((P, w.shape[1]), f)
        out[C - len(w):C] = w
        out[CT] = bias
        return out

    wq, wk = rows(c["Wq"].T, c["q_bias"]), rows(c["Wk"].T, c["k_bias"])
    wq[C:CT] = wq[C - DS:C]
    A["l1_wqk"] = stacked(np.stack([wq, wk], axis=1))
    scale = np.ones((P, 2, HEADS * KD), f)
    scale[0:CT] = np.stack([c["q_scale"], c["k_scale"]])
    A["l1_sqk"] = stacked(scale)
    low = np.zeros((P, 4), f)
    low[np.arange(P) // KD % 4 == 1, 0] = -1
    low[np.arange(P) // KD % 4 == 2, 1] = -1
    low[HEADS:2 * HEADS, 2] = -1
    low[C:CT, 3] = -1
    A["l1_low"] = low
    A["l1_sel"] = np.zeros((P, HEADS, P), f)
    A["l1_sel"][0:2 * HEADS] = np.tile(np.eye(HEADS, dtype=f), (2, 1))[:, :, None]
    A["l1_wv"] = rows(c["Wv"].T, c["v_bias"])[0:CT + 1]
    A["l1_sv"] = np.broadcast_to(c["v_scale"][None], (C, HEADS * DH))
    A["l1_wp"] = np.transpose(c["Wp"].T.reshape(2, C, DS), (1, 0, 2))
    A["l1_sp"] = np.stack([c["p_scale"], c["p_bias"]], axis=1)
    A["l1_wo"] = c["Wo"].T
    A["l1_wx"] = rows(c["Wo"].T, c["o_bias"])[0:CT + 1]
    A["l1_so"] = np.broadcast_to(c["o_scale"][None], (C, C))
    c = {k[8:]: a for k, a in v.items() if k.startswith("L2_conv_")}
    kinds = ("q", "k", "off1", "v")
    A["l2_taps"] = np.stack([c[f"w_{k}"].reshape(C, KS * KS) for k in kinds], axis=1)
    A["l2_bias"] = np.stack([c[f"b_{k}"] for k in kinds], axis=1)
    A["l2_lnp"] = np.stack([c["ln_g"], c["ln_b"]], axis=1)
    A["l2_woff"] = np.repeat(c["w_off2"][::-1].T[:, :, None], P, axis=2)
    line = (np.linspace(0.5, KSIDE - 0.5, KSIDE) / KSIDE * 2 - 1).astype(f)
    ref = np.stack([np.tile(line, KSIDE), np.repeat(line, KSIDE)])
    A["l2_ref"] = np.broadcast_to(ref[None], (P, 2, KPIX))
    px, py = np.arange(P) % SIDE, np.arange(P) // SIDE
    A["l2_coord"] = ((SIDE - 1) / 2 - np.stack([px, py, py + SIDE // 2], axis=1)).astype(f)
    A["l2_mask"] = (np.arange(P)[:, None] % HC2 // (HC2 // 4) == np.arange(HG)[None]).astype(f)
    A["l2_wout"] = c["w_out"].T
    c = {k[8:]: a for k, a in v.items() if k.startswith("L3_conv_")}
    A["l3_taps"] = np.stack([c["wq_dw"].reshape(C, KS * KS), c["wkv_dw"].reshape(C, KS * KS)], axis=1)
    A["l3_bn"] = np.transpose(np.stack([np.stack([c[f"{w}_bn_{a}"] for w in ("wq", "wkv")]) for a in "gbmv"]),
                              (2, 0, 1))
    A["l3_wq"], A["l3_wkv"], A["l3_wo"] = c["wq_pw"].T, c["wkv_pw"].T, c["wo"].T
    A["l3_wvt"] = c["wkv_pw"][INNER:]
    A["l3_bo"] = np.broadcast_to(c["bo"][None], (P, C))
    A["l3_mask"] = np.repeat(np.eye(L3H, dtype=f), L3D, axis=0)
    A["l3_w1"] = np.concatenate([v["L3_ffn_W1"].T, v["L3_ffn_b1"][None]])
    A["l3_w2"] = np.transpose(v["L3_ffn_W2"].T.reshape(KC, P, C), (1, 0, 2))
    A["l3_b2"] = np.broadcast_to(v["L3_ffn_b2"][None], (P, C))
    return {k: np.ascontiguousarray(a) for k, a in A.items()}


def kernel(**inputs):
    import concourse.bacc as bacc
    from concourse.bass_utils import run_bass_kernel_spmd

    arrays = layouts(inputs)
    nc = bacc.Bacc("TRN2", target_bir_lowering=False, num_devices=1)
    A = {name: nc.dram_tensor(name, a.shape, F32, kind="ExternalInput").ap() for name, a in arrays.items()}
    out = nc.dram_tensor("out_tokens", (P, NT, C), F32, kind="ExternalOutput").ap()
    build(nc, A, out)
    y = run_bass_kernel_spmd(nc, [arrays], core_ids=[0]).results[0]["out_tokens"]
    return np.ascontiguousarray(y.reshape(P, NI, 2, C).transpose(1, 3, 2, 0).reshape(NI, C, SIDE, SIDE))
```
